# Optimizing a Trainium2 kernel written in Bass

```python
import numpy as np
import jax
import jax.numpy as jnp

def _softmax(x, axis=-1):
    return jax.nn.softmax(x, axis=axis)

def _gelu(x):
    return jax.nn.gelu(x, approximate=True)

def _silu(x):
    return jax.nn.silu(x)

def _sigmoid(x):
    return jax.nn.sigmoid(x)

def _layernorm(x, axis=-1, eps=1e-05):
    m = jnp.mean(x, axis=axis, keepdims=True)
    v = jnp.var(x, axis=axis, keepdims=True)
    return (x - m) / jnp.sqrt(v + eps)

def _scatter_add(tgt, idx, src, axis=0):
    return tgt.at[idx].add(src)

def _segment_sum(src, seg, n):
    return jax.ops.segment_sum(src, seg, n)
kernel_name = 'mk_xattn_ffn_d2_seqx_r4_f11763'

def setup_inputs(seed: int=0):
    np.random.seed(seed)
    _w = jnp.asarray

    def _rec_inputs():
        import jax
        import jax.numpy as jnp
        _rk = jax.random.key(seed)
        x = -0.0002928 + 1 * jax.random.normal(jax.random.fold_in(_rk, 1), (1, 2048, 256), jnp.float32)
        _lenS = 2048 - jax.random.randint(jax.random.fold_in(_rk, 7), (1,), 0, max(1, 2048 // 4) + 1, jnp.int32)
        _lenS2 = 1601 - jax.random.randint(jax.random.fold_in(_rk, 8), (1,), 0, max(1, 1601 // 4) + 1, jnp.int32)
        _ctx_1024P = jax.random.normal(jax.random.fold_in(_rk, 11), (1, 16, 256), jnp.float32)
        _ctx_1024c = jax.random.dirichlet(jax.random.fold_in(_rk, 511), 0.3 * jnp.ones((16,), jnp.float32), (1, 1601))
        _ctx_1024t = jnp.einsum('bsk,bkd->bsd', _ctx_1024c, _ctx_1024P)
        _ctx_1024t = _ctx_1024t * jax.lax.rsqrt(jnp.mean(jnp.square(_ctx_1024t)) + 1e-12) * 0.953939
        ctx_1024 = -1.39393e-06 + 0.999914 * (_ctx_1024t + 0.3 * jax.random.normal(jax.random.fold_in(_rk, 611), (1, 1601, 256), jnp.float32))
        return (x, ctx_1024)
    x, ctx_1024 = _rec_inputs()

    def _L0_xattn_setup():
        import jax, jax.numpy as jnp
        import numpy as np
        D_MODEL = 256
        NUM_HEADS = 16
        D_K = D_MODEL // NUM_HEADS

        def _split_heads(x):
            B, S, _ = x.shape
            return x.reshape(B, S, NUM_HEADS, D_K).transpose(0, 2, 1, 3)
        key = jax.random.key(seed)
        ks = jax.random.split(key, 11)
        B, S, D = (2, 512, D_MODEL)
        scale = 1.0 / np.sqrt(D)
        inp = {'queries': jax.random.normal(ks[0], (B, S, D), jnp.float32), 'keys': jax.random.normal(ks[1], (B, S, D), jnp.float32), 'values': jax.random.normal(ks[2], (B, S, D), jnp.float32), 'w_q': jax.random.normal(ks[3], (D, D), jnp.float32) * scale, 'b_q': jnp.zeros((D,), jnp.float32), 'w_k': jax.random.normal(ks[4], (D, D), jnp.float32) * scale, 'b_k': jnp.zeros((D,), jnp.float32), 'w_v': jax.random.normal(ks[5], (D, D), jnp.float32) * scale, 'b_v': jnp.zeros((D,), jnp.float32), 'w_o': jax.random.normal(ks[6], (D, D), jnp.float32) * scale, 'b_o': jnp.zeros((D,), jnp.float32)}
        return inp
    _L0_xattn_all = _L0_xattn_setup()
    _L0_xattn_in = {k: v for k, v in _L0_xattn_all.items() if k in ('w_q', 'b_q', 'w_k', 'b_k', 'w_v', 'b_v', 'w_o', 'b_o')}
    del _L0_xattn_all

    def _L0_ffn_setup():
        import jax, jax.numpy as jnp
        import numpy as np
        EMBED = 256
        HEADS = 16
        HEAD_DIM = EMBED // HEADS
        NUM_EXPERTS = 8
        TOP_K = 2
        HIDDEN = (int(2 * (4 * EMBED) / 3) + 63) // 64 * 64
        SEQ = 512
        BATCH = 2
        ROPE_BASE = 10000.0
        EPS = 1e-06

        def _rope_tables(seq_len, dim):
            inv_freq = 1.0 / ROPE_BASE ** (np.arange(0, dim, 2, dtype=np.float32) / dim)
            t = np.arange(seq_len, dtype=np.float32)
            freqs = np.einsum('i,j->ij', t, inv_freq)
            emb = np.concatenate([freqs, freqs], axis=-1)
            return (jnp.asarray(np.cos(emb)), jnp.asarray(np.sin(emb)))

        def _rotate_half(x):
            x1, x2 = jnp.split(x, 2, axis=-1)
            return jnp.concatenate([-x2, x1], axis=-1)

        def _rmsnorm(x, w):
            return x * jax.lax.rsqrt(jnp.mean(x * x, axis=-1, keepdims=True) + EPS) * w

        def _attention(x, wq, wk, wv, wo):
            B, S, _ = x.shape
            q = (x @ wq).reshape(B, S, HEADS, HEAD_DIM).transpose(0, 2, 1, 3)
            k = (x @ wk).reshape(B, S, HEADS, HEAD_DIM).transpose(0, 2, 1, 3)
            v = (x @ wv).reshape(B, S, HEADS, HEAD_DIM).transpose(0, 2, 1, 3)
            cos, sin = _rope_tables(S, HEAD_DIM)
            cos = cos[None, None]
            sin = sin[None, None]
            q = q * cos + _rotate_half(q) * sin
            k = k * cos + _rotate_half(k) * sin
            scale = HEAD_DIM ** (-0.5)
            scores = jnp.einsum('bhqd,bhkd->bhqk', q, k) * scale
            causal = jnp.triu(jnp.ones((S, S), bool), k=1)
            scores = jnp.where(causal, -jnp.inf, scores)
            attn = jax.nn.softmax(scores, axis=-1)
            out = jnp.einsum('bhqk,bhkd->bhqd', attn, v)
            out = out.transpose(0, 2, 1, 3).reshape(B, S, EMBED)
            return out @ wo

        def _moe(x, w_router, wg, wu, wd):
            B, S, E = x.shape
            xf = x.reshape(-1, E)
            logits = xf @ w_router
            probs = jax.nn.softmax(logits, axis=-1)
            topw, topi = jax.lax.top_k(probs, TOP_K)
            topw = topw / jnp.sum(topw, axis=-1, keepdims=True)
            combine = jnp.sum(jax.nn.one_hot(topi, NUM_EXPERTS, dtype=xf.dtype) * topw[..., None], axis=1)
            g = jax.nn.silu(jnp.einsum('td,xdh->txh', xf, wg))
            u = jnp.einsum('td,xdh->txh', xf, wu)
            eo = jnp.einsum('txh,xhd->txd', g * u, wd)
            out = jnp.einsum('txd,tx->td', eo, combine)
            return out.reshape(B, S, E)
        key = jax.random.key(seed)
        ks = jax.random.split(key, 12)
        s = 0.02
        return {'x': jax.random.normal(ks[0], (BATCH, SEQ, EMBED), jnp.float32), 'wq': jax.random.normal(ks[1], (EMBED, EMBED), jnp.float32) * s, 'wk': jax.random.normal(ks[2], (EMBED, EMBED), jnp.float32) * s, 'wv': jax.random.normal(ks[3], (EMBED, EMBED), jnp.float32) * s, 'wo': jax.random.normal(ks[4], (EMBED, EMBED), jnp.float32) * s, 'w_router': jax.random.normal(ks[5], (EMBED, NUM_EXPERTS), jnp.float32) * s, 'wg': jax.random.normal(ks[6], (NUM_EXPERTS, EMBED, HIDDEN), jnp.float32) * s, 'wu': jax.random.normal(ks[7], (NUM_EXPERTS, EMBED, HIDDEN), jnp.float32) * s, 'wd': jax.random.normal(ks[8], (NUM_EXPERTS, HIDDEN, EMBED), jnp.float32) * s, 'g1': jnp.ones((EMBED,), jnp.float32), 'g2': jnp.ones((EMBED,), jnp.float32)}
    _L0_ffn_all = _L0_ffn_setup()
    _L0_ffn_in = {k: v for k, v in _L0_ffn_all.items() if k in ('wq', 'wk', 'wv', 'wo', 'w_router', 'wg', 'wu', 'wd', 'g1', 'g2')}
    del _L0_ffn_all

    def _L1_xattn_setup():
        import jax, jax.numpy as jnp
        import numpy as np
        HEADS = 16
        key = jax.random.key(seed)
        ks = jax.random.split(key, 6)
        b, n, m, dim = (2, 512, 128, 256)
        s = dim ** (-0.5)
        return {'x': jax.random.normal(ks[0], (b, n, dim), jnp.float32), 'mem': jax.random.normal(ks[1], (b, m, dim), jnp.float32), 'Wq': jax.random.normal(ks[2], (dim, dim), jnp.float32) * s, 'Wkv': jax.random.normal(ks[3], (dim, 2 * dim), jnp.float32) * s, 'Wout': jax.random.normal(ks[4], (dim, dim), jnp.float32) * s, 'bout': jnp.zeros((dim,), jnp.float32)}
    _L1_xattn_all = _L1_xattn_setup()
    _L1_xattn_in = {k: v for k, v in _L1_xattn_all.items() if k in ('Wq', 'Wkv', 'Wout', 'bout')}
    del _L1_xattn_all

    def _L1_ffn_setup():
        import jax, jax.numpy as jnp
        import numpy as np
        B, S, D, F, E = (2, 512, 256, 1024, 8)
        LN_EPS = 1e-05

        def _xavier(key, shape, fan_in, fan_out):
            a = np.sqrt(6.0 / (fan_in + fan_out))
            return jax.random.uniform(key, shape, jnp.float32, -a, a)
        key = jax.random.key(seed)
        ks = jax.random.split(key, 8)
        tgt = jax.random.normal(ks[0], (B, S, D), jnp.float32)
        router_w = _xavier(ks[1], (E, D), D, E)
        router_b = jnp.zeros((E,), jnp.float32)
        w1 = _xavier(ks[2], (E, D, F), D, F)
        b1 = jnp.zeros((E, F), jnp.float32)
        w2 = _xavier(ks[3], (E, F, D), F, D)
        b2 = jnp.zeros((E, D), jnp.float32)
        gamma = jnp.ones((D,), jnp.float32)
        beta = jnp.zeros((D,), jnp.float32)
        return {'tgt': tgt, 'router_w': router_w, 'router_b': router_b, 'w1': w1, 'b1': b1, 'w2': w2, 'b2': b2, 'gamma': gamma, 'beta': beta}
    _L1_ffn_all = _L1_ffn_setup()
    _L1_ffn_in = {k: v for k, v in _L1_ffn_all.items() if k in ('router_w', 'router_b', 'w1', 'b1', 'w2', 'b2', 'gamma', 'beta')}
    del _L1_ffn_all
    return {'x': x, 'ctx_1024': ctx_1024, 'L0_xattn_w_q': _L0_xattn_in['w_q'], 'L0_xattn_b_q': _L0_xattn_in['b_q'], 'L0_xattn_w_k': _L0_xattn_in['w_k'], 'L0_xattn_b_k': _L0_xattn_in['b_k'], 'L0_xattn_w_v': _L0_xattn_in['w_v'], 'L0_xattn_b_v': _L0_xattn_in['b_v'], 'L0_xattn_w_o': _L0_xattn_in['w_o'], 'L0_xattn_b_o': _L0_xattn_in['b_o'], 'L0_ffn_wq': _L0_ffn_in['wq'], 'L0_ffn_wk': _L0_ffn_in['wk'], 'L0_ffn_wv': _L0_ffn_in['wv'], 'L0_ffn_wo': _L0_ffn_in['wo'], 'L0_ffn_w_router': _L0_ffn_in['w_router'], 'L0_ffn_wg': _L0_ffn_in['wg'], 'L0_ffn_wu': _L0_ffn_in['wu'], 'L0_ffn_wd': _L0_ffn_in['wd'], 'L0_ffn_g1': _L0_ffn_in['g1'], 'L0_ffn_g2': _L0_ffn_in['g2'], 'L1_xattn_Wq': _L1_xattn_in['Wq'], 'L1_xattn_Wkv': _L1_xattn_in['Wkv'], 'L1_xattn_Wout': _L1_xattn_in['Wout'], 'L1_xattn_bout': _L1_xattn_in['bout'], 'L1_ffn_router_w': _L1_ffn_in['router_w'], 'L1_ffn_router_b': _L1_ffn_in['router_b'], 'L1_ffn_w1': _L1_ffn_in['w1'], 'L1_ffn_b1': _L1_ffn_in['b1'], 'L1_ffn_w2': _L1_ffn_in['w2'], 'L1_ffn_b2': _L1_ffn_in['b2'], 'L1_ffn_gamma': _L1_ffn_in['gamma'], 'L1_ffn_beta': _L1_ffn_in['beta']}

def reference(x, ctx_1024, L0_xattn_w_q, L0_xattn_b_q, L0_xattn_w_k, L0_xattn_b_k, L0_xattn_w_v, L0_xattn_b_v, L0_xattn_w_o, L0_xattn_b_o, L0_ffn_wq, L0_ffn_wk, L0_ffn_wv, L0_ffn_wo, L0_ffn_w_router, L0_ffn_wg, L0_ffn_wu, L0_ffn_wd, L0_ffn_g1, L0_ffn_g2, L1_xattn_Wq, L1_xattn_Wkv, L1_xattn_Wout, L1_xattn_bout, L1_ffn_router_w, L1_ffn_router_b, L1_ffn_w1, L1_ffn_b1, L1_ffn_w2, L1_ffn_b2, L1_ffn_gamma, L1_ffn_beta):
    import jax
    import jax.numpy as jnp

    def _L0_xattn_ref(queries, keys, values, w_q, b_q, w_k, b_k, w_v, b_v, w_o, b_o):
        import jax, jax.numpy as jnp
        import numpy as np
        D_MODEL = 256
        NUM_HEADS = 16
        D_K = D_MODEL // NUM_HEADS

        def _split_heads(x):
            B, S, _ = x.shape
            return x.reshape(B, S, NUM_HEADS, D_K).transpose(0, 2, 1, 3)
        q = _split_heads(queries @ w_q.T + b_q)
        k = _split_heads(keys @ w_k.T + b_k)
        v = _split_heads(values @ w_v.T + b_v)
        scores = jnp.einsum('bhqd,bhkd->bhqk', q, k) / jnp.sqrt(jnp.asarray(D_K, q.dtype))
        weights = jax.nn.softmax(scores, axis=-1)
        attn = jnp.einsum('bhqk,bhkd->bhqd', weights, v)
        B, H, S, dk = attn.shape
        merged = attn.transpose(0, 2, 1, 3).reshape(B, S, H * dk)
        return merged @ w_o.T + b_o

    def _L0_ffn_ref(x, wq, wk, wv, wo, w_router, wg, wu, wd, g1, g2):
        import jax, jax.numpy as jnp
        import numpy as np
        EMBED = 256
        HEADS = 16
        HEAD_DIM = EMBED // HEADS
        NUM_EXPERTS = 8
        TOP_K = 2
        HIDDEN = (int(2 * (4 * EMBED) / 3) + 63) // 64 * 64
        SEQ = 512
        BATCH = 2
        ROPE_BASE = 10000.0
        EPS = 1e-06

        def _rope_tables(seq_len, dim):
            inv_freq = 1.0 / ROPE_BASE ** (np.arange(0, dim, 2, dtype=np.float32) / dim)
            t = np.arange(seq_len, dtype=np.float32)
            freqs = np.einsum('i,j->ij', t, inv_freq)
            emb = np.concatenate([freqs, freqs], axis=-1)
            return (jnp.asarray(np.cos(emb)), jnp.asarray(np.sin(emb)))

        def _rotate_half(x):
            x1, x2 = jnp.split(x, 2, axis=-1)
            return jnp.concatenate([-x2, x1], axis=-1)

        def _rmsnorm(x, w):
            return x * jax.lax.rsqrt(jnp.mean(x * x, axis=-1, keepdims=True) + EPS) * w

        def _attention(x, wq, wk, wv, wo):
            B, S, _ = x.shape
            q = (x @ wq).reshape(B, S, HEADS, HEAD_DIM).transpose(0, 2, 1, 3)
            k = (x @ wk).reshape(B, S, HEADS, HEAD_DIM).transpose(0, 2, 1, 3)
            v = (x @ wv).reshape(B, S, HEADS, HEAD_DIM).transpose(0, 2, 1, 3)
            cos, sin = _rope_tables(S, HEAD_DIM)
            cos = cos[None, None]
            sin = sin[None, None]
            q = q * cos + _rotate_half(q) * sin
            k = k * cos + _rotate_half(k) * sin
            scale = HEAD_DIM ** (-0.5)
            scores = jnp.einsum('bhqd,bhkd->bhqk', q, k) * scale
            causal = jnp.triu(jnp.ones((S, S), bool), k=1)
            scores = jnp.where(causal, -jnp.inf, scores)
            attn = jax.nn.softmax(scores, axis=-1)
            out = jnp.einsum('bhqk,bhkd->bhqd', attn, v)
            out = out.transpose(0, 2, 1, 3).reshape(B, S, EMBED)
            return out @ wo

        def _moe(x, w_router, wg, wu, wd):
            B, S, E = x.shape
            xf = x.reshape(-1, E)
            logits = xf @ w_router
            probs = jax.nn.softmax(logits, axis=-1)
            topw, topi = jax.lax.top_k(probs, TOP_K)
            topw = topw / jnp.sum(topw, axis=-1, keepdims=True)
            combine = jnp.sum(jax.nn.one_hot(topi, NUM_EXPERTS, dtype=xf.dtype) * topw[..., None], axis=1)
            g = jax.nn.silu(jnp.einsum('td,xdh->txh', xf, wg))
            u = jnp.einsum('td,xdh->txh', xf, wu)
            eo = jnp.einsum('txh,xhd->txd', g * u, wd)
            out = jnp.einsum('txd,tx->td', eo, combine)
            return out.reshape(B, S, E)
        h = x + _attention(_rmsnorm(x, g1), wq, wk, wv, wo)
        y = h + _moe(_rmsnorm(h, g2), w_router, wg, wu, wd)
        return y

    def _L1_xattn_ref(x, mem, Wq, Wkv, Wout, bout):
        import jax, jax.numpy as jnp
        import numpy as np
        HEADS = 16
        b, n, dim = x.shape
        h = HEADS
        d = dim // h
        scale = d ** (-0.5)
        mem_len = mem.shape[1]
        q = x @ Wq
        xc = jnp.concatenate((mem, x), axis=1)
        kv = xc @ Wkv
        k, v = jnp.split(kv, 2, axis=-1)

        def to_heads(t):
            bb, nn, _ = t.shape
            return t.reshape(bb, nn, h, d).transpose(0, 2, 1, 3)
        q, k, v = (to_heads(q), to_heads(k), to_heads(v))
        dots = jnp.einsum('bhid,bhjd->bhij', q, k) * scale
        j = dots.shape[-1]
        i_idx = jnp.arange(n)[:, None]
        j_idx = jnp.arange(j)[None, :]
        mask = j_idx > i_idx + mem_len
        dots = jnp.where(mask[None, None], -jnp.inf, dots)
        attn = jax.nn.softmax(dots, axis=-1)
        out = jnp.einsum('bhij,bhjd->bhid', attn, v)
        out = out.transpose(0, 2, 1, 3).reshape(b, n, dim)
        return out @ Wout + bout

    def _L1_ffn_ref(tgt, router_w, router_b, w1, b1, w2, b2, gamma, beta):
        import jax, jax.numpy as jnp
        import numpy as np
        B, S, D, F, E = (2, 512, 256, 1024, 8)
        LN_EPS = 1e-05

        def _xavier(key, shape, fan_in, fan_out):
            a = np.sqrt(6.0 / (fan_in + fan_out))
            return jax.random.uniform(key, shape, jnp.float32, -a, a)
        logits = jnp.einsum('bsd,ed->bse', tgt, router_w) + router_b
        rw = jax.nn.softmax(logits, axis=-1)
        rw = jnp.zeros_like(rw).at[..., 0].set(1.0)
        h = jax.nn.relu(jnp.einsum('bsd,edf->besf', tgt, w1) + b1[None, :, None, :])
        eo = jnp.einsum('besf,efd->besd', h, w2) + b2[None, :, None, :]
        tgt2 = jnp.einsum('besd,bse->bsd', eo, rw)
        x = tgt + tgt2
        mean = jnp.mean(x, axis=-1, keepdims=True)
        var = jnp.mean(jnp.square(x - mean), axis=-1, keepdims=True)
        return (x - mean) * jax.lax.rsqrt(var + LN_EPS) * gamma + beta
    x = x + _L0_xattn_ref(_layernorm(x, axis=-1), ctx_1024, ctx_1024, L0_xattn_w_q, L0_xattn_b_q, L0_xattn_w_k, L0_xattn_b_k, L0_xattn_w_v, L0_xattn_b_v, L0_xattn_w_o, L0_xattn_b_o)
    x = x + _L0_ffn_ref(_layernorm(x, axis=-1), L0_ffn_wq, L0_ffn_wk, L0_ffn_wv, L0_ffn_wo, L0_ffn_w_router, L0_ffn_wg, L0_ffn_wu, L0_ffn_wd, L0_ffn_g1, L0_ffn_g2)
    x = x + _L1_xattn_ref(_layernorm(x, axis=-1), ctx_1024, L1_xattn_Wq, L1_xattn_Wkv, L1_xattn_Wout, L1_xattn_bout)
    x = x + _L1_ffn_ref(_layernorm(x, axis=-1), L1_ffn_router_w, L1_ffn_router_b, L1_ffn_w1, L1_ffn_b1, L1_ffn_w2, L1_ffn_b2, L1_ffn_gamma, L1_ffn_beta)
    return x

_drawn_inputs = setup_inputs


def setup_inputs(seed=0):
    import zlib

    import numpy as np

    out = dict(_drawn_inputs(seed))
    spreads = {'L0_xattn_b_q': (0.0, 0.479),
     'L0_xattn_b_k': (0.0, 2.0),
     'L0_xattn_b_v': (0.0, 0.1),
     'L0_xattn_b_o': (0.0, 0.1),
     'L0_ffn_g1': (1.0, 0.6),
     'L0_ffn_g2': (1.0, 0.6),
     'L1_xattn_bout': (0.0, 0.8),
     'L1_ffn_router_b': (0.0, 0.1),
     'L1_ffn_b1': (0.0, 1.407),
     'L1_ffn_b2': (0.0, 1.192),
     'L1_ffn_gamma': (1.0, 0.6),
     'L1_ffn_beta': (0.0, 0.8)}
    factors = {'L0_ffn_wq': 8.0,
     'L0_ffn_wk': 8.0,
     'L0_ffn_w_router': 6.357,
     'L0_ffn_wg': 5.701,
     'L0_ffn_wu': 5.641,
     'L0_ffn_wd': 5.595,
     'L1_xattn_Wq': 4.643}
    for name, (base, spread) in spreads.items():
        noise = np.random.default_rng([zlib.crc32(name.encode()), seed]).standard_normal(out[name].shape)
        drawn = base * np.exp(spread * noise) if base else spread * noise
        out[name] = jnp.asarray(drawn.astype(out[name].dtype))
    for name, factor in factors.items():
        out[name] = (out[name] * factor).astype(out[name].dtype)
    return out
```

```python
from contextlib import ExitStack

import concourse.bass as bass
from concourse import mybir

ALU = mybir.AluOpType
ACT = mybir.ActivationFunctionType
F32 = mybir.dt.float32
BF16 = mybir.dt.bfloat16
AX_X = mybir.AxisListType.X

P = 128
S = 2048
C = 1601
D = 256
H = 16
DK = D // H
KH = D // P
NT = S // P
NC = -(-C // P)
QB = 512
NB = S // QB
SPB = QB // P
G = 4
NG = H // G
VW = 32
E = 8
F0 = 704
F1 = 1024
NEG = -1.0e30
SCALE = DK ** -0.5
LN_EPS = 1e-5
RMS_EPS = 1e-6

Q_PARTS = (0, 0, 0, 1, 1, 2)
K_PARTS = (0, 1, 2, 0, 1, 0)
PEAK_ROW = 6 * DK
SCORE_ROWS = PEAK_ROW + 3


def dims(ap, *shape):
    if len(shape) == 1:
        return ap
    if len(shape) == 2:
        return ap.rearrange("p (a b) -> p a b", a=shape[0])
    return ap.rearrange("p (a b c) -> p a b c", a=shape[0], b=shape[1])


def build(nc, a, out):
    with ExitStack() as ctx:
        roles = {}

        def sem(role):
            if role not in roles:
                roles[role] = ctx.enter_context(nc.semaphore(role))
            return roles[role]

        def sb(name, shape, dt=F32):
            return ctx.enter_context(nc.sbuf_tensor(name, shape, dt))

        def scratch(name, shape, dt):
            return nc.dram_tensor(name, shape, dt, kind="Internal").ap()

        X = sb("X", [P, NT, D])
        XN = sb("XN", [P, NT, D])
        identity = sb("identity", [P, P])
        identity16 = sb("identity16", [P, P], BF16)
        mask_qk = sb("mask_qk", [P, P], BF16)
        mask_kq = sb("mask_kq", [P, P], BF16)
        ones = sb("ones", [1, P])
        minus_half = sb("minus_half", [P, NT])
        stats = sb("stats", [P, 4, NT])
        values = sb("values", [P, 2, H, VW])
        weights = {}
        for name, width in (("q0", D), ("k0", D), ("v0", D), ("o0", D), ("q1", D), ("q1_turned", D),
                            ("k1", D), ("k1_turned", D), ("v1", D), ("o1", D), ("q2", D), ("kv2", 2 * D),
                            ("o2", D), ("router", E)):
            weights[name] = sb(f"w_{name}", [P, KH, width])
        rows = sb("rows", [1, 4, D])
        ROW = {"v0": 0, "o0": 1, "o2": 2, "b2": 3}
        cols = sb("cols", [P, 4, KH])
        COL = {"q0": 0, "k0": 1, "g1": 2, "g2": 3}
        ARENA = 34000
        arena = sb("arena", [P, ARENA])
        PS = ctx.enter_context(nc.psum_tensor("PS", [P, 8, QB], F32))

        def carver():
            at = [0]

            def take(*shape, dt=F32):
                n = 1
                for x in shape:
                    n *= x
                words = n if dt == F32 else -(-n // 2)
                part = arena[:, at[0]:at[0] + words]
                at[0] += words
                assert at[0] <= ARENA, at[0]
                if dt != F32:
                    part = part.bitcast(dt)[:, 0:n]
                return dims(part, *shape)
            return take

        q_parts = [scratch(f"q_parts{i}", (3, D, S), BF16) for i in range(3)]
        k_parts_ctx = {i: scratch(f"k_parts_ctx{i}", (3, D, C), BF16) for i in (0, 2)}
        k_parts_own = {i: scratch(f"k_parts_own{i}", (3, D, S), BF16) for i in (1, 2)}
        v_ctx = {i: scratch(f"v_ctx{i}", (NC * P, H * VW), F32) for i in (0, 2)}
        v_own = {i: scratch(f"v_own{i}", (S, H * VW), F32) for i in (1, 2)}


        class Setup:

            def __init__(self):
                self.loaded = sem("setup_loaded")
                self.made = sem("setup_made")
                self.weights = (("q0", "wq0"), ("k0", "wk0"), ("v0", "wv0"), ("o0", "wo0"), ("q1", "wq1"),
                                ("q1_turned", "wq1t"), ("k1", "wk1"), ("k1_turned", "wk1t"), ("v1", "wv1"),
                                ("o1", "wo1"), ("q2", "wq2"), ("kv2", "wkv2"), ("o2", "wo2"), ("router", "wr"))
                take = carver()
                self.masks = take(2, P)

            def sp(self, eng):
                eng.dma_start(identity[:], a["identity"]).then_inc(self.loaded, 16)
                eng.dma_start(self.masks, a["masks"].rearrange("m p c -> p m c")).then_inc(self.loaded, 16)
                eng.dma_start(X[:], a["x"].rearrange("(t p) d -> p t d", p=P)).then_inc(self.loaded, 16)
                for name, src in self.weights:
                    eng.dma_start(weights[name][:], a[src].rearrange("(k p) n -> p k n", p=P)).then_inc(self.loaded, 16)
                eng.dma_start(rows[:], a["rows"].rearrange("(o r) d -> o r d", o=1)).then_inc(self.loaded, 16)
                eng.dma_start(cols[:], a["cols"].rearrange("p (r k) -> p r k", r=4)).then_inc(self.loaded, 16)
                eng.wait_ge(self.loaded, 16 * (5 + len(self.weights)))

            def act(self, eng):
                pass

            def pe(self, eng):
                pass

            def dve(self, eng):
                eng.wait_ge(self.loaded, 16 * (5 + len(self.weights)))
                eng.tensor_copy(identity16[:], identity[:])
                eng.tensor_copy(mask_qk[:], self.masks[:, 0, :])
                eng.tensor_copy(mask_kq[:], self.masks[:, 1, :])

            def pool(self, eng):
                eng.memset(ones[:], 1.0)
                eng.memset(minus_half[:], -0.5)
                eng.memset(values[:], 0.0).then_inc(self.made, 1)
                eng.wait_ge(self.made, 1)
                eng.memset(values[:, :, :, DK:DK + 1], 1.0)

        class Turn:

            def __init__(self, sources, dst, gain=None):
                self.sources, self.dst, self.gain = sources, dst, gain
                self.turned, self.copied = sem("turn_turned"), sem("turn_copied")
                self.jobs = [(b, half) for b in range(0, len(sources), SPB) for half in range(KH)]

            def pe(self, eng):
                for n, (b, half) in enumerate(self.jobs):
                    if n >= 2:
                        eng.wait_ge(self.copied, n - 1)
                    for i, (src, r) in enumerate(self.sources[b:b + SPB]):
                        last = eng.transpose(PS[:, n % 2, i * P:i * P + r], src[0:r, half * P:(half + 1) * P],
                                             identity[0:r, 0:r])
                    last.then_inc(self.turned, 1)

            def act(self, eng):
                for n, (b, half) in enumerate(self.jobs):
                    w = sum(r for _, r in self.sources[b:b + SPB])
                    eng.wait_ge(self.turned, n + 1)
                    scale = 1.0 if self.gain is None else self.gain[:, half:half + 1]
                    eng.activation(self.dst[:, half, b * P:b * P + w], PS[:, n % 2, 0:w], ACT.Identity,
                                   scale=scale).then_inc(self.copied, 1)

        class Project:

            def __init__(self, take, src, jobs, value_jobs, cos=None, sin=None):
                self.src, self.jobs, self.value_jobs, self.cos, self.sin = src, jobs, value_jobs, cos, sin
                self.full = take(4, QB)
                self.parts = take(4, 3, QB, dt=BF16)
                self.rope = take(2, QB) if cos is not None else None
                self.projected = sem("project_projected")
                self.full_ready = sem("project_full_ready")
                self.high_ready = sem("project_high_ready")
                self.rest_ready = sem("project_rest_ready")
                self.middle_ready = sem("project_middle_ready")
                self.low_ready = sem("project_low_ready")
                self.rotated = sem("project_rotated")
                self.parts_stored = [sem(f"project_parts_stored{i}") for i in range(4)]
                self.value_projected = sem("project_value_projected")
                self.value_staged = sem("project_value_staged")
                self.value_stored = [sem(f"project_value_stored{i}") for i in range(2)]
                self.steps = max(len(jobs), len(value_jobs))

            def pe(self, eng):
                for n in range(self.steps):
                    if n < len(self.jobs):
                        j = self.jobs[n]
                        if n >= 3:
                            eng.wait_ge(self.full_ready, n - 2)
                        for bank, w in ((n % 3, j["w"]), (3 + n % 3, j.get("turned"))):
                            if w is None:
                                continue
                            for k in range(KH):
                                last = eng.matmul(PS[:, bank, 0:j["n"]], w[:, k, j["half"] * P:(j["half"] + 1) * P],
                                                  self.src[:, k, j["c0"]:j["c0"] + j["n"]],
                                                  start=(k == 0), stop=(k == KH - 1))
                        last.then_inc(self.projected, 1)
                    if n < len(self.value_jobs):
                        v = self.value_jobs[n]
                        if n >= 2:
                            eng.wait_ge(self.value_staged, n - 1)
                        r, dst = v["rows"], PS[0:v["rows"], 6 + n % 2, 0:D]
                        for k in range(KH):
                            last = eng.matmul(dst, self.src[:, k, v["c0"]:v["c0"] + r], v["w"][:, k, :],
                                              start=(k == 0), stop=(k == KH - 1 and v["bias"] is None))
                        if v["bias"] is not None:
                            last = eng.matmul(dst, ones[0:1, 0:r], v["bias"], start=False, stop=True)
                        last.then_inc(self.value_projected, 1)

            def act(self, eng):
                for n in range(max(self.steps, len(self.jobs) + 1)):
                    if n < len(self.jobs):
                        j = self.jobs[n]
                        eng.wait_ge(self.full_ready, n + 1)
                        if n >= 4:
                            eng.wait_ge(self.parts_stored[n % 4], 16 * (n // 4))
                        eng.activation(self.parts[:, n % 4, 0, 0:j["n"]], self.full[:, n % 4, 0:j["n"]],
                                       ACT.Copy).then_inc(self.high_ready, 1)
                    if 1 <= n <= len(self.jobs):
                        m = n - 1
                        w = self.jobs[m]["n"]
                        eng.wait_ge(self.rest_ready, m + 1)
                        eng.activation(self.parts[:, m % 4, 1, 0:w], self.full[:, m % 4, 0:w],
                                       ACT.Copy).then_inc(self.middle_ready, 1)
                    if n < len(self.value_jobs):
                        r = self.value_jobs[n]["rows"]
                        eng.wait_ge(self.value_projected, n + 1)
                        if n >= 2:
                            eng.wait_ge(self.value_stored[n % 2], 16 * (n // 2))
                        eng.activation(values[0:r, n % 2, :, 0:DK],
                                       PS[0:r, 6 + n % 2, 0:D].rearrange("p (h d) -> p h d", h=H),
                                       ACT.Copy).then_inc(self.value_staged, 1)

            def dve(self, eng):
                turned = 0
                for n in range(len(self.jobs) + 2):
                    if n < len(self.jobs):
                        j = self.jobs[n]
                        w, full = j["n"], self.full[:, n % 4, 0:j["n"]]
                        eng.wait_ge(self.projected, n + 1)
                        if n >= 4:
                            eng.wait_ge(self.low_ready, n - 3)
                        if j.get("turned") is not None:
                            rope = slice(j["c0"], j["c0"] + w)
                            if n:
                                eng.wait_ge(self.full_ready, n)
                            eng.scalar_tensor_tensor(out=self.rope[:, 0, 0:w], in0=PS[:, n % 3, 0:w], scalar=j["scale"],
                                                     in1=self.cos[:, rope], op0=ALU.mult, op1=ALU.mult)
                            eng.scalar_tensor_tensor(out=self.rope[:, 1, 0:w], in0=PS[:, 3 + n % 3, 0:w],
                                                     scalar=j["scale"], in1=self.sin[:, rope], op0=ALU.mult,
                                                     op1=ALU.mult).then_inc(self.rotated, 1)
                            turned += 1
                            eng.wait_ge(self.rotated, turned)
                            eng.tensor_tensor(full, self.rope[:, 0, 0:w], self.rope[:, 1, 0:w],
                                              ALU.add).then_inc(self.full_ready, 1)
                        elif j.get("bias") is not None:
                            eng.tensor_scalar(full, PS[:, n % 3, 0:w], j["bias"], j["scale"], ALU.add,
                                              ALU.mult).then_inc(self.full_ready, 1)
                        else:
                            eng.tensor_scalar(full, PS[:, n % 3, 0:w], j["scale"], None,
                                              ALU.mult).then_inc(self.full_ready, 1)
                    if 1 <= n <= len(self.jobs):
                        m = n - 1
                        w = self.jobs[m]["n"]
                        eng.wait_ge(self.high_ready, m + 1)
                        eng.tensor_tensor(self.full[:, m % 4, 0:w], self.full[:, m % 4, 0:w],
                                          self.parts[:, m % 4, 0, 0:w], ALU.subtract).then_inc(self.rest_ready, 1)
                    if n >= 2:
                        m = n - 2
                        w = self.jobs[m]["n"]
                        eng.wait_ge(self.middle_ready, m + 1)
                        eng.tensor_tensor(self.parts[:, m % 4, 2, 0:w], self.full[:, m % 4, 0:w],
                                          self.parts[:, m % 4, 1, 0:w], ALU.subtract).then_inc(self.low_ready, 1)

            def sp(self, eng):
                for n in range(self.steps):
                    if n < len(self.value_jobs):
                        v = self.value_jobs[n]
                        r = v["rows"]
                        eng.wait_ge(self.value_staged, n + 1)
                        eng.dma_start(v["dst"][v["c0"]:v["c0"] + r, :],
                                      values[0:r, n % 2].rearrange("p h d -> p (h d)")
                                      ).then_inc(self.value_stored[n % 2], 16)
                    if n < len(self.jobs):
                        j = self.jobs[n]
                        eng.wait_ge(self.low_ready, n + 1)
                        dst = j["dst"][:, j["half"] * P:(j["half"] + 1) * P, j["c0"]:j["c0"] + j["n"]]
                        eng.dma_start(dst.rearrange("a p c -> p a c"),
                                      self.parts[:, n % 4, :, 0:j["n"]]).then_inc(self.parts_stored[n % 4], 16)
                for i in range(4):
                    eng.wait_ge(self.parts_stored[i], 16 * len(range(i, len(self.jobs), 4)))
                for i in range(2):
                    eng.wait_ge(self.value_stored[i], 16 * len(range(i, len(self.value_jobs), 2)))

        def feature_jobs(w, dst, width, scale=1.0, bias=None, turned=None):
            return [dict(w=w, turned=turned, bias=None if bias is None else bias[:, half:half + 1], scale=scale,
                         dst=dst, half=half, c0=c0, n=min(QB, width - c0))
                    for c0 in range(0, width, QB) for half in range(KH)]

        def value_jobs(w, dst, width, bias=None):
            return [dict(w=w, bias=bias, dst=dst, c0=c0, rows=min(P, width - c0)) for c0 in range(0, width, P)]

        class Context:

            def __init__(self):
                take = carver()
                self.rows = take(NC, D)
                turned = take(KH, NC * P)
                self.loaded = sem("ctx_loaded")
                self.turn = Turn([(self.rows[:, t], min(P, C - t * P)) for t in range(NC)], turned)
                kv2 = weights["kv2"]
                self.project = Project(
                    take, turned,
                    feature_jobs(weights["k0"], k_parts_ctx[0], C, bias=cols[:, COL["k0"], :])
                    + feature_jobs(kv2[:, :, 0:D], k_parts_ctx[2], C),
                    value_jobs(weights["v0"], v_ctx[0], C, bias=rows[:, ROW["v0"], :])
                    + value_jobs(kv2[:, :, D:2 * D], v_ctx[2], C))

            def sp(self, eng):
                full = C // P
                eng.dma_start(self.rows[:, 0:full, :], a["ctx"][0:full * P, :].rearrange("(t p) d -> p t d", p=P)
                              ).then_inc(self.loaded, 16)
                eng.dma_start(self.rows[0:C - full * P, full, :], a["ctx"][full * P:C, :]).then_inc(self.loaded, 16)
                self.project.sp(eng)

            def pe(self, eng):
                eng.wait_ge(self.loaded, 32)
                self.turn.pe(eng)
                eng.wait_ge(self.turn.copied, len(self.turn.jobs))
                self.project.pe(eng)

            def act(self, eng):
                self.turn.act(eng)
                self.project.act(eng)

            def dve(self, eng):
                self.project.dve(eng)

            def pool(self, eng):
                pass

        class Normalize:

            def __init__(self, name, x, xn, squares, layer=True, rms=False):
                self.x, self.xn, self.squares, self.layer, self.rms = x, xn, squares, layer, rms
                self.step = sem(f"{name}_norm_step")
                self.centred = sem(f"{name}_centred")
                self.squared = sem(f"{name}_squared")
                self.spread = sem(f"{name}_spread")
                self.inverse = sem(f"{name}_inverse")
                self.done = sem(f"{name}_normed")
                self.rounds = int(layer) + int(rms)
                self.result = squares if rms else xn

            def over_rows(self, i):
                return stats[:, i, :].unsqueeze(2).to_broadcast([P, NT, D])

            def dve(self, eng):
                steps = 0
                if self.layer:
                    eng.tensor_reduce(stats[:, 0, :], self.x, AX_X, ALU.add).then_inc(self.step, 1)
                    eng.wait_ge(self.step, 1)
                    eng.tensor_scalar(stats[:, 1, :], stats[:, 0, :], 1.0 / D, None, ALU.mult).then_inc(self.step, 1)
                    eng.wait_ge(self.step, 2)
                    eng.tensor_tensor(self.xn, self.x, self.over_rows(1), ALU.subtract).then_inc(self.centred, 1)
                    steps = 2
                for n in range(self.rounds):
                    is_rms = self.rms and n == self.rounds - 1
                    eng.wait_ge(self.squared, n + 1)
                    eng.tensor_reduce(stats[:, 2, :], self.squares, AX_X, ALU.add).then_inc(self.step, 1)
                    steps += 1
                    eng.wait_ge(self.step, steps)
                    eng.tensor_scalar(stats[:, 2, :], stats[:, 2, :], 1.0 / D, RMS_EPS if is_rms else LN_EPS,
                                      ALU.mult, ALU.add).then_inc(self.spread, 1)
                    eng.wait_ge(self.inverse, n + 1)
                    eng.tensor_tensor(self.squares if is_rms else self.xn, self.xn, self.over_rows(3),
                                      ALU.mult).then_inc(self.done, 1)

            def act(self, eng):
                for n in range(self.rounds):
                    if n == 0 and self.layer:
                        eng.wait_ge(self.centred, 1)
                    elif n:
                        eng.wait_ge(self.done, n)
                    eng.activation(self.squares, self.xn, ACT.Square).then_inc(self.squared, 1)

            def pool(self, eng):
                for n in range(self.rounds):
                    eng.wait_ge(self.spread, n + 1)
                    eng.tensor_tensor(stats[:, 3, :], stats[:, 2, :], minus_half[:], ALU.pow).then_inc(self.inverse, 1)

        class Prepare:

            def __init__(self, i):
                self.i = i
                take = carver()
                squares = take(NT, D)
                turned = take(KH, S)
                self.norm = Normalize("norm", X[:], XN[:], squares, rms=(i == 1))
                self.turn = Turn([(self.norm.result[:, t], P) for t in range(NT)], turned,
                                 gain=cols[:, COL["g1"], :] if i == 1 else None)
                self.tables_loaded = None
                if i == 0:
                    jobs, values_of = feature_jobs(weights["q0"], q_parts[0], S, SCALE, cols[:, COL["q0"], :]), []
                    self.project = Project(take, turned, jobs, values_of)
                elif i == 1:
                    self.tables = take(2, S)
                    self.tables_loaded = sem("prep1_tables_loaded")
                    jobs = (feature_jobs(weights["q1"], q_parts[1], S, SCALE, turned=weights["q1_turned"])
                            + feature_jobs(weights["k1"], k_parts_own[1], S, turned=weights["k1_turned"]))
                    self.project = Project(take, turned, jobs, value_jobs(weights["v1"], v_own[1], S),
                                           cos=self.tables[:, 0], sin=self.tables[:, 1])
                else:
                    jobs = (feature_jobs(weights["q2"], q_parts[2], S, SCALE)
                            + feature_jobs(weights["kv2"][:, :, 0:D], k_parts_own[2], S))
                    self.project = Project(take, turned, jobs,
                                           value_jobs(weights["kv2"][:, :, D:2 * D], v_own[2], S))

            def sp(self, eng):
                if self.tables_loaded is not None:
                    eng.dma_start(self.tables, a["rope"].rearrange("m p s -> p m s")).then_inc(self.tables_loaded, 16)
                self.project.sp(eng)

            def pe(self, eng):
                eng.wait_ge(self.norm.done, self.norm.rounds)
                self.turn.pe(eng)
                eng.wait_ge(self.turn.copied, len(self.turn.jobs))
                self.project.pe(eng)

            def act(self, eng):
                self.norm.act(eng)
                self.turn.act(eng)
                self.project.act(eng)

            def dve(self, eng):
                self.norm.dve(eng)
                if self.tables_loaded is not None:
                    eng.wait_ge(self.tables_loaded, 16)
                self.project.dve(eng)

            def pool(self, eng):
                self.norm.pool(eng)

        class Attention:

            BLOCKS = 2 * NB

            def __init__(self, i, has_ctx, has_own):
                self.i, self.has_ctx, self.has_own = i, has_ctx, has_own
                name = "attention"
                self.own0 = C + C % 2 if has_ctx else 0
                self.keys = self.own0 + (S if has_own else 0)
                self.nctx = NC if has_ctx else 0
                self.nv = self.nctx + (NT if has_own else 0)
                take = carver()
                self.k = [take(G, self.keys, dt=BF16) for _ in range(2)]
                self.v = [take(self.nv, G, VW) for _ in range(2)]
                self.q = [take(G, QB, dt=BF16) for _ in range(NB)]
                self.probs = [[take(2, QB) for _ in range(2)] for _ in range(2)]
                self.sums = [take(QB) for _ in range(2)]
                self.attended = XN[:] if i != 1 else take(NT, D)
                self.peaks = take(SPB * G, 8)
                self.peak = take(3, SPB * G)
                self.peak_parts = take(P // (SPB * G), SPB * G, dt=BF16)
                self.peak_rows = take(P, dt=BF16)
                self.inverse = take(SPB, G)
                self.kv_landed = [sem(f"{name}_kv_landed{i}") for i in range(2)]
                self.q_landed = [sem(f"{name}_q_landed{i}") for i in range(NB)]
                self.ones_set = sem(f"{name}_ones_set")
                self.ring_ready = sem(f"{name}_ring_ready")
                self.ring_read = sem(f"{name}_ring_read")
                self.peaks_split = sem(f"{name}_peaks_split")
                self.peaks_copied = sem(f"{name}_peaks_copied")
                self.peaks_landed = sem(f"{name}_peaks_landed")
                self.scores_ready = sem(f"{name}_scores_ready")
                self.probs_ready = sem(f"{name}_probs_ready")
                self.probs_used = sem(f"{name}_probs_used")
                self.sums_copied = sem(f"{name}_sums_copied")
                self.chain = sem(f"{name}_chain")
                self.plan()


            RING = (4, 5, 7)

            def plan(self):
                self.pieces = [self.pieces_of(b) for b in range(NB)]
                self.units = [self.units_of(b) for b in range(NB)]
                while (2 * sum(map(len, self.pieces)) + 2 * self.BLOCKS) % len(self.RING):
                    self.pieces[0].append(min(self.pieces[0], key=lambda x: sum(w for _, _, w, _ in x[3])))
                self.units_loop = 2 * sum(map(len, self.units))
                assert self.units_loop % 2 == 0
                self.first = [("piece", 0, k) for k in range(len(self.pieces[0]))] + [("peaks", 0, 0)]
                self.steps, last = [], None
                for n in range(self.BLOCKS):
                    nu, np = len(self.units[n % NB]), len(self.pieces[(n + 1) % NB])
                    until, k = 4 * max(nu - 3, 1), 0
                    for u in range(nu):
                        for spot in range(4):
                            if spot < 2:
                                self.steps.append(("scores", n, (u, spot)))
                            elif spot == 2 and last is not None:
                                self.steps.append(("attend", *last))
                            while k < np and k * until < (4 * u + spot + 1) * np:
                                self.steps.append(("piece", n + 1, k))
                                k += 1
                        if n and u == 1:
                            self.steps.append(("sums", n - 1, 0))
                        if u == max(nu - 2, 1):
                            assert k == np
                            self.steps.append(("peaks", n + 1, 0))
                        last = (n, u)
                self.steps += [("attend", *last), ("sums", self.BLOCKS - 1, 0)]
                in_ring = ("piece", "peaks", "sums")
                self.ring_first = len(self.first)
                self.ring_loop = sum(x[0] in in_ring for x in self.steps)
                assert self.ring_loop % len(self.RING) == 0

            def walk(self, steps, start):
                for what, n, x in steps:
                    if what in ("piece", "peaks", "sums"):
                        yield what, n, x, start
                        start += 1
                    else:
                        yield what, n, x, None

            def ring_bank(self, r):
                return self.RING[r % len(self.RING)]

            def pieces_of(self, b):
                found = []
                for j in range(G):
                    for s in range(SPB):
                        runs = [(0, C, None)] if self.has_ctx else []
                        if self.has_own:
                            own = (SPB * b + s) * P
                            if own:
                                runs.append((self.own0, own, None))
                            runs.append((self.own0 + own, P, 0))
                        banks, at = [[]], 0
                        for k0, n, m in runs:
                            while n:
                                if at == QB:
                                    banks.append([])
                                    at = 0
                                w = min(n, QB - at)
                                banks[-1].append((at, k0, w, m))
                                at, k0, n = at + w, k0 + w, n - w
                                m = None if m is None else m + w
                        found += [(j, s, c, parts) for c, parts in enumerate(banks)]
                return found

            def banks(self, b, s):
                return 1 + max(c for _, t, c, _ in self.pieces[b] if t == s)

            def units_of(self, b):
                units = [(t * P, min(P, C - t * P), t, 0, False) for t in range(self.nctx)]
                if self.has_own:
                    for t in range(SPB * (b + 1)):
                        units.append((self.own0 + t * P, P, self.nctx + t, max(0, t - SPB * b) * P, t >= SPB * b))
                return units

            def before(self, n, of):
                return sum(len(of[m % NB]) for m in range(n))

            def attended_count(self, it, n):
                return it * self.units_loop + self.before(n + 1, self.units) + 2


            def pe(self, eng):
                def piece(it, n, k, r):
                    b, par = n % NB, n // NB % 2
                    j, s, _, parts = self.pieces[b][k]
                    if k == 0:
                        eng.wait_ge(self.q_landed[b], it * (2 * 96) + 96 * (n // NB + 1))
                        if b == 0:
                            kv = 16 * self.kv_loads
                            eng.wait_ge(self.kv_landed[par], it * kv + kv * (1 + n // self.BLOCKS))
                    eng.wait_ge(self.ring_read, it * self.ring_loop + r + 1)
                    todo = [(at, w, self.q[b][0:PEAK_ROW, j, s * P:(s + 1) * P],
                             self.k[par][0:PEAK_ROW, j, k0:k0 + w]) for at, k0, w, _ in parts]
                    todo += [(at, w, identity16[:], mask_qk[:, m:m + w]) for at, _, w, m in parts if m is not None]
                    for x, (at, w, lhs, rhs) in enumerate(todo):
                        last = eng.matmul(PS[:, self.ring_bank(r), at:at + w], lhs, rhs, start=(x == 0),
                                          stop=(x == len(todo) - 1))
                    last.then_inc(self.ring_ready, 1)

                def turn_peaks(it, n, r):
                    eng.wait_ge(self.peaks_split, it * self.BLOCKS + n + 1)
                    eng.wait_ge(self.ring_read, it * self.ring_loop + r + 1)
                    eng.transpose(PS[:, self.ring_bank(r), :].bitcast(BF16)[:, 0:P],
                                  self.peak_parts[:, :, :].rearrange("p a b -> p (a b)"),
                                  identity16[:]).then_inc(self.ring_ready, 1)

                def scores(it, n, u, pair):
                    b, par = n % NB, n // NB
                    count = self.before(n, self.units) + u
                    k0, r, _, q0, masked = self.units[b][u]
                    if u == 0 and pair == 0:
                        eng.wait_ge(self.peaks_landed, it * (16 * self.BLOCKS) + 16 * (n + 1))
                    eng.wait_ge(self.probs_ready, it * (2 * self.units_loop) + 2 * count + pair + 1)
                    for h in range(2):
                        j = 2 * pair + h
                        last = eng.matmul(PS[0:r, j, q0:QB], self.k[par][0:SCORE_ROWS, j, k0:k0 + r],
                                          self.q[b][0:SCORE_ROWS, j, q0:QB], start=True, stop=not masked)
                        if masked:
                            last = eng.matmul(PS[:, j, q0:q0 + P], identity16[:], mask_kq[:], start=False, stop=True)
                    last.then_inc(self.scores_ready, 1)

                def attend(it, n, u):
                    b, par = n % NB, n // NB
                    count = self.before(n, self.units) + u
                    _, r, t, q0, _ = self.units[b][u]
                    eng.wait_ge(self.probs_ready, it * (2 * self.units_loop) + 2 * count + 4)
                    if u == 0:
                        eng.wait_ge(self.sums_copied, it * self.BLOCKS + n + 1)
                    for j in range(G):
                        last = eng.matmul(PS[VW * j:VW * (j + 1), 6, q0:QB], self.v[par][0:r, t, j, :],
                                          self.probs[count % 2][j // 2][0:r, j % 2, q0:QB],
                                          start=(u == 0), stop=(u == len(self.units[b]) - 1))
                    last.then_inc(self.probs_used, 1)

                def turn_sums(it, n, r):
                    eng.wait_ge(self.sums_copied, it * self.BLOCKS + n + 2)
                    eng.wait_ge(self.ring_read, it * self.ring_loop + r + 1)
                    for s in range(SPB):
                        last = eng.transpose(PS[:, self.ring_bank(r), s * P:(s + 1) * P],
                                             self.sums[n % 2][:, s * P:(s + 1) * P], identity[:])
                    last.then_inc(self.ring_ready, 1)

                def do(it, steps, start):
                    for what, n, x, r in self.walk(steps, start):
                        if what == "piece":
                            piece(it, n, x, r)
                        elif what == "peaks":
                            turn_peaks(it, n, r)
                        elif what == "sums":
                            turn_sums(it, n, r)
                        elif what == "scores":
                            scores(it, n, *x)
                        else:
                            attend(it, n, x)

                eng.sem_inc(self.probs_used, 2)
                eng.wait_ge(self.ones_set, 2)
                do(0, self.first, 0)
                with eng.Fori(0, NG // 2) as it:
                    do(it, self.steps, self.ring_first)


            def act(self, eng):
                eng.sem_inc(self.probs_ready, 2)
                with eng.Fori(0, NG // 2) as it:
                    count = 0
                    for n in range(self.BLOCKS):
                        for _, r, _, q0, _ in self.units[n % NB]:
                            eng.wait_ge(self.probs_used, it * self.units_loop + count + 1)
                            for pair in range(2):
                                eng.wait_ge(self.scores_ready, it * (2 * self.units_loop) + 2 * count + pair + 1)
                                eng.activation(self.probs[count % 2][pair][0:r, :, q0:QB],
                                               PS[0:r, 2 * pair:2 * pair + 2, q0:QB], ACT.Exp
                                               ).then_inc(self.probs_ready, 1)
                            count += 1


            def dve(self, eng):
                LINKS = 5 * self.BLOCKS
                links = [0]

                def link(it, ins):
                    links[0] += 1
                    ins.then_inc(self.chain, 1)
                    eng.wait_ge(self.chain, it * LINKS + links[0])

                def piece(it, n, k, r):
                    j, s, c, parts = self.pieces[n % NB][k]
                    width = parts[-1][0] + parts[-1][2]
                    eng.wait_ge(self.ring_ready, it * self.ring_loop + r + 1)
                    if self.pieces[n % NB].index(self.pieces[n % NB][k]) < k:
                        eng.wait_ge(self.ring_read, it * self.ring_loop + r + 3)
                    eng.tensor_reduce(self.peaks[:, G * s + j, c:c + 1], PS[:, self.ring_bank(r), 0:width], AX_X,
                                      ALU.max).then_inc(self.ring_read, 1)

                def split_peaks(it, n, r):
                    eng.wait_ge(self.ring_read, it * self.ring_loop + r + 4)
                    for s in range(SPB):
                        last = eng.tensor_reduce(self.peak[:, 0, :].rearrange("p (j s) -> p j s", j=G)[:, :, s],
                                                 self.peaks[:, G * s:G * (s + 1), 0:self.banks(n % NB, s)], AX_X,
                                                 ALU.max, negate=True)
                    link(it, last)
                    link(it, eng.tensor_copy(self.peak_parts[:, 0, :], self.peak[:, 0, :]))
                    link(it, eng.tensor_tensor(self.peak[:, 1, :], self.peak[:, 0, :], self.peak_parts[:, 0, :],
                                               ALU.subtract))
                    link(it, eng.tensor_copy(self.peak_parts[:, 1, :], self.peak[:, 1, :]))
                    eng.tensor_tensor(self.peak_parts[:, 2, :], self.peak[:, 1, :], self.peak_parts[:, 1, :],
                                      ALU.subtract).then_inc(self.peaks_split, 1)

                def copy_peaks(it, n, r):
                    eng.wait_ge(self.ring_ready, it * self.ring_loop + r + 1)
                    if n:
                        eng.wait_ge(self.peaks_landed, it * (16 * self.BLOCKS) + 16 * n)
                    rows48 = 3 * SPB * G
                    eng.tensor_copy(self.peak_rows[0:rows48, :],
                                    PS[0:rows48, self.ring_bank(r), :].bitcast(BF16)[:, 0:P]
                                    ).then_inc(self.peaks_copied, 1)
                    eng.wait_ge(self.peaks_copied, it * self.BLOCKS + n + 1)
                    eng.sem_inc(self.ring_read, 1)

                def copy_sums(it, n):
                    eng.wait_ge(self.probs_used, self.attended_count(it, n))
                    eng.tensor_copy(self.sums[n % 2], PS[:, 6, :]).then_inc(self.sums_copied, 1)

                def divide(it, n, r):
                    b, group = n % NB, n // NB
                    eng.wait_ge(self.ring_ready, it * self.ring_loop + r + 1)
                    turned = PS[:, self.ring_bank(r), :].rearrange("p (s j d) -> p s j d", s=SPB, j=G)
                    link(it, eng.reciprocal(self.inverse, turned[:, :, :, DK]))
                    dst = self.attended[:, SPB * b:SPB * (b + 1), bass.ds(it * (2 * G * DK) + group * (G * DK), G * DK)]
                    eng.tensor_tensor(dst.rearrange("p s (j d) -> p s j d", j=G), turned[:, :, :, 0:DK],
                                      self.inverse.unsqueeze(3).to_broadcast([P, SPB, G, DK]),
                                      ALU.mult).then_inc(self.ring_read, 1)

                def do(it, steps, start):
                    for what, n, x, r in self.walk(steps, start):
                        if what == "piece":
                            piece(it, n, x, r)
                            if x == len(self.pieces[n % NB]) - 1:
                                split_peaks(it, n, r)
                        elif what == "peaks":
                            copy_peaks(it, n, r)
                        elif what == "sums":
                            divide(it, n, r)
                        elif what == "attend" and x == len(self.units[n % NB]) - 1:
                            copy_sums(it, n)

                eng.sem_inc(self.ring_read, 3)
                eng.sem_inc(self.sums_copied, 1)
                link(0, eng.memset(self.peak_parts, 0.0))
                for par in range(2):
                    eng.memset(self.k[par][PEAK_ROW:SCORE_ROWS, :, :], 1.0).then_inc(self.ones_set, 1)
                do(0, self.first, 0)
                before = links[0]
                with eng.Fori(0, NG // 2) as it:
                    do(it, self.steps, self.ring_first)
                assert links[0] - before == LINKS, links[0]

            def pool(self, eng):
                pass


            @property
            def kv_loads(self):
                return (6 + 2) * self.has_ctx + (6 + 1) * self.has_own

            def sp(self, eng):
                i, GD = self.i, G * DK

                def load_group(par, group):
                    done, n = self.kv_landed[par], 0
                    for own, src, c0, w in ((False, k_parts_ctx.get(i), 0, C), (True, k_parts_own.get(i), self.own0, S)):
                        if not (self.has_own if own else self.has_ctx):
                            continue
                        for slot, part in enumerate(K_PARTS):
                            eng.dma_start(self.k[par][slot * DK:(slot + 1) * DK, :, c0:c0 + w],
                                          src[part, bass.ds(group * GD, GD), :].rearrange("(j d) c -> d j c", d=DK)
                                          ).then_inc(done, 16)
                            n += 1
                    cols_of = bass.ds(group * (G * VW), G * VW)
                    if self.has_ctx:
                        full = C // P
                        eng.dma_start(self.v[par][:, 0:full].rearrange("p t j w -> p t (j w)"),
                                      v_ctx[i][0:full * P, cols_of].rearrange("(t p) w -> p t w", p=P)).then_inc(done, 16)
                        eng.dma_start(self.v[par][0:C - full * P, full].rearrange("p j w -> p (j w)"),
                                      v_ctx[i][full * P:C, cols_of]).then_inc(done, 16)
                        n += 2
                    if self.has_own:
                        eng.dma_start(self.v[par][:, self.nctx:self.nv].rearrange("p t j w -> p t (j w)"),
                                      v_own[i][:, cols_of].rearrange("(t p) w -> p t w", p=P)).then_inc(done, 16)
                        n += 1
                    assert n == self.kv_loads, (n, self.kv_loads)

                def load_queries(b, group):
                    for slot, part in enumerate(Q_PARTS):
                        eng.dma_start(self.q[b][slot * DK:(slot + 1) * DK, :, :],
                                      q_parts[i][part, bass.ds(group * GD, GD), b * QB:(b + 1) * QB]
                                      .rearrange("(j d) c -> d j c", d=DK)).then_inc(self.q_landed[b], 16)

                def store_peaks(it, n):
                    eng.wait_ge(self.peaks_copied, it * self.BLOCKS + n + 1)
                    b = n % NB
                    eng.dma_start(self.q[b][PEAK_ROW:SCORE_ROWS].rearrange("p j (s c) -> p (j s) c", s=SPB),
                                  self.peak_rows[0:3 * SPB * G, :]).then_inc(self.peaks_landed, 16)

                load_queries(0, 0)
                load_group(0, 0)
                for b in range(1, NB):
                    load_queries(b, 0)
                load_group(1, 1)
                store_peaks(0, 0)
                with eng.Fori(0, NG // 2) as it:
                    for n in range(self.BLOCKS):
                        b, second = n % NB, n // NB
                        store_peaks(it, n + 1)
                        eng.wait_ge(self.probs_used, self.attended_count(it, n))
                        load_queries(b, it * 2 + 1 if not second else it * (-2) + 2)
                        if b == NB - 1:
                            load_group(second, it * (-2) + 2 + second)
                loops = NG // 2
                for b in range(NB):
                    eng.wait_ge(self.q_landed[b], 96 * (1 + 2 * loops))
                for par in range(2):
                    eng.wait_ge(self.kv_landed[par], 16 * self.kv_loads * (1 + loops))
                eng.wait_ge(self.peaks_landed, 16 * (1 + loops * self.BLOCKS))

        class Output:

            def __init__(self, i, attended, residual, dst, w, bias):
                self.w, self.bias, self.residual, self.dst = w, bias, residual, dst
                take = carver()
                if i == 1:
                    take(ARENA - KH * S)
                self.turned = take(KH, S)
                self.turn = Turn([(attended[:, t], P) for t in range(NT)], self.turned)
                self.projected, self.added = sem("out_projected"), sem("out_added")

            def pe(self, eng):
                self.turn.pe(eng)
                eng.wait_ge(self.turn.copied, len(self.turn.jobs))
                for n in range(NT // 2):
                    if n >= 4:
                        eng.wait_ge(self.added, n - 3)
                    for h in range(2):
                        t, dst = 2 * n + h, PS[:, 2 + n % 4, h * D:(h + 1) * D]
                        for k in range(KH):
                            last = eng.matmul(dst, self.turned[:, k, t * P:(t + 1) * P], self.w[:, k, :],
                                              start=(k == 0), stop=(k == KH - 1 and self.bias is None))
                        if self.bias is not None:
                            last = eng.matmul(dst, ones[0:1, :], self.bias, start=False, stop=True)
                    last.then_inc(self.projected, 1)

            def act(self, eng):
                self.turn.act(eng)

            def dve(self, eng):
                for n in range(NT // 2):
                    eng.wait_ge(self.projected, n + 1)
                    eng.tensor_tensor(self.dst[:, 2 * n:2 * n + 2, :],
                                      PS[:, 2 + n % 4, :].rearrange("p (t d) -> p t d", t=2),
                                      self.residual[:, 2 * n:2 * n + 2, :], ALU.add).then_inc(self.added, 1)

            def sp(self, eng):
                pass

            def pool(self, eng):
                pass

        class Experts:

            FT = -(-F0 // P)
            PER_PASS = 2 * NB * FT
            MIXED_PER_PASS = 4 * NB

            def __init__(self):
                take = carver()
                squares = take(NT, D)
                self.turned = take(KH, S)
                self.norm = Normalize("norm", None, XN[:], squares, layer=False, rms=True)
                self.turn = Turn([(squares[:, t], P) for t in range(NT)], self.turned,
                                 gain=cols[:, COL["g2"], :])
                self.router = [take(NT, E) for _ in range(5)]
                self.pairs = [take(NT, E * E) for _ in range(2)]
                self.earlier = take(E * E)
                self.row = [take(NT) for _ in range(2)]
                self.share = take(E, NT)
                self.shares = [take(NT) for _ in range(2)]
                self.gate = [take(KH, F0) for _ in range(2)]
                self.up = [take(KH, F0) for _ in range(2)]
                self.down = [take(self.FT, D) for _ in range(2)]
                self.acted = [take(QB) for _ in range(2)]
                self.hidden = [take(self.FT, QB) for _ in range(2)]
                self.earlier_loaded = sem("moe_earlier_loaded")
                self.w_landed = [sem(f"moe_w_landed{i}") for i in range(2)]
                self.routed = sem("moe_routed")
                self.router_read = sem("moe_router_read")
                self.route_chain = sem("moe_route_chain")
                self.shifted = sem("moe_shifted")
                self.route_exp = sem("moe_route_exp")
                self.hidden_ready = sem("moe_hidden_ready")
                self.activated = sem("moe_activated")
                self.gated = sem("moe_gated")
                self.mixed = sem("moe_mixed")
                self.added = sem("moe_added")
                self.share_set = sem("moe_share_set")

            def sp(self, eng):
                eng.dma_start(self.earlier, a["earlier"]).then_inc(self.earlier_loaded, 16)

                def load(par, e):
                    full = F0 // P
                    for dst, src in ((self.gate[par], a["wg"]), (self.up[par], a["wu"])):
                        eng.dma_start(dst, src[bass.ds(e * D, D), :].rearrange("(k p) f -> p k f", p=P)
                                      ).then_inc(self.w_landed[par], 16)
                    eng.dma_start(self.down[par][:, 0:full, :],
                                  a["wd"][bass.ds(e * F0, full * P), :].rearrange("(t p) d -> p t d", p=P)
                                  ).then_inc(self.w_landed[par], 16)
                    eng.dma_start(self.down[par][0:F0 - full * P, full, :],
                                  a["wd"][bass.ds(e * F0 + full * P, F0 - full * P), :]
                                  ).then_inc(self.w_landed[par], 16)

                load(0, 0)
                load(1, 1)
                with eng.Fori(0, E // 2 - 1) as it:
                    for par in range(2):
                        eng.wait_ge(self.mixed, it * self.MIXED_PER_PASS + 2 * NB * (par + 1) + 4)
                        load(par, it * 2 + (2 + par))
                eng.wait_ge(self.earlier_loaded, 16)
                for par in range(2):
                    eng.wait_ge(self.w_landed[par], 64 * (E // 2))

            def pool(self, eng):
                self.norm.pool(eng)

            def pe(self, eng):
                FT = self.FT
                eng.wait_ge(self.norm.done, 1)
                self.turn.pe(eng)
                eng.wait_ge(self.turn.copied, len(self.turn.jobs))
                for t in range(NT):
                    for k in range(KH):
                        last = eng.matmul(PS[:, 7, t * E:(t + 1) * E], self.turned[:, k, t * P:(t + 1) * P],
                                          weights["router"][:, k, :], start=(k == 0), stop=(k == KH - 1))
                last.then_inc(self.routed, 1)
                eng.sem_inc(self.mixed, 4)

                def mix(it, x):
                    eng.wait_ge(self.gated, it * self.PER_PASS + FT * (x + 1) + 2)
                    for half in range(2):
                        eng.wait_ge(self.added, it * self.MIXED_PER_PASS + 2 * x + half + 1)
                        for h in range(2):
                            s = 2 * half + h
                            for f in range(FT):
                                r = min(P, F0 - f * P)
                                last = eng.matmul(PS[:, 4 + half, h * D:(h + 1) * D],
                                                  self.hidden[x % 2][0:r, f, s * P:(s + 1) * P],
                                                  self.down[x // NB][0:r, f, :], start=(f == 0), stop=(f == FT - 1))
                        last.then_inc(self.mixed, 1)

                with eng.Fori(0, E // 2) as it:
                    for x in range(2 * NB):
                        par, b = x // NB, x % NB
                        if b == 0:
                            eng.wait_ge(self.w_landed[par], it * 64 + 64)
                        for f in range(FT):
                            r, count = min(P, F0 - f * P), x * FT + f
                            eng.wait_ge(self.gated, it * self.PER_PASS + count + 1)
                            for bank, w in ((2 * (count % 2), self.gate[par]), (2 * (count % 2) + 1, self.up[par])):
                                for k in range(KH):
                                    last = eng.matmul(PS[0:r, bank, :], w[:, k, f * P:f * P + r],
                                                      self.turned[:, k, b * QB:(b + 1) * QB],
                                                      start=(k == 0), stop=(k == KH - 1))
                            last.then_inc(self.hidden_ready, 1)
                            if x and f == 1:
                                mix(it, x - 1)
                    mix(it, 2 * NB - 1)

            def act(self, eng):
                FT = self.FT
                self.norm.act(eng)
                self.turn.act(eng)
                eng.wait_ge(self.shifted, 1)
                eng.activation(self.router[1], self.router[0], ACT.Exp).then_inc(self.route_exp, 1)
                with eng.Fori(0, E // 2) as it:
                    for count in range(self.PER_PASS):
                        r = min(P, F0 - count % FT * P)
                        eng.wait_ge(self.hidden_ready, it * self.PER_PASS + count + 1)
                        eng.wait_ge(self.gated, it * self.PER_PASS + count + 1)
                        eng.activation(self.acted[count % 2][0:r, :], PS[0:r, 2 * (count % 2), :],
                                       ACT.Silu).then_inc(self.activated, 1)

            def dve(self, eng):
                FT = self.FT
                chained = [0]

                def link(ins):
                    chained[0] += 1
                    ins.then_inc(self.route_chain, 1)
                    eng.wait_ge(self.route_chain, chained[0])

                eng.sem_inc(self.gated, 2)
                eng.sem_inc(self.added, 2)
                self.norm.dve(eng)
                link(eng.tensor_tensor(X[:], X[:], XN[:], ALU.add))
                logits = PS[:, 7, 0:NT * E].rearrange("p (t e) -> p t e", t=NT)
                shifted, powers, probs, rank, kept = self.router
                top, total = self.row

                def rows_of(x):
                    return x.unsqueeze(2).to_broadcast([P, NT, E])

                eng.wait_ge(self.routed, 1)
                link(eng.tensor_reduce(top, logits, AX_X, ALU.max))
                eng.tensor_tensor(shifted, logits, rows_of(top), ALU.subtract).then_inc(self.shifted, 1)
                eng.wait_ge(self.route_exp, 1)
                link(eng.tensor_reduce(total, powers, AX_X, ALU.add))
                link(eng.reciprocal(total, total))
                link(eng.tensor_tensor(probs, powers, rows_of(total), ALU.mult))
                eng.wait_ge(self.earlier_loaded, 16)
                other = probs.unsqueeze(2).to_broadcast([P, NT, E, E])
                this = probs.unsqueeze(3).to_broadcast([P, NT, E, E])
                better, as_good = [x.rearrange("p t (e o) -> p t e o", e=E) for x in self.pairs]
                eng.tensor_tensor(better, other, this, ALU.is_gt)
                link(eng.tensor_tensor(as_good, other, this, ALU.is_equal))
                link(eng.tensor_tensor(self.pairs[1], self.pairs[1],
                                       self.earlier.unsqueeze(1).to_broadcast([P, NT, E * E]), ALU.mult))
                link(eng.tensor_tensor(self.pairs[0], self.pairs[0], self.pairs[1], ALU.add))
                link(eng.tensor_reduce(rank, better, AX_X, ALU.add))
                link(eng.tensor_scalar(kept, rank, 1.5, None, ALU.is_lt))
                link(eng.tensor_tensor(kept, kept, probs, ALU.mult))
                link(eng.tensor_reduce(total, kept, AX_X, ALU.add))
                link(eng.reciprocal(total, total))
                link(eng.tensor_tensor(self.share.rearrange("p e t -> p t e"), kept, rows_of(total), ALU.mult))

                def add(it, x):
                    for half in range(2):
                        eng.wait_ge(self.mixed, it * self.MIXED_PER_PASS + 2 * x + half + 1 + 4)
                        for h in range(2):
                            t = SPB * (x % NB) + 2 * half + h
                            last = eng.scalar_tensor_tensor(out=X[:, t, :], in0=PS[:, 4 + half, h * D:(h + 1) * D],
                                                            scalar=self.shares[x // NB][:, t:t + 1], in1=X[:, t, :],
                                                            op0=ALU.mult, op1=ALU.add)
                        last.then_inc(self.added, 1)

                with eng.Fori(0, E // 2) as it:
                    for x in range(2 * NB):
                        par, b = x // NB, x % NB
                        if b == 0:
                            eng.tensor_copy(self.shares[par].unsqueeze(1), self.share[:, bass.ds(it * 2 + par, 1), :]
                                            ).then_inc(self.share_set, 1)
                            eng.wait_ge(self.share_set, it * 2 + (par + 1))
                        for f in range(FT):
                            r, count = min(P, F0 - f * P), x * FT + f
                            eng.wait_ge(self.activated, it * self.PER_PASS + count + 1)
                            if f == 0:
                                eng.wait_ge(self.mixed, it * self.MIXED_PER_PASS + 2 * x + 2)
                            eng.tensor_tensor(self.hidden[x % 2][0:r, f, :], PS[0:r, 2 * (count % 2) + 1, :],
                                              self.acted[count % 2][0:r, :], ALU.mult).then_inc(self.gated, 1)
                            if x and f == 1:
                                add(it, x - 1)
                    add(it, 2 * NB - 1)

        class FeedForward:

            FT = F1 // P
            PER_PASS = 2 * FT

            def __init__(self):
                take = carver()
                squares = take(NT, D)
                self.turned = take(KH, S)
                self.norm = Normalize("norm", X[:], XN[:], squares)
                self.turn = Turn([(XN[:, t], P) for t in range(NT)], self.turned)
                self.w1, self.w2 = take(KH, F1), take(self.FT, D)
                self.b1 = take(self.FT)
                self.affine = take(2, D)
                self.hidden = [take(self.FT, QB) for _ in range(2)]
                self.y = take(NT, D)
                self.last_norm = Normalize("last", self.y, self.y, squares)
                self.loaded = sem("ffn_loaded")
                self.hidden_ready = sem("ffn_hidden_ready")
                self.activated = sem("ffn_activated")
                self.mixed = sem("ffn_mixed")
                self.added = sem("ffn_added")
                self.chain = sem("ffn_chain")
                self.final = sem("ffn_final")
                self.stored = sem("ffn_stored")

            def sp(self, eng):
                eng.dma_start(self.w1, a["w1"].rearrange("(k p) f -> p k f", p=P)).then_inc(self.loaded, 16)
                eng.dma_start(self.w2, a["w2"].rearrange("(t p) d -> p t d", p=P)).then_inc(self.loaded, 16)
                eng.dma_start(self.b1, a["b1"]).then_inc(self.loaded, 16)
                eng.dma_start(self.affine, a["affine"].rearrange("p (r d) -> p r d", r=2)).then_inc(self.loaded, 16)
                for c in range(4):
                    eng.wait_ge(self.final, c + 1)
                    t = slice(c * NT // 4, (c + 1) * NT // 4)
                    eng.dma_start(out[0].rearrange("(t p) d -> p t d", p=P)[:, t, :], self.y[:, t, :]
                                  ).then_inc(self.stored, 16)
                eng.wait_ge(self.stored, 64)

            def pool(self, eng):
                self.norm.pool(eng)
                self.last_norm.pool(eng)

            def pe(self, eng):
                eng.wait_ge(self.norm.done, 1)
                self.turn.pe(eng)
                eng.wait_ge(self.turn.copied, len(self.turn.jobs))
                eng.wait_ge(self.loaded, 64)
                eng.sem_inc(self.mixed, 4)

                def mix(it, x):
                    eng.wait_ge(self.activated, it * self.PER_PASS + self.FT * (x + 1) + 4)
                    for half in range(2):
                        eng.wait_ge(self.added, it * 4 + 2 * x + half + 1)
                        for h in range(2):
                            s, dst = 2 * half + h, PS[:, 4 + half, h * D:(h + 1) * D]
                            for f in range(self.FT):
                                eng.matmul(dst, self.hidden[x][:, f, s * P:(s + 1) * P], self.w2[:, f, :],
                                           start=(f == 0), stop=False)
                            last = eng.matmul(dst, ones[0:1, :], rows[:, ROW["b2"], :], start=False, stop=True)
                        last.then_inc(self.mixed, 1)

                with eng.Fori(0, NB // 2) as it:
                    for x in range(2):
                        for f in range(self.FT):
                            count = x * self.FT + f
                            eng.wait_ge(self.activated, it * self.PER_PASS + count + 1)
                            for k in range(KH):
                                last = eng.matmul(PS[:, count % 4, :], self.w1[:, k, f * P:(f + 1) * P],
                                                  self.turned[:, k, bass.ds(it * (2 * QB) + x * QB, QB)],
                                                  start=(k == 0), stop=(k == KH - 1))
                            last.then_inc(self.hidden_ready, 1)
                            if x and f == 1:
                                mix(it, 0)
                    mix(it, 1)

            def act(self, eng):
                self.norm.act(eng)
                self.turn.act(eng)
                eng.wait_ge(self.loaded, 64)
                eng.sem_inc(self.activated, 4)
                with eng.Fori(0, NB // 2) as it:
                    for x in range(2):
                        for f in range(self.FT):
                            count = x * self.FT + f
                            eng.wait_ge(self.hidden_ready, it * self.PER_PASS + count + 1)
                            if f == 0:
                                eng.wait_ge(self.mixed, it * 4 + 2 * x + 2)
                            eng.activation(self.hidden[x][:, f, :], PS[:, count % 4, :], ACT.Relu,
                                           bias=self.b1[:, f:f + 1]).then_inc(self.activated, 1)
                self.last_norm.act(eng)

            def dve(self, eng):
                eng.sem_inc(self.added, 2)
                self.norm.dve(eng)
                with eng.Fori(0, NB // 2) as it:
                    for x in range(2):
                        for half in range(2):
                            eng.wait_ge(self.mixed, it * 4 + 2 * x + half + 1 + 4)
                            tiles = bass.ds(it * (2 * SPB) + (x * SPB + 2 * half), 2)
                            eng.tensor_tensor(self.y[:, tiles, :],
                                              PS[:, 4 + half, :].rearrange("p (t d) -> p t d", t=2),
                                              XN[:, tiles, :], ALU.add).then_inc(self.added, 1)
                eng.wait_ge(self.added, 2 + 2 * NB)
                self.last_norm.dve(eng)
                eng.wait_ge(self.last_norm.done, 1)
                chained = 0
                for c in range(4):
                    y = self.y[:, c * NT // 4:(c + 1) * NT // 4, :]
                    shape = [P, NT // 4, D]
                    for op, other in ((ALU.mult, self.affine[:, 0, :].unsqueeze(1).to_broadcast(shape)),
                                      (ALU.add, self.affine[:, 1, :].unsqueeze(1).to_broadcast(shape))):
                        chained += 1
                        eng.tensor_tensor(y, y, other, op).then_inc(self.chain, 1)
                        eng.wait_ge(self.chain, chained)
                    eng.tensor_tensor(y, y, X[:, c * NT // 4:(c + 1) * NT // 4, :], ALU.add).then_inc(self.final, 1)

        stages = [Setup(), Context(),
                  Prepare(0), Attention(0, True, False), None,
                  Prepare(1), Attention(1, False, True), None, Experts(),
                  Prepare(2), Attention(2, True, True), None, FeedForward()]
        stages[4] = Output(0, stages[3].attended, X[:], X[:], weights["o0"], rows[:, ROW["o0"], :])
        stages[7] = Output(1, stages[6].attended, XN[:], XN[:], weights["o1"], None)
        stages[11] = Output(2, stages[10].attended, X[:], X[:], weights["o2"], rows[:, ROW["o2"], :])

        numbers = sorted(x.num for x in roles.values())
        assert numbers == list(range(numbers[0], numbers[-1] + 1))

        stage_semaphores = range(numbers[0], numbers[-1] + 1)

        for stage in stages:
            with nc.Block() as block:
                @block.sync
                def _(eng):
                    stage.sp(eng)

                @block.scalar
                def _(eng):
                    stage.act(eng)

                @block.tensor
                def _(eng):
                    stage.pe(eng)

                @block.vector
                def _(eng):
                    stage.dve(eng)

                @block.gpsimd
                def _(eng):
                    stage.pool(eng)

            nc.all_engine_barrier(sems_to_clear=stage_semaphores)


def kernel(**inputs):
    import numpy as np
    import concourse.bacc as bacc
    from concourse.bass_utils import run_bass_kernel_spmd

    f = {k: np.asarray(v) for k, v in inputs.items()}

    def turned_heads(w):
        return w.reshape(D, H, 2, DK // 2)[:, :, ::-1, :].reshape(D, D)

    def column(v):
        return v.reshape(-1, P).T

    inverse_frequency = 1.0 / 10000.0 ** (np.arange(0, DK, 2, dtype=np.float32) / DK)
    angles = np.einsum("i,j->ij", np.arange(S, dtype=np.float32), inverse_frequency)
    angles = np.concatenate([angles, angles], axis=-1).astype(np.float32)
    sign = np.where(np.arange(DK) < DK // 2, -1.0, 1.0).astype(np.float32)
    rope = np.stack([np.tile(np.cos(angles).T, (P // DK, 1)), np.tile((np.sin(angles) * sign).T, (P // DK, 1))])
    later = np.triu(np.full((P, P), NEG, np.float32), 1)
    earlier = np.tril(np.ones((E, E), np.float32), -1).reshape(1, E * E).repeat(P, 0)

    arrays = {
        "x": f["x"][0], "ctx": f["ctx_1024"][0],
        "identity": np.eye(P, dtype=np.float32), "masks": np.stack([later, later.T]),
        "rope": rope.astype(np.float32), "earlier": earlier,
        "wq0": f["L0_xattn_w_q"].T, "wk0": f["L0_xattn_w_k"].T, "wv0": f["L0_xattn_w_v"].T, "wo0": f["L0_xattn_w_o"].T,
        "wq1": f["L0_ffn_wq"], "wq1t": turned_heads(f["L0_ffn_wq"]), "wk1": f["L0_ffn_wk"],
        "wk1t": turned_heads(f["L0_ffn_wk"]), "wv1": f["L0_ffn_wv"], "wo1": f["L0_ffn_wo"],
        "wq2": f["L1_xattn_Wq"], "wkv2": f["L1_xattn_Wkv"], "wo2": f["L1_xattn_Wout"],
        "wr": f["L0_ffn_w_router"],
        "rows": np.stack([f["L0_xattn_b_v"], f["L0_xattn_b_o"], f["L1_xattn_bout"], f["L1_ffn_b2"][0]]),
        "cols": np.concatenate([column(f[k]) for k in ("L0_xattn_b_q", "L0_xattn_b_k", "L0_ffn_g1", "L0_ffn_g2")], 1),
        "wg": f["L0_ffn_wg"].reshape(E * D, F0), "wu": f["L0_ffn_wu"].reshape(E * D, F0),
        "wd": f["L0_ffn_wd"].reshape(E * F0, D),
        "w1": f["L1_ffn_w1"][0], "w2": f["L1_ffn_w2"][0], "b1": column(f["L1_ffn_b1"][0]),
        "affine": np.stack([f["L1_ffn_gamma"], f["L1_ffn_beta"]]).reshape(1, 2 * D).repeat(P, 0),
    }
    arrays = {f"in_{k}": np.ascontiguousarray(v) for k, v in arrays.items()}
    nc = bacc.Bacc("TRN2", target_bir_lowering=False, num_devices=1)
    args = {k[3:]: nc.dram_tensor(k, v.shape, mybir.dt.from_np(v.dtype), kind="ExternalInput").ap()
            for k, v in arrays.items()}
    out = nc.dram_tensor("out_x", (1, S, D), F32, kind="ExternalOutput").ap()
    build(nc, args, out)
    result = run_bass_kernel_spmd(nc, [arrays], core_ids=[0])
    return result.results[0]["out_x"]
```

```python
from contextlib import ExitStack

import concourse.bass as bass
from concourse import mybir

ALU = mybir.AluOpType
ACT = mybir.ActivationFunctionType
F32 = mybir.dt.float32
BF16 = mybir.dt.bfloat16
AX_X = mybir.AxisListType.X

P = 128
S = 2048
C = 1601
D = 256
H = 16
DK = D // H
KH = D // P
NT = S // P
NC = -(-C // P)
QB = 512
NB = S // QB
SPB = QB // P
G = 4
NG = H // G
VW = 32
E = 8
F0 = 704
F1 = 1024
NEG = -1.0e30
SCALE = DK ** -0.5
LN_EPS = 1e-5
RMS_EPS = 1e-6

Q_PARTS = (0, 0, 0, 1, 1, 2)
K_PARTS = (0, 1, 2, 0, 1, 0)
PEAK_ROW = 6 * DK
SCORE_ROWS = PEAK_ROW + 3


def dims(ap, *shape):
    if len(shape) == 1:
        return ap
    if len(shape) == 2:
        return ap.rearrange("p (a b) -> p a b", a=shape[0])
    return ap.rearrange("p (a b c) -> p a b c", a=shape[0], b=shape[1])


def build(nc, a, out):
    with ExitStack() as ctx:
        roles = {}

        def sem(role):
            if role not in roles:
                roles[role] = ctx.enter_context(nc.semaphore(role))
            return roles[role]

        def sb(name, shape, dt=F32):
            return ctx.enter_context(nc.sbuf_tensor(name, shape, dt))

        def scratch(name, shape, dt):
            return nc.dram_tensor(name, shape, dt, kind="Internal").ap()

        X = sb("X", [P, NT, D])
        XN = sb("XN", [P, NT, D])
        identity = sb("identity", [P, P])
        identity16 = sb("identity16", [P, P], BF16)
        mask_qk = sb("mask_qk", [P, P], BF16)
        mask_kq = sb("mask_kq", [P, P], BF16)
        ones = sb("ones", [1, P])
        minus_half = sb("minus_half", [P, NT])
        stats = sb("stats", [P, 4, NT])
        rows = sb("rows", [1, 4, D])
        ROW = {"v0": 0, "o0": 1, "o2": 2, "b2": 3}
        cols = sb("cols", [P, 4, KH])
        COL = {"q0": 0, "k0": 1, "g1": 2, "g2": 3}
        ARENA = 43000
        arena = sb("arena", [P, ARENA])
        PS = ctx.enter_context(nc.psum_tensor("PS", [P, 8, QB], F32))

        def carver():
            at = [0]

            def take(*shape, dt=F32):
                n = 1
                for x in shape:
                    n *= x
                words = n if dt == F32 else -(-n // 2)
                part = arena[:, at[0]:at[0] + words]
                at[0] += words
                assert at[0] <= ARENA, at[0]
                if dt != F32:
                    part = part.bitcast(dt)[:, 0:n]
                return dims(part, *shape)
            return take

        WEIGHTS = {"q0": D, "k0": D, "v0": D, "o0": D, "q1": D, "q1_turned": D, "k1": D, "k1_turned": D, "v1": D,
                   "o1": D, "q2": D, "kv2": 2 * D, "o2": D, "router": E}

        class Weights:

            def __init__(self, take, *names):
                self.at = {name: take(KH, WEIGHTS[name]) for name in names}
                self.landed = sem("weights_landed")

            def __getitem__(self, name):
                return self.at[name]

            def sp(self, eng):
                for name, dst in self.at.items():
                    eng.dma_start(dst, a[f"w_{name}"].rearrange("(k p) n -> p k n", p=P)).then_inc(self.landed, 16)

            def wait(self, eng):
                eng.wait_ge(self.landed, 16 * len(self.at))

        q_parts = [scratch(f"q_parts{i}", (3, D, S), BF16) for i in range(3)]
        k_parts_ctx = {i: scratch(f"k_parts_ctx{i}", (3, D, C), BF16) for i in (0, 2)}
        k_parts_own = {i: scratch(f"k_parts_own{i}", (3, D, S), BF16) for i in (1, 2)}
        v_ctx = {i: scratch(f"v_ctx{i}", (NC * P, H * VW), F32) for i in (0, 2)}
        rows_sorted = scratch("rows_sorted", ((2 * S // P + E) * P, D), F32)
        results_sorted = scratch("results_sorted", ((2 * S // P + E - 1) * P, D), F32)
        v_own = {i: scratch(f"v_own{i}", (S, H * VW), F32) for i in (1, 2)}


        class Setup:

            def __init__(self):
                self.loaded = sem("setup_loaded")
                take = carver()
                self.masks = take(2, P)

            def sp(self, eng):
                eng.dma_start(identity[:], a["identity"]).then_inc(self.loaded, 16)
                eng.dma_start(self.masks, a["masks"].rearrange("m p c -> p m c")).then_inc(self.loaded, 16)
                eng.dma_start(X[:], a["x"].rearrange("(t p) d -> p t d", p=P)).then_inc(self.loaded, 16)
                eng.dma_start(rows[:], a["rows"].rearrange("(o r) d -> o r d", o=1)).then_inc(self.loaded, 16)
                eng.dma_start(cols[:], a["cols"].rearrange("p (r k) -> p r k", r=4)).then_inc(self.loaded, 16)
                eng.wait_ge(self.loaded, 16 * 5)

            def act(self, eng):
                pass

            def pe(self, eng):
                pass

            def dve(self, eng):
                eng.wait_ge(self.loaded, 16 * 5)
                eng.tensor_copy(identity16[:], identity[:])
                eng.tensor_copy(mask_qk[:], self.masks[:, 0, :])
                eng.tensor_copy(mask_kq[:], self.masks[:, 1, :])

            def pool(self, eng):
                eng.memset(ones[:], 1.0)
                eng.memset(minus_half[:], -0.5)

        class Turn:

            def __init__(self, sources, dst, gain=None):
                self.sources, self.dst, self.gain = sources, dst, gain
                self.turned, self.copied = sem("turn_turned"), sem("turn_copied")
                self.jobs = [(b, half) for b in range(0, len(sources), SPB) for half in range(KH)]

            def pe(self, eng):
                for n, (b, half) in enumerate(self.jobs):
                    if n >= 2:
                        eng.wait_ge(self.copied, n - 1)
                    for i, (src, r) in enumerate(self.sources[b:b + SPB]):
                        last = eng.transpose(PS[:, n % 2, i * P:i * P + r], src[0:r, half * P:(half + 1) * P],
                                             identity[0:r, 0:r])
                    last.then_inc(self.turned, 1)

            def act(self, eng):
                for n, (b, half) in enumerate(self.jobs):
                    w = sum(r for _, r in self.sources[b:b + SPB])
                    eng.wait_ge(self.turned, n + 1)
                    scale = 1.0 if self.gain is None else self.gain[:, half:half + 1]
                    eng.activation(self.dst[:, half, b * P:b * P + w], PS[:, n % 2, 0:w], ACT.Identity,
                                   scale=scale).then_inc(self.copied, 1)

        class Project:

            def __init__(self, take, src, jobs, value_jobs, cos=None, sin=None):
                self.src, self.jobs, self.value_jobs, self.cos, self.sin = src, jobs, value_jobs, cos, sin
                self.full = take(4, QB)
                self.parts = take(4, 3, QB, dt=BF16)
                self.values = take(2 * H, VW).rearrange("p (s h) w -> p s h w", s=2)
                self.values_set = sem("project_values_set")
                self.rope = take(2, QB) if cos is not None else None
                self.projected = sem("project_projected")
                self.full_ready = sem("project_full_ready")
                self.high_ready = sem("project_high_ready")
                self.rest_ready = sem("project_rest_ready")
                self.middle_ready = sem("project_middle_ready")
                self.low_ready = sem("project_low_ready")
                self.rotated = sem("project_rotated")
                self.parts_stored = [sem(f"project_parts_stored{i}") for i in range(4)]
                self.value_projected = sem("project_value_projected")
                self.value_staged = sem("project_value_staged")
                self.value_stored = [sem(f"project_value_stored{i}") for i in range(2)]
                self.steps = max(len(jobs), len(value_jobs))

            def pe(self, eng):
                for n in range(self.steps):
                    if n < len(self.jobs):
                        j = self.jobs[n]
                        if n >= 3:
                            eng.wait_ge(self.full_ready, n - 2)
                        for bank, w in ((n % 3, j["w"]), (3 + n % 3, j.get("turned"))):
                            if w is None:
                                continue
                            for k in range(KH):
                                last = eng.matmul(PS[:, bank, 0:j["n"]], w[:, k, j["half"] * P:(j["half"] + 1) * P],
                                                  self.src[:, k, j["c0"]:j["c0"] + j["n"]],
                                                  start=(k == 0), stop=(k == KH - 1))
                        last.then_inc(self.projected, 1)
                    if n < len(self.value_jobs):
                        v = self.value_jobs[n]
                        if n >= 2:
                            eng.wait_ge(self.value_staged, n - 1)
                        r, dst = v["rows"], PS[0:v["rows"], 6 + n % 2, 0:D]
                        for k in range(KH):
                            last = eng.matmul(dst, self.src[:, k, v["c0"]:v["c0"] + r], v["w"][:, k, :],
                                              start=(k == 0), stop=(k == KH - 1 and v["bias"] is None))
                        if v["bias"] is not None:
                            last = eng.matmul(dst, ones[0:1, 0:r], v["bias"], start=False, stop=True)
                        last.then_inc(self.value_projected, 1)

            def act(self, eng):
                eng.wait_ge(self.values_set, 2)
                for n in range(max(self.steps, len(self.jobs) + 1)):
                    if n < len(self.jobs):
                        j = self.jobs[n]
                        eng.wait_ge(self.full_ready, n + 1)
                        if n >= 4:
                            eng.wait_ge(self.parts_stored[n % 4], 16 * (n // 4))
                        eng.activation(self.parts[:, n % 4, 0, 0:j["n"]], self.full[:, n % 4, 0:j["n"]],
                                       ACT.Copy).then_inc(self.high_ready, 1)
                    if 1 <= n <= len(self.jobs):
                        m = n - 1
                        w = self.jobs[m]["n"]
                        eng.wait_ge(self.rest_ready, m + 1)
                        eng.activation(self.parts[:, m % 4, 1, 0:w], self.full[:, m % 4, 0:w],
                                       ACT.Copy).then_inc(self.middle_ready, 1)
                    if n < len(self.value_jobs):
                        r = self.value_jobs[n]["rows"]
                        eng.wait_ge(self.value_projected, n + 1)
                        if n >= 2:
                            eng.wait_ge(self.value_stored[n % 2], 16 * (n // 2))
                        eng.activation(self.values[0:r, n % 2, :, 0:DK],
                                       PS[0:r, 6 + n % 2, 0:D].rearrange("p (h d) -> p h d", h=H),
                                       ACT.Copy).then_inc(self.value_staged, 1)

            def dve(self, eng):
                turned = 0
                for n in range(len(self.jobs) + 2):
                    if n < len(self.jobs):
                        j = self.jobs[n]
                        w, full = j["n"], self.full[:, n % 4, 0:j["n"]]
                        eng.wait_ge(self.projected, n + 1)
                        if n >= 4:
                            eng.wait_ge(self.low_ready, n - 3)
                        if j.get("turned") is not None:
                            rope = slice(j["c0"], j["c0"] + w)
                            if n:
                                eng.wait_ge(self.full_ready, n)
                            eng.scalar_tensor_tensor(out=self.rope[:, 0, 0:w], in0=PS[:, n % 3, 0:w], scalar=j["scale"],
                                                     in1=self.cos[:, rope], op0=ALU.mult, op1=ALU.mult)
                            eng.scalar_tensor_tensor(out=self.rope[:, 1, 0:w], in0=PS[:, 3 + n % 3, 0:w],
                                                     scalar=j["scale"], in1=self.sin[:, rope], op0=ALU.mult,
                                                     op1=ALU.mult).then_inc(self.rotated, 1)
                            turned += 1
                            eng.wait_ge(self.rotated, turned)
                            eng.tensor_tensor(full, self.rope[:, 0, 0:w], self.rope[:, 1, 0:w],
                                              ALU.add).then_inc(self.full_ready, 1)
                        elif j.get("bias") is not None:
                            eng.tensor_scalar(full, PS[:, n % 3, 0:w], j["bias"], j["scale"], ALU.add,
                                              ALU.mult).then_inc(self.full_ready, 1)
                        else:
                            eng.tensor_scalar(full, PS[:, n % 3, 0:w], j["scale"], None,
                                              ALU.mult).then_inc(self.full_ready, 1)
                    if 1 <= n <= len(self.jobs):
                        m = n - 1
                        w = self.jobs[m]["n"]
                        eng.wait_ge(self.high_ready, m + 1)
                        eng.tensor_tensor(self.full[:, m % 4, 0:w], self.full[:, m % 4, 0:w],
                                          self.parts[:, m % 4, 0, 0:w], ALU.subtract).then_inc(self.rest_ready, 1)
                    if n >= 2:
                        m = n - 2
                        w = self.jobs[m]["n"]
                        eng.wait_ge(self.middle_ready, m + 1)
                        eng.tensor_tensor(self.parts[:, m % 4, 2, 0:w], self.full[:, m % 4, 0:w],
                                          self.parts[:, m % 4, 1, 0:w], ALU.subtract).then_inc(self.low_ready, 1)

            def pool(self, eng):
                eng.memset(self.values, 0.0).then_inc(self.values_set, 1)
                eng.wait_ge(self.values_set, 1)
                eng.memset(self.values[:, :, :, DK:DK + 1], 1.0).then_inc(self.values_set, 1)

            def sp(self, eng):
                for n in range(self.steps):
                    if n < len(self.value_jobs):
                        v = self.value_jobs[n]
                        r = v["rows"]
                        eng.wait_ge(self.value_staged, n + 1)
                        eng.dma_start(v["dst"][v["c0"]:v["c0"] + r, :],
                                      self.values[0:r, n % 2].rearrange("p h d -> p (h d)")
                                      ).then_inc(self.value_stored[n % 2], 16)
                    if n < len(self.jobs):
                        j = self.jobs[n]
                        eng.wait_ge(self.low_ready, n + 1)
                        dst = j["dst"][:, j["half"] * P:(j["half"] + 1) * P, j["c0"]:j["c0"] + j["n"]]
                        eng.dma_start(dst.rearrange("a p c -> p a c"),
                                      self.parts[:, n % 4, :, 0:j["n"]]).then_inc(self.parts_stored[n % 4], 16)
                for i in range(4):
                    eng.wait_ge(self.parts_stored[i], 16 * len(range(i, len(self.jobs), 4)))
                for i in range(2):
                    eng.wait_ge(self.value_stored[i], 16 * len(range(i, len(self.value_jobs), 2)))

        def feature_jobs(w, dst, width, scale=1.0, bias=None, turned=None):
            return [dict(w=w, turned=turned, bias=None if bias is None else bias[:, half:half + 1], scale=scale,
                         dst=dst, half=half, c0=c0, n=min(QB, width - c0))
                    for c0 in range(0, width, QB) for half in range(KH)]

        def value_jobs(w, dst, width, bias=None):
            return [dict(w=w, bias=bias, dst=dst, c0=c0, rows=min(P, width - c0)) for c0 in range(0, width, P)]

        class Context:

            def __init__(self):
                take = carver()
                self.rows = take(NC, D)
                turned = take(KH, NC * P)
                self.loaded = sem("ctx_loaded")
                self.turn = Turn([(self.rows[:, t], min(P, C - t * P)) for t in range(NC)], turned)
                self.weights = weights = Weights(take, "k0", "v0", "kv2")
                kv2 = weights["kv2"]
                self.project = Project(
                    take, turned,
                    feature_jobs(weights["k0"], k_parts_ctx[0], C, bias=cols[:, COL["k0"], :])
                    + feature_jobs(kv2[:, :, 0:D], k_parts_ctx[2], C),
                    value_jobs(weights["v0"], v_ctx[0], C, bias=rows[:, ROW["v0"], :])
                    + value_jobs(kv2[:, :, D:2 * D], v_ctx[2], C))

            def sp(self, eng):
                full = C // P
                eng.dma_start(self.rows[:, 0:full, :], a["ctx"][0:full * P, :].rearrange("(t p) d -> p t d", p=P)
                              ).then_inc(self.loaded, 16)
                eng.dma_start(self.rows[0:C - full * P, full, :], a["ctx"][full * P:C, :]).then_inc(self.loaded, 16)
                self.weights.sp(eng)
                self.project.sp(eng)

            def pe(self, eng):
                eng.wait_ge(self.loaded, 32)
                self.turn.pe(eng)
                eng.wait_ge(self.turn.copied, len(self.turn.jobs))
                self.weights.wait(eng)
                self.project.pe(eng)

            def act(self, eng):
                self.turn.act(eng)
                self.project.act(eng)

            def dve(self, eng):
                self.project.dve(eng)

            def pool(self, eng):
                self.project.pool(eng)

        class Normalize:

            def __init__(self, name, x, xn, squares, layer=True, rms=False):
                self.x, self.xn, self.squares, self.layer, self.rms = x, xn, squares, layer, rms
                self.step = sem(f"{name}_norm_step")
                self.centred = sem(f"{name}_centred")
                self.squared = sem(f"{name}_squared")
                self.spread = sem(f"{name}_spread")
                self.inverse = sem(f"{name}_inverse")
                self.done = sem(f"{name}_normed")
                self.rounds = int(layer) + int(rms)
                self.result = squares if rms else xn

            def over_rows(self, i):
                return stats[:, i, :].unsqueeze(2).to_broadcast([P, NT, D])

            def dve(self, eng):
                steps = 0
                if self.layer:
                    eng.tensor_reduce(stats[:, 0, :], self.x, AX_X, ALU.add).then_inc(self.step, 1)
                    eng.wait_ge(self.step, 1)
                    eng.tensor_scalar(stats[:, 1, :], stats[:, 0, :], 1.0 / D, None, ALU.mult).then_inc(self.step, 1)
                    eng.wait_ge(self.step, 2)
                    eng.tensor_tensor(self.xn, self.x, self.over_rows(1), ALU.subtract).then_inc(self.centred, 1)
                    steps = 2
                for n in range(self.rounds):
                    is_rms = self.rms and n == self.rounds - 1
                    eng.wait_ge(self.squared, n + 1)
                    eng.tensor_reduce(stats[:, 2, :], self.squares, AX_X, ALU.add).then_inc(self.step, 1)
                    steps += 1
                    eng.wait_ge(self.step, steps)
                    eng.tensor_scalar(stats[:, 2, :], stats[:, 2, :], 1.0 / D, RMS_EPS if is_rms else LN_EPS,
                                      ALU.mult, ALU.add).then_inc(self.spread, 1)
                    eng.wait_ge(self.inverse, n + 1)
                    eng.tensor_tensor(self.squares if is_rms else self.xn, self.xn, self.over_rows(3),
                                      ALU.mult).then_inc(self.done, 1)

            def act(self, eng):
                for n in range(self.rounds):
                    if n == 0 and self.layer:
                        eng.wait_ge(self.centred, 1)
                    elif n:
                        eng.wait_ge(self.done, n)
                    eng.activation(self.squares, self.xn, ACT.Square).then_inc(self.squared, 1)

            def pool(self, eng):
                for n in range(self.rounds):
                    eng.wait_ge(self.spread, n + 1)
                    eng.tensor_tensor(stats[:, 3, :], stats[:, 2, :], minus_half[:], ALU.pow).then_inc(self.inverse, 1)

        class Prepare:

            def __init__(self, i):
                self.i = i
                take = carver()
                squares = take(NT, D)
                turned = take(KH, S)
                self.norm = Normalize("norm", X[:], XN[:], squares, rms=(i == 1))
                self.turn = Turn([(self.norm.result[:, t], P) for t in range(NT)], turned,
                                 gain=cols[:, COL["g1"], :] if i == 1 else None)
                self.tables_loaded = None
                self.weights = weights = Weights(take, *(("q0",), ("q1", "q1_turned", "k1", "k1_turned", "v1"),
                                                         ("q2", "kv2"))[i])
                if i == 0:
                    jobs, values_of = feature_jobs(weights["q0"], q_parts[0], S, SCALE, cols[:, COL["q0"], :]), []
                    self.project = Project(take, turned, jobs, values_of)
                elif i == 1:
                    self.tables = take(2, S)
                    self.tables_loaded = sem("prep1_tables_loaded")
                    jobs = (feature_jobs(weights["q1"], q_parts[1], S, SCALE, turned=weights["q1_turned"])
                            + feature_jobs(weights["k1"], k_parts_own[1], S, turned=weights["k1_turned"]))
                    self.project = Project(take, turned, jobs, value_jobs(weights["v1"], v_own[1], S),
                                           cos=self.tables[:, 0], sin=self.tables[:, 1])
                else:
                    jobs = (feature_jobs(weights["q2"], q_parts[2], S, SCALE)
                            + feature_jobs(weights["kv2"][:, :, 0:D], k_parts_own[2], S))
                    self.project = Project(take, turned, jobs,
                                           value_jobs(weights["kv2"][:, :, D:2 * D], v_own[2], S))

            def sp(self, eng):
                self.weights.sp(eng)
                if self.tables_loaded is not None:
                    eng.dma_start(self.tables, a["rope"].rearrange("m p s -> p m s")).then_inc(self.tables_loaded, 16)
                self.project.sp(eng)

            def pe(self, eng):
                eng.wait_ge(self.norm.done, self.norm.rounds)
                self.turn.pe(eng)
                eng.wait_ge(self.turn.copied, len(self.turn.jobs))
                self.weights.wait(eng)
                self.project.pe(eng)

            def act(self, eng):
                self.norm.act(eng)
                self.turn.act(eng)
                self.project.act(eng)

            def dve(self, eng):
                self.norm.dve(eng)
                if self.tables_loaded is not None:
                    eng.wait_ge(self.tables_loaded, 16)
                self.project.dve(eng)

            def pool(self, eng):
                self.project.pool(eng)
                self.norm.pool(eng)

        class Attention:

            BLOCKS = 2 * NB

            def __init__(self, i, has_ctx, has_own):
                self.i, self.has_ctx, self.has_own = i, has_ctx, has_own
                name = "attention"
                self.own0 = C + C % 2 if has_ctx else 0
                self.keys = self.own0 + (S if has_own else 0)
                self.nctx = NC if has_ctx else 0
                self.nv = self.nctx + (NT if has_own else 0)
                take = carver()
                self.k = [take(G, self.keys, dt=BF16) for _ in range(2)]
                self.v = [take(self.nv, G, VW) for _ in range(2)]
                self.q = [take(G, QB, dt=BF16) for _ in range(NB)]
                self.probs = [[take(2, QB) for _ in range(2)] for _ in range(2)]
                self.sums = [take(QB) for _ in range(2)]
                self.attended = XN[:] if i != 1 else take(NT, D)
                self.peaks = take(SPB * G, 8)
                self.peak = take(3, SPB * G)
                self.peak_parts = take(P // (SPB * G), SPB * G, dt=BF16)
                self.peak_rows = take(P, dt=BF16)
                self.inverse = take(SPB, G)
                self.kv_landed = [sem(f"{name}_kv_landed{i}") for i in range(2)]
                self.q_landed = [sem(f"{name}_q_landed{i}") for i in range(NB)]
                self.ones_set = sem(f"{name}_ones_set")
                self.ring_ready = sem(f"{name}_ring_ready")
                self.ring_read = sem(f"{name}_ring_read")
                self.peaks_split = sem(f"{name}_peaks_split")
                self.peaks_copied = sem(f"{name}_peaks_copied")
                self.peaks_landed = sem(f"{name}_peaks_landed")
                self.scores_ready = sem(f"{name}_scores_ready")
                self.probs_ready = sem(f"{name}_probs_ready")
                self.probs_used = sem(f"{name}_probs_used")
                self.sums_copied = sem(f"{name}_sums_copied")
                self.chain = sem(f"{name}_chain")
                self.plan()


            RING = (4, 5, 7)

            LOOK = 3

            def plan(self):
                self.pieces = [self.pieces_of(b) for b in range(NB)]
                self.units = [self.units_of(b) for b in range(NB)]
                while (2 * sum(map(len, self.pieces)) + 2 * self.BLOCKS) % len(self.RING):
                    self.pieces[0].append(min(self.pieces[0], key=self.width))
                self.units_loop = 2 * sum(map(len, self.units))
                assert self.units_loop % 2 == 0
                jobs = [(what, n, k) for n in range(2 * self.BLOCKS)
                        for what, k in [("piece", k) for k in range(len(self.pieces[n % NB]))] + [("peaks", 0)]]
                a_pass = sum(n < self.BLOCKS for _, n, _ in jobs)
                least = len(self.pieces[0]) + 1
                most = sum(len(self.pieces[n]) + 1 for n in range(self.LOOK))
                tries = [(lead, slack) for lead in range(least, most, 2) for slack in (0.01, 0.03, 0.06, 0.1, 0.2, 1.0)]
                _, best = min((self.lay_out(jobs, a_pass, *x)[0], x) for x in tries)
                self.modelled, self.first, self.steps = self.lay_out(jobs, a_pass, *best)
                in_ring = ("piece", "peaks", "sums")
                self.ring_first = len(self.first)
                self.ring_loop = sum(x[0] in in_ring for x in self.steps)
                assert self.ring_loop % len(self.RING) == 0

            def lay_out(self, jobs, a_pass, lead, slack):
                column, fixed, word, signal = 1 / 2.4, 66, 1.04, 150
                tensor = vector = scalar = 0.0
                read = [0.0] * len(self.RING)
                probs, ready = [0.0] * 2, [0.0] * 2
                all_words = 2 * sum(self.width(x) for b in range(NB) for x in self.pieces[b])
                all_keys = 2 * sum(QB - q0 for b in range(NB) for _, _, _, q0, _ in self.units[b])
                steps, at, words, keys, split = [], 0, 0, 0, 0.0

                def job(what, n, k):
                    nonlocal tensor, vector, words, split
                    steps.append((what, n, k))
                    tensor = max(tensor, read[-len(self.RING)])
                    if what == "piece":
                        width = self.width(self.pieces[n % NB][k])
                        words += width
                        tensor += column * width
                        vector = max(vector, tensor + signal) + fixed + word * width
                        if k == len(self.pieces[n % NB]) - 1:
                            split = vector = vector + 1300
                    elif what == "peaks":
                        tensor = max(tensor, split + signal) + 60
                        vector = max(vector, tensor + signal) + 300
                    else:
                        tensor += 900
                        vector = max(vector, tensor + signal) + 400
                    read.append(vector + signal)

                def next_jobs(block, forced):
                    nonlocal at
                    while at < lead + a_pass:
                        what, n, k = jobs[at]
                        if not (forced and n <= block):
                            if n > block + self.LOOK - 1 or read[-len(self.RING)] > tensor:
                                return
                            if what == "peaks" and split + signal > tensor:
                                return
                            if words / all_words - keys / all_keys > before + slack:
                                return
                        job(what, n, k)
                        at += 1

                while at < lead:
                    job(*jobs[at])
                    at += 1
                before = words / all_words
                first, last = len(steps), None
                start = tensor
                for n in range(self.BLOCKS):
                    nu = len(self.units[n % NB])
                    for u in range(nu):
                        q0 = self.units[n % NB][u][3]
                        if u == 0:
                            next_jobs(n, True)
                        for pair in range(2):
                            steps.append(("scores", n, (u, pair)))
                            tensor = max(tensor, probs[pair]) + 2 * column * (QB - q0)
                            scalar = max(scalar, tensor + signal) + 1.67 * (QB - q0) + 50
                            probs[pair] = scalar + signal
                            next_jobs(n, False)
                        if last is not None:
                            steps.append(("attend", *last))
                            tensor = max(tensor, *ready) + 4 * column * (QB - q0) + 60
                            if u == 0:
                                scalar = max(scalar, tensor + signal) + 480
                        if u == 1 and n:
                            job("sums", n - 1, 0)
                        keys += QB - q0
                        next_jobs(n + 1 if u >= nu - 2 else n, u >= nu - 2)
                        ready = list(probs)
                        last = (n, u)
                steps += [("attend", *last), ("sums", self.BLOCKS - 1, 0)]
                while at < lead + a_pass:
                    job(*jobs[at])
                    at += 1
                time = start + (NG // 2) * (max(tensor, vector) - start)
                return time, steps[:first], steps[first:]

            @staticmethod
            def width(piece):
                return sum(w for _, _, _, w, _ in piece[4])

            def walk(self, steps, start):
                for what, n, x in steps:
                    if what in ("piece", "peaks", "sums"):
                        yield what, n, x, start
                        start += 1
                    else:
                        yield what, n, x, None

            def ring_bank(self, r):
                return self.RING[r % len(self.RING)]

            def pieces_of(self, b):
                found = []
                for s in range(SPB):
                    runs = [(0, C, None)] if self.has_ctx else []
                    if self.has_own:
                        own = (SPB * b + s) * P
                        if own:
                            runs.append((self.own0, own, None))
                        runs.append((self.own0 + own, P, 0))
                    banks, at = [[]], 0
                    for k0, n, m in runs:
                        while n:
                            if at == QB:
                                banks.append([])
                                at = 0
                            w = min(n, QB - at)
                            banks[-1].append((at, k0, w, m))
                            at, k0, n = at + w, k0 + w, n - w
                            m = None if m is None else m + w
                    for c, parts in enumerate(banks):
                        heads = min(QB // at, G) if c == len(banks) - 1 else 1
                        for j in range(0, G, heads):
                            heads = min(heads, G - j)
                            found.append((j, heads, s, c, [(j + h, h * at + x, k0, w, m)
                                                           for h in range(heads) for x, k0, w, m in parts]))
                return found

            def banks(self, b, s):
                return 1 + max(c for _, _, t, c, _ in self.pieces[b] if t == s)

            def units_of(self, b):
                units = [(t * P, min(P, C - t * P), t, 0, False) for t in range(self.nctx)]
                if self.has_own:
                    for t in range(SPB * (b + 1)):
                        units.append((self.own0 + t * P, P, self.nctx + t, max(0, t - SPB * b) * P, t >= SPB * b))
                return units

            def before(self, n, of):
                return sum(len(of[m % NB]) for m in range(n))

            def attended_count(self, it, n):
                return it * self.units_loop + self.before(n + 1, self.units) + 2


            def pe(self, eng):
                def piece(it, n, k, r):
                    b, par = n % NB, n // NB % 2
                    _, _, s, _, parts = self.pieces[b][k]
                    if k == 0:
                        eng.wait_ge(self.q_landed[b], it * (2 * 96) + 96 * (n // NB + 1))
                        if b == 0:
                            kv = 16 * self.kv_loads
                            eng.wait_ge(self.kv_landed[par], it * kv + kv * (1 + n // self.BLOCKS))
                    eng.wait_ge(self.ring_read, it * self.ring_loop + r + 1)
                    todo = [(at, w, self.q[b][0:PEAK_ROW, j, s * P:(s + 1) * P],
                             self.k[par][0:PEAK_ROW, j, k0:k0 + w]) for j, at, k0, w, _ in parts]
                    todo += [(at, w, identity16[:], mask_qk[:, m:m + w]) for _, at, _, w, m in parts if m is not None]
                    for x, (at, w, lhs, rhs) in enumerate(todo):
                        last = eng.matmul(PS[:, self.ring_bank(r), at:at + w], lhs, rhs, start=(x == 0),
                                          stop=(x == len(todo) - 1))
                    last.then_inc(self.ring_ready, 1)

                def turn_peaks(it, n, r):
                    eng.wait_ge(self.peaks_split, it * self.BLOCKS + n + 1)
                    eng.wait_ge(self.ring_read, it * self.ring_loop + r + 1)
                    eng.transpose(PS[:, self.ring_bank(r), :].bitcast(BF16)[:, 0:P],
                                  self.peak_parts[:, :, :].rearrange("p a b -> p (a b)"),
                                  identity16[:]).then_inc(self.ring_ready, 1)

                def scores(it, n, u, pair):
                    b, par = n % NB, n // NB
                    count = self.before(n, self.units) + u
                    k0, r, _, q0, masked = self.units[b][u]
                    if u == 0 and pair == 0:
                        eng.wait_ge(self.peaks_landed, it * (16 * self.BLOCKS) + 16 * (n + 1))
                    eng.wait_ge(self.probs_ready, it * (2 * self.units_loop) + 2 * count + pair + 1)
                    for h in range(2):
                        j = 2 * pair + h
                        last = eng.matmul(PS[0:r, j, q0:QB], self.k[par][0:SCORE_ROWS, j, k0:k0 + r],
                                          self.q[b][0:SCORE_ROWS, j, q0:QB], start=True, stop=not masked)
                        if masked:
                            last = eng.matmul(PS[:, j, q0:q0 + P], identity16[:], mask_kq[:], start=False, stop=True)
                    last.then_inc(self.scores_ready, 1)

                def attend(it, n, u):
                    b, par = n % NB, n // NB
                    count = self.before(n, self.units) + u
                    _, r, t, q0, _ = self.units[b][u]
                    eng.wait_ge(self.probs_ready, it * (2 * self.units_loop) + 2 * count + 4)
                    if u == 0:
                        eng.wait_ge(self.sums_copied, it * self.BLOCKS + n + 1)
                    for j in range(G):
                        last = eng.matmul(PS[VW * j:VW * (j + 1), 6, q0:QB], self.v[par][0:r, t, j, :],
                                          self.probs[count % 2][j // 2][0:r, j % 2, q0:QB],
                                          start=(u == 0), stop=(u == len(self.units[b]) - 1))
                    last.then_inc(self.probs_used, 1)

                def turn_sums(it, n, r):
                    eng.wait_ge(self.sums_copied, it * self.BLOCKS + n + 2)
                    eng.wait_ge(self.ring_read, it * self.ring_loop + r + 1)
                    for s in range(SPB):
                        last = eng.transpose(PS[:, self.ring_bank(r), s * P:(s + 1) * P],
                                             self.sums[n % 2][:, s * P:(s + 1) * P], identity[:])
                    last.then_inc(self.ring_ready, 1)

                def do(it, steps, start):
                    for what, n, x, r in self.walk(steps, start):
                        if what == "piece":
                            piece(it, n, x, r)
                        elif what == "peaks":
                            turn_peaks(it, n, r)
                        elif what == "sums":
                            turn_sums(it, n, r)
                        elif what == "scores":
                            scores(it, n, *x)
                        else:
                            attend(it, n, x)

                eng.sem_inc(self.probs_used, 2)
                eng.wait_ge(self.ones_set, 2)
                do(0, self.first, 0)
                with eng.Fori(0, NG // 2) as it:
                    do(it, self.steps, self.ring_first)


            def act(self, eng):
                def exponentials(it, n, u, pair):
                    count = self.before(n, self.units) + u
                    _, r, _, q0, _ = self.units[n % NB][u]
                    if pair == 0:
                        eng.wait_ge(self.probs_used, it * self.units_loop + count + 1)
                    eng.wait_ge(self.scores_ready, it * (2 * self.units_loop) + 2 * count + pair + 1)
                    eng.activation(self.probs[count % 2][pair][0:r, :, q0:QB], PS[0:r, 2 * pair:2 * pair + 2, q0:QB],
                                   ACT.Exp).then_inc(self.probs_ready, 1)

                def copy_sums(it, n):
                    eng.wait_ge(self.probs_used, self.attended_count(it, n))
                    eng.activation(self.sums[n % 2], PS[:, 6, :], ACT.Copy).then_inc(self.sums_copied, 1)

                eng.sem_inc(self.probs_ready, 2)
                with eng.Fori(0, NG // 2) as it:
                    for what, n, x in self.steps:
                        if what == "scores":
                            exponentials(it, n, *x)
                        elif what == "attend" and x == len(self.units[n % NB]) - 1:
                            copy_sums(it, n)


            def dve(self, eng):
                LINKS = 5 * self.BLOCKS
                links = [0]

                def link(it, ins):
                    links[0] += 1
                    ins.then_inc(self.chain, 1)
                    eng.wait_ge(self.chain, it * LINKS + links[0])

                def piece(it, n, k, r):
                    j, heads, s, c, parts = self.pieces[n % NB][k]
                    width = self.width(self.pieces[n % NB][k])
                    eng.wait_ge(self.ring_ready, it * self.ring_loop + r + 1)
                    if self.pieces[n % NB].index(self.pieces[n % NB][k]) < k:
                        eng.wait_ge(self.ring_read, it * self.ring_loop + r + 3)
                    eng.tensor_reduce(self.peaks[:, G * s + j:G * s + j + heads, c],
                                      PS[:, self.ring_bank(r), 0:width].rearrange("p (j k) -> p j k", j=heads), AX_X,
                                      ALU.max).then_inc(self.ring_read, 1)

                def split_peaks(it, n, r):
                    eng.wait_ge(self.ring_read, it * self.ring_loop + r + 4)
                    for s in range(SPB):
                        last = eng.tensor_reduce(self.peak[:, 0, :].rearrange("p (j s) -> p j s", j=G)[:, :, s],
                                                 self.peaks[:, G * s:G * (s + 1), 0:self.banks(n % NB, s)], AX_X,
                                                 ALU.max, negate=True)
                    link(it, last)
                    link(it, eng.tensor_copy(self.peak_parts[:, 0, :], self.peak[:, 0, :]))
                    link(it, eng.tensor_tensor(self.peak[:, 1, :], self.peak[:, 0, :], self.peak_parts[:, 0, :],
                                               ALU.subtract))
                    link(it, eng.tensor_copy(self.peak_parts[:, 1, :], self.peak[:, 1, :]))
                    eng.tensor_tensor(self.peak_parts[:, 2, :], self.peak[:, 1, :], self.peak_parts[:, 1, :],
                                      ALU.subtract).then_inc(self.peaks_split, 1)

                def copy_peaks(it, n, r):
                    eng.wait_ge(self.ring_ready, it * self.ring_loop + r + 1)
                    if n:
                        eng.wait_ge(self.peaks_landed, it * (16 * self.BLOCKS) + 16 * n)
                    rows48 = 3 * SPB * G
                    eng.tensor_copy(self.peak_rows[0:rows48, :],
                                    PS[0:rows48, self.ring_bank(r), :].bitcast(BF16)[:, 0:P]
                                    ).then_inc(self.peaks_copied, 1)
                    eng.wait_ge(self.peaks_copied, it * self.BLOCKS + n + 1)
                    eng.sem_inc(self.ring_read, 1)

                def divide(it, n, r):
                    b, group = n % NB, n // NB
                    eng.wait_ge(self.ring_ready, it * self.ring_loop + r + 1)
                    turned = PS[:, self.ring_bank(r), :].rearrange("p (s j d) -> p s j d", s=SPB, j=G)
                    link(it, eng.reciprocal(self.inverse, turned[:, :, :, DK]))
                    dst = self.attended[:, SPB * b:SPB * (b + 1), bass.ds(it * (2 * G * DK) + group * (G * DK), G * DK)]
                    eng.tensor_tensor(dst.rearrange("p s (j d) -> p s j d", j=G), turned[:, :, :, 0:DK],
                                      self.inverse.unsqueeze(3).to_broadcast([P, SPB, G, DK]),
                                      ALU.mult).then_inc(self.ring_read, 1)

                def do(it, steps, start):
                    for what, n, x, r in self.walk(steps, start):
                        if what == "piece":
                            piece(it, n, x, r)
                            if x == len(self.pieces[n % NB]) - 1:
                                split_peaks(it, n, r)
                        elif what == "peaks":
                            copy_peaks(it, n, r)
                        elif what == "sums":
                            divide(it, n, r)

                eng.sem_inc(self.ring_read, 3)
                eng.sem_inc(self.sums_copied, 1)
                link(0, eng.memset(self.peak_parts, 0.0))
                for par in range(2):
                    eng.memset(self.k[par][PEAK_ROW:SCORE_ROWS, :, :], 1.0).then_inc(self.ones_set, 1)
                do(0, self.first, 0)
                before = links[0]
                with eng.Fori(0, NG // 2) as it:
                    do(it, self.steps, self.ring_first)
                assert links[0] - before == LINKS, links[0]

            def pool(self, eng):
                pass


            @property
            def kv_loads(self):
                return (6 + 2) * self.has_ctx + (6 + 1) * self.has_own

            def sp(self, eng):
                i, GD = self.i, G * DK

                def load_group(par, group):
                    done, n = self.kv_landed[par], 0
                    for own, src, c0, w in ((False, k_parts_ctx.get(i), 0, C), (True, k_parts_own.get(i), self.own0, S)):
                        if not (self.has_own if own else self.has_ctx):
                            continue
                        for slot, part in enumerate(K_PARTS):
                            eng.dma_start(self.k[par][slot * DK:(slot + 1) * DK, :, c0:c0 + w],
                                          src[part, bass.ds(group * GD, GD), :].rearrange("(j d) c -> d j c", d=DK)
                                          ).then_inc(done, 16)
                            n += 1
                    cols_of = bass.ds(group * (G * VW), G * VW)
                    if self.has_ctx:
                        full = C // P
                        eng.dma_start(self.v[par][:, 0:full].rearrange("p t j w -> p t (j w)"),
                                      v_ctx[i][0:full * P, cols_of].rearrange("(t p) w -> p t w", p=P)).then_inc(done, 16)
                        eng.dma_start(self.v[par][0:C - full * P, full].rearrange("p j w -> p (j w)"),
                                      v_ctx[i][full * P:C, cols_of]).then_inc(done, 16)
                        n += 2
                    if self.has_own:
                        eng.dma_start(self.v[par][:, self.nctx:self.nv].rearrange("p t j w -> p t (j w)"),
                                      v_own[i][:, cols_of].rearrange("(t p) w -> p t w", p=P)).then_inc(done, 16)
                        n += 1
                    assert n == self.kv_loads, (n, self.kv_loads)

                def load_queries(b, group):
                    for slot, part in enumerate(Q_PARTS):
                        eng.dma_start(self.q[b][slot * DK:(slot + 1) * DK, :, :],
                                      q_parts[i][part, bass.ds(group * GD, GD), b * QB:(b + 1) * QB]
                                      .rearrange("(j d) c -> d j c", d=DK)).then_inc(self.q_landed[b], 16)

                def store_peaks(it, n):
                    eng.wait_ge(self.peaks_copied, it * self.BLOCKS + n + 1)
                    b = n % NB
                    eng.dma_start(self.q[b][PEAK_ROW:SCORE_ROWS].rearrange("p j (s c) -> p (j s) c", s=SPB),
                                  self.peak_rows[0:3 * SPB * G, :]).then_inc(self.peaks_landed, 16)

                load_queries(0, 0)
                load_group(0, 0)
                for b in range(1, NB):
                    load_queries(b, 0)
                for what, n, _ in self.first:
                    if what == "peaks":
                        store_peaks(0, n)
                with eng.Fori(0, NG // 2) as it:
                    eng.wait_ge(self.probs_used, it * self.units_loop + 2)
                    load_group(1, it * 2 + 1)
                    for what, n, x in self.steps:
                        if what == "peaks":
                            store_peaks(it, n)
                        elif what == "attend" and x == len(self.units[n % NB]) - 1:
                            b, second = n % NB, n // NB
                            eng.wait_ge(self.probs_used, self.attended_count(it, n))
                            load_queries(b, it * 2 + 1 if not second else it * (-2) + 2)
                            if b == NB - 1 and not second:
                                load_group(0, it * (-2) + 2)
                loops = NG // 2
                for b in range(NB):
                    eng.wait_ge(self.q_landed[b], 96 * (1 + 2 * loops))
                for par in range(2):
                    eng.wait_ge(self.kv_landed[par], 16 * self.kv_loads * (1 - par + loops))
                early = sum(what == "peaks" for what, _, _ in self.first)
                eng.wait_ge(self.peaks_landed, 16 * (early + loops * self.BLOCKS))

        class Output:

            def __init__(self, i, attended, residual, dst, bias):
                self.bias, self.residual, self.dst = bias, residual, dst
                take = carver()
                if i == 1:
                    take(ARENA - KH * S - KH * D)
                self.turned = take(KH, S)
                self.weights = Weights(take, f"o{i}")
                self.w = self.weights[f"o{i}"]
                self.turn = Turn([(attended[:, t], P) for t in range(NT)], self.turned)
                self.projected, self.added = sem("out_projected"), sem("out_added")

            def pe(self, eng):
                self.turn.pe(eng)
                eng.wait_ge(self.turn.copied, len(self.turn.jobs))
                self.weights.wait(eng)
                for n in range(NT // 2):
                    if n >= 4:
                        eng.wait_ge(self.added, n - 3)
                    for h in range(2):
                        t, dst = 2 * n + h, PS[:, 2 + n % 4, h * D:(h + 1) * D]
                        for k in range(KH):
                            last = eng.matmul(dst, self.turned[:, k, t * P:(t + 1) * P], self.w[:, k, :],
                                              start=(k == 0), stop=(k == KH - 1 and self.bias is None))
                        if self.bias is not None:
                            last = eng.matmul(dst, ones[0:1, :], self.bias, start=False, stop=True)
                    last.then_inc(self.projected, 1)

            def act(self, eng):
                self.turn.act(eng)

            def dve(self, eng):
                for n in range(NT // 2):
                    eng.wait_ge(self.projected, n + 1)
                    eng.tensor_tensor(self.dst[:, 2 * n:2 * n + 2, :],
                                      PS[:, 2 + n % 4, :].rearrange("p (t d) -> p t d", t=2),
                                      self.residual[:, 2 * n:2 * n + 2, :], ALU.add).then_inc(self.added, 1)

            def sp(self, eng):
                self.weights.sp(eng)

            def pool(self, eng):
                pass

        class Experts:

            FT = -(-F0 // P)
            FC = F0 // 2
            BLOCKS = 2 * S // P + E - 1
            K = BLOCKS + 1

            def __init__(self):
                take = carver()
                self.gate_up = take(E * 2 * KH, F0)
                self.down = take(E * self.FT, D)
                self.normed = take(NT, D)
                normed, used = self.normed.rearrange("p t d -> p (t d)"), [0]

                def reuse(n):
                    used[0] += n
                    assert used[0] <= NT * D
                    return normed[:, used[0] - n:used[0]]

                self.x_in = [reuse(D) for _ in range(2)]
                self.x_turned = [dims(reuse(KH * P), KH, P) for _ in range(2)]
                self.silu = [reuse(self.FC) for _ in range(2)]
                self.hidden = [reuse(F0) for _ in range(2)]
                self.hidden_turned = [take(self.FT, P) for _ in range(2)]
                self.y = [take(D) for _ in range(2)]
                self.weights = Weights(take, "router")
                self.share = [take(NT) for _ in range(2)]
                self.place = take(2 * NT).bitcast(mybir.dt.int32).rearrange("p (c t) -> p c t", c=2)
                self.expert = take(self.K).bitcast(mybir.dt.int32)
                self.norm = Normalize("norm", None, XN[:], self.normed, layer=False, rms=True)
                words = XN[:].rearrange("p t d -> p (t d)")
                self.turned = words.rearrange("p (k s) -> p k s", k=KH)
                self.turn = Turn([(self.normed[:, t], P) for t in range(NT)], self.turned, gain=cols[:, COL["g2"], :])
                at = [0]

                def part(n):
                    at[0] += n
                    assert at[0] <= NT * D
                    return words[:, at[0] - n:at[0]]

                self.grid = [part(E * NT * NT) for _ in range(1)][0]
                self.by_expert = [part(NT * E) for _ in range(9)]
                self.few = [part(E) for _ in range(5)]
                self.row = [part(NT) for _ in range(2)]
                self.constants = part(E * E + NT * NT + NT + self.K)
                self.gathered = [self.gate_up[:, 2 * i:2 * i + 1, 0:2 * D].rearrange("p a (c d) -> p (a c) d", c=2)
                                 for i in range(4)]
                self.counting = self.hidden_turned[0][:, 0:2, :]
                self.constants_landed = sem("moe_constants_landed")
                self.counting_landed = sem("moe_counting_landed")
                self.zeroed = sem("moe_zeroed")
                self.zeros_stored = sem("moe_zeros_stored")
                self.w_landed = sem("moe_w_landed")
                self.routed = sem("moe_routed")
                self.chain = sem("moe_chain")
                self.shifted = sem("moe_shifted")
                self.route_exp = sem("moe_route_exp")
                self.chosen = sem("moe_chosen")
                self.counted = sem("moe_counted")
                self.placed = sem("moe_placed")
                self.scattered = sem("moe_scattered")
                self.x_landed = [sem(f"moe_x_landed{i}") for i in range(2)]
                self.x_read = sem("moe_x_read")
                self.x_copied = sem("moe_x_copied")
                self.multiplied = sem("moe_multiplied")
                self.activated = sem("moe_activated")
                self.gated = sem("moe_gated")
                self.hidden_read = sem("moe_hidden_read")
                self.hidden_copied = sem("moe_hidden_copied")
                self.mixed = sem("moe_mixed")
                self.y_copied = sem("moe_y_copied")
                self.y_stored = [sem(f"moe_y_stored{i}") for i in range(2)]
                self.gathered_row = [sem(f"moe_gathered{i}") for i in range(4)]
                self.added = sem("moe_added")

            def sp(self, eng):
                eng.wait_ge(self.zeroed, 1)
                eng.dma_start(rows_sorted.rearrange("(k p) d -> p k d", p=P),
                              self.y[0].unsqueeze(1).to_broadcast([P, self.K, D])).then_inc(self.zeros_stored, 16)
                self.weights.sp(eng)
                eng.dma_start(self.counting, a["counting"].rearrange("p (r c) -> p r c", r=2)
                              ).then_inc(self.counting_landed, 16)
                full, n = F0 // P, 0
                for e in range(E):
                    for g, src in enumerate((a["wg"], a["wu"])):
                        at = (e * 2 + g) * KH
                        eng.dma_start(self.gate_up[:, at:at + KH, :],
                                      src[e * D:(e + 1) * D, :].rearrange("(k p) f -> p k f", p=P)
                                      ).then_inc(self.w_landed, 16)
                    eng.dma_start(self.down[:, e * self.FT:e * self.FT + full, :],
                                  a["wd"][e * F0:e * F0 + full * P, :].rearrange("(t p) d -> p t d", p=P)
                                  ).then_inc(self.w_landed, 16)
                    eng.dma_start(self.down[0:F0 - full * P, e * self.FT + full, :],
                                  a["wd"][e * F0 + full * P:(e + 1) * F0, :]).then_inc(self.w_landed, 16)
                    if e == 0:
                        eng.wait_ge(self.routed, 1)
                        eng.dma_start(self.constants, a["routing"]).then_inc(self.constants_landed, 16)
                eng.wait_ge(self.scattered, 16 * 2 * NT)

                def load(k, par):
                    eng.dma_start(self.x_in[par], rows_sorted[bass.ds(k * P, P), :]).then_inc(self.x_landed[par], 16)

                def store(k, par):
                    eng.wait_ge(self.y_copied, k + 2)
                    eng.dma_start(results_sorted[bass.ds(k * P, P), :], self.y[par]).then_inc(self.y_stored[par], 16)

                load(0, 0)
                load(1, 1)
                with eng.Fori(0, (self.BLOCKS - 1) // 2) as it:
                    for j in range(2):
                        k = it * 2 + (1 + j)
                        eng.wait_ge(self.x_read, k)
                        load(k + 1, j)
                        store(k - 1, j)
                store(self.BLOCKS - 1, (self.BLOCKS - 1) % 2)

            def pool(self, eng):
                eng.memset(self.y[0], 0.0).then_inc(self.zeroed, 1)
                self.norm.pool(eng)
                eng.wait_ge(self.zeros_stored, 16)
                eng.wait_ge(self.placed, 1)
                for t in range(NT):
                    for c in range(2):
                        eng.indirect_dma_start(rows_sorted, bass.IndirectOffsetOnAxis(self.place[:, c, t:t + 1], 0),
                                               self.normed[:, t, :], None).then_inc(self.scattered, 16)
                for par in range(2):
                    eng.wait_ge(self.y_stored[par], 16 * (1 + len(range(par, self.BLOCKS, 2))))
                for t in range(NT):
                    if t >= 4:
                        eng.wait_ge(self.added, t - 3)
                    for c in range(2):
                        eng.indirect_dma_start(self.gathered[t % 4][:, c, :], None, results_sorted,
                                               bass.IndirectOffsetOnAxis(self.place[:, c, t:t + 1], 0)
                                               ).then_inc(self.gathered_row[t % 4], 16)

            def pe(self, eng):
                FT, FC = self.FT, self.FC
                eng.wait_ge(self.norm.done, 1)
                self.turn.pe(eng)
                eng.wait_ge(self.turn.copied, len(self.turn.jobs))
                self.weights.wait(eng)
                for t in range(NT):
                    for k in range(KH):
                        last = eng.matmul(PS[:, 7, t * E:(t + 1) * E], self.turned[:, k, t * P:(t + 1) * P],
                                          self.weights["router"][:, k, :], start=(k == 0), stop=(k == KH - 1))
                last.then_inc(self.routed, 1)
                eng.wait_ge(self.chosen, 1)
                eng.wait_ge(self.counting_landed, 16)
                for i in range(2):
                    last = eng.matmul(PS[:, 6, i * P:(i + 1) * P], self.counting[:, i, :], self.by_expert[4],
                                      start=True, stop=True)
                last.then_inc(self.counted, 1)
                eng.sem_inc(self.mixed, 2)
                eng.sem_inc(self.hidden_read, 4)
                eng.wait_ge(self.placed, 1)
                eng.wait_ge(self.w_landed, 16 * 4 * E)

                def turn_x(k, par, first=0):
                    eng.wait_ge(self.x_landed[par], first)
                    eng.wait_ge(self.x_copied, k + 1)
                    for h in range(KH):
                        last = eng.transpose(PS[:, 7, h * P:(h + 1) * P], self.x_in[par][:, h * P:(h + 1) * P],
                                             identity[:])
                    last.then_inc(self.x_read, 1)

                def multiply(k, par, c, e):
                    if c == 0:
                        eng.wait_ge(self.x_copied, k + 2)
                    eng.wait_ge(self.gated, k * 2 + (c + 1))
                    for g in range(2):
                        for h in range(KH):
                            w = self.gate_up[:, bass.ds(e * (2 * KH) + (g * KH + h), 1), c * FC:(c + 1) * FC]
                            last = eng.matmul(PS[:, 2 * c + g, 0:FC], self.x_turned[par][:, h, :],
                                              w.rearrange("p a f -> p (a f)"), start=(h == 0), stop=(h == KH - 1))
                    last.then_inc(self.multiplied, 1)

                def turn_hidden(k, par):
                    eng.wait_ge(self.gated, k * 2 + 4)
                    for h in range(2):
                        eng.wait_ge(self.hidden_copied, k * 2 + (h + 1))
                        for f in range(3 * h, 3 * h + 3):
                            r = min(P, F0 - f * P)
                            last = eng.transpose(PS[0:r, 4 + h, (f - 3 * h) * P:(f - 3 * h + 1) * P],
                                                 self.hidden[par][:, f * P:f * P + r], identity[:])
                        last.then_inc(self.hidden_read, 1)

                def mix(k, par, e):
                    eng.wait_ge(self.hidden_copied, k * 2 + 4)
                    eng.wait_ge(self.y_copied, k + 1)
                    for f in range(FT):
                        r = min(P, F0 - f * P)
                        w = self.down[0:r, bass.ds(e * FT + f, 1), :].rearrange("p a d -> p (a d)")
                        last = eng.matmul(PS[:, 6, 0:D], self.hidden_turned[par][0:r, f, :], w,
                                          start=(f == 0), stop=(f == FT - 1))
                    last.then_inc(self.mixed, 1)

                def expert_of(k):
                    return eng.value_load(self.expert[0:1, bass.ds(k, 1)], min_val=0, max_val=E - 1)

                turn_x(0, 0, 16)
                e = expert_of(0)
                for c in range(2):
                    multiply(0, 0, c, e)
                turn_x(1, 1, 16)
                with eng.Fori(0, (self.BLOCKS - 1) // 2) as it:
                    for j in range(2):
                        k, par = it * 2 + (1 + j), 1 - j
                        e = expert_of(k)
                        multiply(k, par, 0, e)
                        turn_hidden(k - 1, 1 - par)
                        multiply(k, par, 1, e)
                        mix(k - 1, 1 - par, expert_of(k - 1))
                        turn_x(k + 1, 1 - par, it * 16 + 32)
                k = self.BLOCKS - 1
                turn_hidden(k, k % 2)
                mix(k, k % 2, expert_of(k))

            def act(self, eng):
                self.norm.act(eng)
                self.turn.act(eng)
                eng.wait_ge(self.shifted, 1)
                eng.activation(self.by_expert[1], self.by_expert[0], ACT.Exp).then_inc(self.route_exp, 1)
                eng.sem_inc(self.hidden_copied, 2)

                def silu(k, c):
                    eng.wait_ge(self.multiplied, k * 2 + (c + 1))
                    eng.wait_ge(self.gated, k * 2 + (c + 1))
                    eng.activation(self.silu[c], PS[:, 2 * c, 0:self.FC], ACT.Silu).then_inc(self.activated, 1)

                def copy_hidden(k, par):
                    eng.wait_ge(self.mixed, k + 1)
                    for h in range(2):
                        eng.wait_ge(self.hidden_read, k * 2 + (h + 5))
                        dst, left = self.hidden_turned[par], F0 - 5 * P
                        src = PS[:, 4 + h, 0:3 * P].rearrange("p (f c) -> p f c", f=3)
                        if h == 0:
                            last = eng.activation(dst[:, 0:3, :], src, ACT.Copy)
                        else:
                            eng.activation(dst[:, 3:5, :], src[:, 0:2, :], ACT.Copy)
                            last = eng.activation(dst[0:left, 5, :], src[0:left, 2, :], ACT.Copy)
                        last.then_inc(self.hidden_copied, 1)

                for c in range(2):
                    silu(0, c)
                with eng.Fori(0, (self.BLOCKS - 1) // 2) as it:
                    for j in range(2):
                        k, par = it * 2 + (1 + j), 1 - j
                        silu(k, 0)
                        copy_hidden(k - 1, 1 - par)
                        silu(k, 1)
                copy_hidden(self.BLOCKS - 1, (self.BLOCKS - 1) % 2)

            def dve(self, eng):
                chained = [0]

                def link(ins):
                    chained[0] += 1
                    ins.then_inc(self.chain, 1)
                    eng.wait_ge(self.chain, chained[0])

                eng.sem_inc(self.gated, 2)
                eng.sem_inc(self.x_copied, 1)
                eng.sem_inc(self.y_copied, 1)
                for par in range(2):
                    eng.sem_inc(self.y_stored[par], 16)
                link(eng.tensor_tensor(X[:], X[:], XN[:], ALU.add))
                self.norm.dve(eng)
                logits = PS[:, 7, 0:NT * E].rearrange("p (t e) -> p t e", t=NT)
                flat = self.by_expert
                shifted, powers, probs, rank, chosen, share, first, second, place = [
                    x.rearrange("p (t e) -> p t e", t=NT) for x in flat]
                total, other_total = self.row
                rows_in, blocks_in, block_start, block_end, start = self.few
                at = 0
                consts = []
                for n in (E * E, NT * NT, NT, self.K):
                    consts.append(self.constants[:, at:at + n])
                    at += n
                earlier = consts[0].rearrange("p (e o) -> p e o", e=E)
                tile_before = consts[1].rearrange("p (t u) -> p t u", t=NT)
                tile_rows, block_number = consts[2:]

                def over_experts(x):
                    return x.unsqueeze(2).to_broadcast([P, NT, E])

                eng.wait_ge(self.routed, 1)
                link(eng.tensor_reduce(total, logits, AX_X, ALU.max))
                eng.tensor_tensor(shifted, logits, over_experts(total), ALU.subtract).then_inc(self.shifted, 1)
                eng.wait_ge(self.route_exp, 1)
                link(eng.tensor_reduce(other_total, powers, AX_X, ALU.add))
                link(eng.reciprocal(total, other_total))
                link(eng.tensor_tensor(probs, powers, over_experts(total), ALU.mult))
                eng.wait_ge(self.constants_landed, 16)
                half = NT * E * E
                better, as_good = [self.grid[:, i * half:(i + 1) * half].rearrange("p (t e o) -> p t e o", t=NT, e=E)
                                   for i in range(2)]
                earlier_all = earlier.unsqueeze(1).to_broadcast([P, NT, E, E])
                other = probs.unsqueeze(2).to_broadcast([P, NT, E, E])
                this = probs.unsqueeze(3).to_broadcast([P, NT, E, E])
                eng.tensor_tensor(better, other, this, ALU.is_gt)
                link(eng.tensor_tensor(as_good, other, this, ALU.is_equal))
                link(eng.tensor_tensor(as_good, as_good, earlier_all, ALU.mult))
                link(eng.tensor_tensor(better, better, as_good, ALU.add))
                link(eng.tensor_reduce(rank, better, AX_X, ALU.add))
                eng.tensor_scalar(chosen, rank, 1.5, None, ALU.is_lt).then_inc(self.chosen, 1)
                eng.wait_ge(self.chosen, 1)
                link(eng.tensor_tensor(share, chosen, probs, ALU.mult))
                link(eng.tensor_reduce(other_total, share, AX_X, ALU.add))
                link(eng.reciprocal(total, other_total))
                link(eng.tensor_tensor(share, share, over_experts(total), ALU.mult))
                link(eng.tensor_tensor(better, chosen.unsqueeze(2).to_broadcast([P, NT, E, E]), earlier_all, ALU.mult))
                link(eng.tensor_reduce(rank, better, AX_X, ALU.add))
                link(eng.tensor_scalar(rank, rank, 0.5, None, ALU.is_lt))
                link(eng.tensor_tensor(first, rank, chosen, ALU.mult))
                link(eng.tensor_tensor(second, chosen, first, ALU.subtract))
                eng.wait_ge(self.counted, 1)
                counts = PS[:, 6, P:2 * P].rearrange("p (t e) -> p e t", t=NT)
                link(eng.tensor_copy(powers.rearrange("p t e -> p (t e)"), PS[:, 6, P:2 * P]))
                link(eng.tensor_reduce(rows_in, counts, AX_X, ALU.add))
                tiles = self.grid.rearrange("p (e t u) -> p e t u", e=E, t=NT)
                by_tile = powers.rearrange("p t e -> p e t").unsqueeze(2).to_broadcast([P, E, NT, NT])
                link(eng.tensor_tensor(tiles, by_tile, tile_before.unsqueeze(1).to_broadcast([P, E, NT, NT]), ALU.mult))
                link(eng.tensor_reduce(shifted.rearrange("p t e -> p e t"), tiles, AX_X, ALU.add))
                filled = self.grid[:, 0:E * NT].rearrange("p (e t) -> p e t", e=E)
                link(eng.tensor_tensor(filled, rows_in.unsqueeze(2).to_broadcast([P, E, NT]),
                                       tile_rows.unsqueeze(1).to_broadcast([P, E, NT]), ALU.is_gt))
                link(eng.tensor_reduce(blocks_in, filled, AX_X, ALU.add))
                before = self.grid[:, 0:E * E].rearrange("p (e o) -> p e o", e=E)
                link(eng.tensor_tensor(before, blocks_in.unsqueeze(1).to_broadcast([P, E, E]), earlier, ALU.mult))
                link(eng.tensor_reduce(block_start, before, AX_X, ALU.add))
                link(eng.tensor_tensor(block_end, block_start, blocks_in, ALU.add))
                ended = self.grid[:, 0:self.K * E].rearrange("p (k e) -> p k e", e=E)
                link(eng.tensor_tensor(ended, block_end.unsqueeze(1).to_broadcast([P, self.K, E]),
                                       block_number.unsqueeze(2).to_broadcast([P, self.K, E]), ALU.is_le))
                number = self.grid[:, E * self.K:E * self.K + self.K]
                link(eng.tensor_reduce(number, ended, AX_X, ALU.add))
                eng.tensor_scalar(self.expert, number, float(E - 1), None, ALU.min)
                link(eng.tensor_scalar(start, block_start, float(P), None, ALU.mult))
                link(eng.tensor_tensor(place, PS[:, 6, 0:P].rearrange("p (t e) -> p t e", t=NT), shifted, ALU.add))
                link(eng.tensor_tensor(place, place, start.unsqueeze(1).to_broadcast([P, NT, E]), ALU.add))
                for c, which in enumerate((first, second)):
                    link(eng.tensor_tensor(powers, which, share, ALU.mult))
                    link(eng.tensor_reduce(self.share[c], powers, AX_X, ALU.add))
                    link(eng.tensor_tensor(powers, which, place, ALU.mult))
                    link(eng.tensor_reduce(total, powers, AX_X, ALU.add))
                    link(eng.tensor_copy(self.place[:, c, :], total))
                eng.sem_inc(self.placed, 1)

                def copy_x(k, par):
                    eng.wait_ge(self.x_read, k + 1)
                    if not isinstance(k, int) or k >= 2:
                        eng.wait_ge(self.multiplied, k * 2 - 2)
                    for h in range(KH):
                        last = eng.tensor_scalar(self.x_turned[par][:, h, :], PS[:, 7, h * P:(h + 1) * P],
                                                 cols[:, COL["g2"], h:h + 1], None, ALU.mult)
                    last.then_inc(self.x_copied, 1)

                def gate(k, par, c):
                    if c == 0:
                        eng.wait_ge(self.hidden_read, k * 2 + 2)
                    eng.wait_ge(self.activated, k * 2 + (c + 1))
                    eng.tensor_tensor(self.hidden[par][:, c * self.FC:(c + 1) * self.FC], PS[:, 2 * c + 1, 0:self.FC],
                                      self.silu[c], ALU.mult).then_inc(self.gated, 1)

                def copy_y(k, par, stored):
                    eng.wait_ge(self.mixed, k + 3)
                    eng.wait_ge(self.y_stored[par], stored)
                    eng.tensor_copy(self.y[par], PS[:, 6, 0:D]).then_inc(self.y_copied, 1)

                copy_x(0, 0)
                for c in range(2):
                    gate(0, 0, c)
                copy_x(1, 1)
                with eng.Fori(0, (self.BLOCKS - 1) // 2) as it:
                    for j in range(2):
                        k, par = it * 2 + (1 + j), 1 - j
                        for c in range(2):
                            gate(k, par, c)
                        copy_y(k - 1, 1 - par, it * 16 + 16)
                        copy_x(k + 1, 1 - par)
                copy_y(self.BLOCKS - 1, (self.BLOCKS - 1) % 2, 16 * (1 + (self.BLOCKS - 1) // 2))
                for t in range(NT):
                    eng.wait_ge(self.gathered_row[t % 4], 32 * (t // 4 + 1))
                    link(eng.scalar_tensor_tensor(out=X[:, t, :], in0=self.gathered[t % 4][:, 0, :],
                                                  scalar=self.share[0][:, t:t + 1], in1=X[:, t, :],
                                                  op0=ALU.mult, op1=ALU.add))
                    eng.scalar_tensor_tensor(out=X[:, t, :], in0=self.gathered[t % 4][:, 1, :],
                                             scalar=self.share[1][:, t:t + 1], in1=X[:, t, :],
                                             op0=ALU.mult, op1=ALU.add).then_inc(self.added, 1)

        class FeedForward:

            FT = F1 // P
            PER_PASS = 2 * FT

            def __init__(self):
                take = carver()
                squares = take(NT, D)
                self.turned = take(KH, S)
                self.norm = Normalize("norm", X[:], XN[:], squares)
                self.turn = Turn([(XN[:, t], P) for t in range(NT)], self.turned)
                self.w1, self.w2 = take(KH, F1), take(self.FT, D)
                self.b1 = take(self.FT)
                self.affine = take(2, D)
                self.hidden = [take(self.FT, QB) for _ in range(2)]
                self.y = take(NT, D)
                self.last_norm = Normalize("last", self.y, self.y, squares)
                self.loaded = sem("ffn_loaded")
                self.hidden_ready = sem("ffn_hidden_ready")
                self.activated = sem("ffn_activated")
                self.mixed = sem("ffn_mixed")
                self.added = sem("ffn_added")
                self.chain = sem("ffn_chain")
                self.final = sem("ffn_final")
                self.stored = sem("ffn_stored")

            def sp(self, eng):
                eng.dma_start(self.w1, a["w1"].rearrange("(k p) f -> p k f", p=P)).then_inc(self.loaded, 16)
                eng.dma_start(self.w2, a["w2"].rearrange("(t p) d -> p t d", p=P)).then_inc(self.loaded, 16)
                eng.dma_start(self.b1, a["b1"]).then_inc(self.loaded, 16)
                eng.dma_start(self.affine, a["affine"].rearrange("p (r d) -> p r d", r=2)).then_inc(self.loaded, 16)
                for c in range(4):
                    eng.wait_ge(self.final, c + 1)
                    t = slice(c * NT // 4, (c + 1) * NT // 4)
                    eng.dma_start(out[0].rearrange("(t p) d -> p t d", p=P)[:, t, :], self.y[:, t, :]
                                  ).then_inc(self.stored, 16)
                eng.wait_ge(self.stored, 64)

            def pool(self, eng):
                self.norm.pool(eng)
                self.last_norm.pool(eng)

            def pe(self, eng):
                eng.wait_ge(self.norm.done, 1)
                self.turn.pe(eng)
                eng.wait_ge(self.turn.copied, len(self.turn.jobs))
                eng.wait_ge(self.loaded, 64)
                eng.sem_inc(self.mixed, 4)

                def mix(it, x):
                    eng.wait_ge(self.activated, it * self.PER_PASS + self.FT * (x + 1) + 4)
                    for half in range(2):
                        eng.wait_ge(self.added, it * 4 + 2 * x + half + 1)
                        for h in range(2):
                            s, dst = 2 * half + h, PS[:, 4 + half, h * D:(h + 1) * D]
                            for f in range(self.FT):
                                eng.matmul(dst, self.hidden[x][:, f, s * P:(s + 1) * P], self.w2[:, f, :],
                                           start=(f == 0), stop=False)
                            last = eng.matmul(dst, ones[0:1, :], rows[:, ROW["b2"], :], start=False, stop=True)
                        last.then_inc(self.mixed, 1)

                with eng.Fori(0, NB // 2) as it:
                    for x in range(2):
                        for f in range(self.FT):
                            count = x * self.FT + f
                            eng.wait_ge(self.activated, it * self.PER_PASS + count + 1)
                            for k in range(KH):
                                last = eng.matmul(PS[:, count % 4, :], self.w1[:, k, f * P:(f + 1) * P],
                                                  self.turned[:, k, bass.ds(it * (2 * QB) + x * QB, QB)],
                                                  start=(k == 0), stop=(k == KH - 1))
                            last.then_inc(self.hidden_ready, 1)
                            if x and f == 1:
                                mix(it, 0)
                    mix(it, 1)

            def act(self, eng):
                self.norm.act(eng)
                self.turn.act(eng)
                eng.wait_ge(self.loaded, 64)
                eng.sem_inc(self.activated, 4)
                with eng.Fori(0, NB // 2) as it:
                    for x in range(2):
                        for f in range(self.FT):
                            count = x * self.FT + f
                            eng.wait_ge(self.hidden_ready, it * self.PER_PASS + count + 1)
                            if f == 0:
                                eng.wait_ge(self.mixed, it * 4 + 2 * x + 2)
                            eng.activation(self.hidden[x][:, f, :], PS[:, count % 4, :], ACT.Relu,
                                           bias=self.b1[:, f:f + 1]).then_inc(self.activated, 1)
                self.last_norm.act(eng)

            def dve(self, eng):
                eng.sem_inc(self.added, 2)
                self.norm.dve(eng)
                with eng.Fori(0, NB // 2) as it:
                    for x in range(2):
                        for half in range(2):
                            eng.wait_ge(self.mixed, it * 4 + 2 * x + half + 1 + 4)
                            tiles = bass.ds(it * (2 * SPB) + (x * SPB + 2 * half), 2)
                            eng.tensor_tensor(self.y[:, tiles, :],
                                              PS[:, 4 + half, :].rearrange("p (t d) -> p t d", t=2),
                                              XN[:, tiles, :], ALU.add).then_inc(self.added, 1)
                eng.wait_ge(self.added, 2 + 2 * NB)
                self.last_norm.dve(eng)
                eng.wait_ge(self.last_norm.done, 1)
                chained = 0
                for c in range(4):
                    y = self.y[:, c * NT // 4:(c + 1) * NT // 4, :]
                    shape = [P, NT // 4, D]
                    for op, other in ((ALU.mult, self.affine[:, 0, :].unsqueeze(1).to_broadcast(shape)),
                                      (ALU.add, self.affine[:, 1, :].unsqueeze(1).to_broadcast(shape))):
                        chained += 1
                        eng.tensor_tensor(y, y, other, op).then_inc(self.chain, 1)
                        eng.wait_ge(self.chain, chained)
                    eng.tensor_tensor(y, y, X[:, c * NT // 4:(c + 1) * NT // 4, :], ALU.add).then_inc(self.final, 1)

        stages = [Setup(), Context(),
                  Prepare(0), Attention(0, True, False), None,
                  Prepare(1), Attention(1, False, True), None, Experts(),
                  Prepare(2), Attention(2, True, True), None, FeedForward()]
        stages[4] = Output(0, stages[3].attended, X[:], X[:], rows[:, ROW["o0"], :])
        stages[7] = Output(1, stages[6].attended, XN[:], XN[:], None)
        stages[11] = Output(2, stages[10].attended, X[:], X[:], rows[:, ROW["o2"], :])

        numbers = sorted(x.num for x in roles.values())
        assert numbers == list(range(numbers[0], numbers[-1] + 1))

        stage_semaphores = range(numbers[0], numbers[-1] + 1)

        for stage in stages:
            with nc.Block() as block:
                @block.sync
                def _(eng):
                    stage.sp(eng)

                @block.scalar
                def _(eng):
                    stage.act(eng)

                @block.tensor
                def _(eng):
                    stage.pe(eng)

                @block.vector
                def _(eng):
                    stage.dve(eng)

                @block.gpsimd
                def _(eng):
                    stage.pool(eng)

            nc.all_engine_barrier(sems_to_clear=stage_semaphores)


def kernel(**inputs):
    import numpy as np
    import concourse.bacc as bacc
    from concourse.bass_utils import run_bass_kernel_spmd

    f = {k: np.asarray(v) for k, v in inputs.items()}

    def turned_heads(w):
        return w.reshape(D, H, 2, DK // 2)[:, :, ::-1, :].reshape(D, D)

    def column(v):
        return v.reshape(-1, P).T

    inverse_frequency = 1.0 / 10000.0 ** (np.arange(0, DK, 2, dtype=np.float32) / DK)
    angles = np.einsum("i,j->ij", np.arange(S, dtype=np.float32), inverse_frequency)
    angles = np.concatenate([angles, angles], axis=-1).astype(np.float32)
    sign = np.where(np.arange(DK) < DK // 2, -1.0, 1.0).astype(np.float32)
    rope = np.stack([np.tile(np.cos(angles).T, (P // DK, 1)), np.tile((np.sin(angles) * sign).T, (P // DK, 1))])
    later = np.triu(np.full((P, P), NEG, np.float32), 1)
    routing = np.concatenate([np.tril(np.ones((E, E)), -1).ravel(), np.tril(np.ones((NT, NT)), -1).ravel(),
                              P * np.arange(NT), np.arange(2 * S // P + E)]).astype(np.float32)
    counting = np.concatenate([np.triu(np.ones((P, P)), 1), np.ones((P, P))], 1).astype(np.float32)

    arrays = {
        "x": f["x"][0], "ctx": f["ctx_1024"][0],
        "identity": np.eye(P, dtype=np.float32), "masks": np.stack([later, later.T]),
        "rope": rope.astype(np.float32), "routing": routing.reshape(1, -1).repeat(P, 0),
        "counting": counting,
        "w_q0": f["L0_xattn_w_q"].T, "w_k0": f["L0_xattn_w_k"].T, "w_v0": f["L0_xattn_w_v"].T, "w_o0": f["L0_xattn_w_o"].T,
        "w_q1": f["L0_ffn_wq"], "w_q1_turned": turned_heads(f["L0_ffn_wq"]), "w_k1": f["L0_ffn_wk"],
        "w_k1_turned": turned_heads(f["L0_ffn_wk"]), "w_v1": f["L0_ffn_wv"], "w_o1": f["L0_ffn_wo"],
        "w_q2": f["L1_xattn_Wq"], "w_kv2": f["L1_xattn_Wkv"], "w_o2": f["L1_xattn_Wout"],
        "w_router": f["L0_ffn_w_router"],
        "rows": np.stack([f["L0_xattn_b_v"], f["L0_xattn_b_o"], f["L1_xattn_bout"], f["L1_ffn_b2"][0]]),
        "cols": np.concatenate([column(f[k]) for k in ("L0_xattn_b_q", "L0_xattn_b_k", "L0_ffn_g1", "L0_ffn_g2")], 1),
        "wg": f["L0_ffn_wg"].reshape(E * D, F0), "wu": f["L0_ffn_wu"].reshape(E * D, F0),
        "wd": f["L0_ffn_wd"].reshape(E * F0, D),
        "w1": f["L1_ffn_w1"][0], "w2": f["L1_ffn_w2"][0], "b1": column(f["L1_ffn_b1"][0]),
        "affine": np.stack([f["L1_ffn_gamma"], f["L1_ffn_beta"]]).reshape(1, 2 * D).repeat(P, 0),
    }
    arrays = {f"in_{k}": np.ascontiguousarray(v) for k, v in arrays.items()}
    nc = bacc.Bacc("TRN2", target_bir_lowering=False, num_devices=1)
    args = {k[3:]: nc.dram_tensor(k, v.shape, mybir.dt.from_np(v.dtype), kind="ExternalInput").ap()
            for k, v in arrays.items()}
    out = nc.dram_tensor("out_x", (1, S, D), F32, kind="ExternalOutput").ap()
    build(nc, args, out)
    result = run_bass_kernel_spmd(nc, [arrays], core_ids=[0])
    return result.results[0]["out_x"]
```

```python
from contextlib import ExitStack

import concourse.bass as bass
from concourse import mybir

ALU = mybir.AluOpType
ACT = mybir.ActivationFunctionType
F32 = mybir.dt.float32
BF16 = mybir.dt.bfloat16
AX_X = mybir.AxisListType.X

P = 128
S = 2048
C = 1601
D = 256
H = 16
DK = D // H
KH = D // P
NT = S // P
NC = -(-C // P)
QB = 512
NB = S // QB
SPB = QB // P
G = 4
NG = H // G
VW = 32
E = 8
F0 = 704
F1 = 1024
NEG = -1.0e30
SCALE = DK ** -0.5
LN_EPS = 1e-5
RMS_EPS = 1e-6

Q_PARTS = (0, 0, 0, 1, 1, 2)
K_PARTS = (0, 1, 2, 0, 1, 0)
PEAK_ROW = 6 * DK
SCORE_ROWS = PEAK_ROW + 3


def dims(ap, *shape):
    if len(shape) == 1:
        return ap
    if len(shape) == 2:
        return ap.rearrange("p (a b) -> p a b", a=shape[0])
    return ap.rearrange("p (a b c) -> p a b c", a=shape[0], b=shape[1])


def build(nc, a, out):
    with ExitStack() as ctx:
        roles = {}

        def sem(role):
            if role not in roles:
                roles[role] = ctx.enter_context(nc.semaphore(role))
            return roles[role]

        def sb(name, shape, dt=F32):
            return ctx.enter_context(nc.sbuf_tensor(name, shape, dt))

        def scratch(name, shape, dt):
            return nc.dram_tensor(name, shape, dt, kind="Internal").ap()

        X = sb("X", [P, NT, D])
        XN = sb("XN", [P, NT, D])
        identity = sb("identity", [P, P])
        identity16 = sb("identity16", [P, P], BF16)
        mask_qk = sb("mask_qk", [P, P], BF16)
        mask_kq = sb("mask_kq", [P, P], BF16)
        ones = sb("ones", [1, P])
        minus_half = sb("minus_half", [P, NT])
        stats = sb("stats", [P, 4, NT])
        rows = sb("rows", [1, 4, D])
        ROW = {"v0": 0, "o0": 1, "o2": 2, "b2": 3}
        cols = sb("cols", [P, 4, KH])
        COL = {"q0": 0, "k0": 1, "g1": 2, "g2": 3}
        ARENA = 43000
        arena = sb("arena", [P, ARENA])
        PS = ctx.enter_context(nc.psum_tensor("PS", [P, 8, QB], F32))

        def carver():
            at = [0]

            def take(*shape, dt=F32):
                n = 1
                for x in shape:
                    n *= x
                words = n if dt == F32 else -(-n // 2)
                part = arena[:, at[0]:at[0] + words]
                at[0] += words
                assert at[0] <= ARENA, at[0]
                if dt != F32:
                    part = part.bitcast(dt)[:, 0:n]
                return dims(part, *shape)
            take.at = at
            return take

        WEIGHTS = {"q0": D, "k0": D, "v0": D, "o0": D, "q1": D, "q1_turned": D, "k1": D, "k1_turned": D, "v1": D,
                   "o1": D, "q2": D, "kv2": 2 * D, "o2": D, "router": E}

        class Weights:

            def __init__(self, take, *names, landed="weights_landed"):
                self.at = {name: take(KH, WEIGHTS[name]) for name in names}
                self.landed = sem(landed)

            def __getitem__(self, name):
                return self.at[name]

            def sp(self, eng):
                for name, dst in self.at.items():
                    eng.dma_start(dst, a[f"w_{name}"].rearrange("(k p) n -> p k n", p=P)).then_inc(self.landed, 16)

            def wait(self, eng):
                eng.wait_ge(self.landed, 16 * len(self.at))

        q_parts = [scratch(f"q_parts{i}", (3, D, S), BF16) for i in range(3)]
        k_parts_ctx = {i: scratch(f"k_parts_ctx{i}", (3, D, C), BF16) for i in (0, 2)}
        k_parts_own = {i: scratch(f"k_parts_own{i}", (3, D, S), BF16) for i in (1, 2)}
        v_ctx = {i: scratch(f"v_ctx{i}", (NC * P, H * VW), F32) for i in (0, 2)}
        rows_sorted = scratch("rows_sorted", ((2 * S // P + E) * P, D), F32)
        results_sorted = scratch("results_sorted", ((2 * S // P + E - 1) * P, D), F32)
        v_own = {i: scratch(f"v_own{i}", (S, H * VW), F32) for i in (1, 2)}


        class Setup:

            def __init__(self):
                self.loaded = sem("setup_loaded")
                take = carver()
                self.masks = take(2, P)

            def sp(self, eng):
                eng.dma_start(identity[:], a["identity"]).then_inc(self.loaded, 16)
                eng.dma_start(self.masks, a["masks"].rearrange("m p c -> p m c")).then_inc(self.loaded, 16)
                eng.dma_start(rows[:], a["rows"].rearrange("(o r) d -> o r d", o=1)).then_inc(self.loaded, 16)
                eng.dma_start(cols[:], a["cols"].rearrange("p (r k) -> p r k", r=4)).then_inc(self.loaded, 16)
                eng.wait_ge(self.loaded, 16 * 4)

            def act(self, eng):
                pass

            def pe(self, eng):
                pass

            def dve(self, eng):
                eng.wait_ge(self.loaded, 16 * 4)
                eng.tensor_copy(identity16[:], identity[:])
                eng.tensor_copy(mask_qk[:], self.masks[:, 0, :])
                eng.tensor_copy(mask_kq[:], self.masks[:, 1, :])

            def pool(self, eng):
                eng.memset(ones[:], 1.0)
                eng.memset(minus_half[:], -0.5)

        class Turn:

            def __init__(self, sources, dst, gain=None, name="turn", norm=None):
                self.sources, self.dst, self.gain, self.norm = sources, dst, gain, norm
                self.turned, self.copied = sem(f"{name}_turned"), sem(f"{name}_copied")
                self.jobs = [(b, half) for b in range(0, len(sources), SPB) for half in range(KH)]

            def pe(self, eng):
                for n, (b, half) in enumerate(self.jobs):
                    if self.norm is not None and half == 0:
                        self.norm.wait(eng, b // SPB)
                    if n >= 2:
                        eng.wait_ge(self.copied, n - 1)
                    for i, (src, r) in enumerate(self.sources[b:b + SPB]):
                        last = eng.transpose(PS[:, n % 2, i * P:i * P + r], src[0:r, half * P:(half + 1) * P],
                                             identity[0:r, 0:r])
                    last.then_inc(self.turned, 1)

            def act(self, eng):
                for n, (b, half) in enumerate(self.jobs):
                    w = sum(r for _, r in self.sources[b:b + SPB])
                    eng.wait_ge(self.turned, n + 1)
                    scale = 1.0 if self.gain is None else self.gain[:, half:half + 1]
                    eng.activation(self.dst[:, half, b * P:b * P + w], PS[:, n % 2, 0:w], ACT.Identity,
                                   scale=scale).then_inc(self.copied, 1)

        class Project:

            SLOTS = 4

            def __init__(self, take, src, jobs, value_jobs, cos=None, sin=None):
                self.src, self.jobs, self.value_jobs, self.cos, self.sin = src, jobs, value_jobs, cos, sin
                self.full = take(4, QB)
                self.parts = take(4, 3, QB, dt=BF16)
                self.values = take(self.SLOTS * H, VW).rearrange("p (s h) w -> p s h w", s=self.SLOTS)
                self.values_set = sem("project_values_set")
                self.rope = take(2, QB) if cos is not None else None
                self.projected = sem("project_projected")
                self.full_ready = sem("project_full_ready")
                self.high_ready = sem("project_high_ready")
                self.rest_ready = sem("project_rest_ready")
                self.middle_ready = sem("project_middle_ready")
                self.low_ready = sem("project_low_ready")
                self.rotated = sem("project_rotated")
                self.parts_stored = [sem(f"project_parts_stored{i}") for i in range(4)]
                self.value_projected = sem("project_value_projected")
                self.value_staged = sem("project_value_staged")
                self.value_stored = [sem(f"project_value_stored{i}") for i in range(self.SLOTS)]
                self.steps = len(jobs)

            def values_at(self, n):
                total = len(self.value_jobs)
                return range(n * total // self.steps, (n + 1) * total // self.steps)

            def pe(self, eng):
                for n in range(self.steps):
                    if n < len(self.jobs):
                        j = self.jobs[n]
                        if n >= 3:
                            eng.wait_ge(self.full_ready, n - 2)
                        for bank, w in ((n % 3, j["w"]), (3 + n % 3, j.get("turned"))):
                            if w is None:
                                continue
                            for k in range(KH):
                                last = eng.matmul(PS[:, bank, 0:j["n"]], w[:, k, j["half"] * P:(j["half"] + 1) * P],
                                                  self.src[:, k, j["c0"]:j["c0"] + j["n"]],
                                                  start=(k == 0), stop=(k == KH - 1))
                        last.then_inc(self.projected, 1)
                    for m in self.values_at(n):
                        v = self.value_jobs[m]
                        if m >= 2:
                            eng.wait_ge(self.value_staged, m - 1)
                        r, dst = v["rows"], PS[0:v["rows"], 6 + m % 2, 0:D]
                        for k in range(KH):
                            last = eng.matmul(dst, self.src[:, k, v["c0"]:v["c0"] + r], v["w"][:, k, :],
                                              start=(k == 0), stop=(k == KH - 1 and v["bias"] is None))
                        if v["bias"] is not None:
                            last = eng.matmul(dst, ones[0:1, 0:r], v["bias"], start=False, stop=True)
                        last.then_inc(self.value_projected, 1)

            def act(self, eng, between=None):
                eng.wait_ge(self.values_set, 2)
                for n in range(self.steps + 1):
                    if between is not None:
                        between(n)
                    if n < len(self.jobs):
                        j = self.jobs[n]
                        eng.wait_ge(self.full_ready, n + 1)
                        if n >= 4:
                            eng.wait_ge(self.parts_stored[n % 4], 16 * (n // 4))
                        eng.activation(self.parts[:, n % 4, 0, 0:j["n"]], self.full[:, n % 4, 0:j["n"]],
                                       ACT.Copy).then_inc(self.high_ready, 1)
                    if 1 <= n <= len(self.jobs):
                        m = n - 1
                        w = self.jobs[m]["n"]
                        eng.wait_ge(self.rest_ready, m + 1)
                        eng.activation(self.parts[:, m % 4, 1, 0:w], self.full[:, m % 4, 0:w],
                                       ACT.Copy).then_inc(self.middle_ready, 1)
                    for m in self.values_at(n) if n < self.steps else ():
                        r = self.value_jobs[m]["rows"]
                        eng.wait_ge(self.value_projected, m + 1)
                        if m >= self.SLOTS:
                            eng.wait_ge(self.value_stored[m % self.SLOTS], 16 * (m // self.SLOTS))
                        eng.activation(self.values[0:r, m % self.SLOTS, :, 0:DK],
                                       PS[0:r, 6 + m % 2, 0:D].rearrange("p (h d) -> p h d", h=H),
                                       ACT.Copy).then_inc(self.value_staged, 1)

            def dve(self, eng, between=None):
                turned = 0
                for n in range(len(self.jobs) + 2):
                    if between is not None:
                        between(n)
                    if n < len(self.jobs):
                        j = self.jobs[n]
                        w, full = j["n"], self.full[:, n % 4, 0:j["n"]]
                        eng.wait_ge(self.projected, n + 1)
                        if n >= 4:
                            eng.wait_ge(self.low_ready, n - 3)
                        if j.get("turned") is not None:
                            rope = slice(j["c0"], j["c0"] + w)
                            if n:
                                eng.wait_ge(self.full_ready, n)
                            eng.scalar_tensor_tensor(out=self.rope[:, 0, 0:w], in0=PS[:, n % 3, 0:w], scalar=j["scale"],
                                                     in1=self.cos[:, rope], op0=ALU.mult, op1=ALU.mult)
                            eng.scalar_tensor_tensor(out=self.rope[:, 1, 0:w], in0=PS[:, 3 + n % 3, 0:w],
                                                     scalar=j["scale"], in1=self.sin[:, rope], op0=ALU.mult,
                                                     op1=ALU.mult).then_inc(self.rotated, 1)
                            turned += 1
                            eng.wait_ge(self.rotated, turned)
                            eng.tensor_tensor(full, self.rope[:, 0, 0:w], self.rope[:, 1, 0:w],
                                              ALU.add).then_inc(self.full_ready, 1)
                        elif j.get("bias") is not None:
                            eng.tensor_scalar(full, PS[:, n % 3, 0:w], j["bias"], j["scale"], ALU.add,
                                              ALU.mult).then_inc(self.full_ready, 1)
                        else:
                            eng.tensor_scalar(full, PS[:, n % 3, 0:w], j["scale"], None,
                                              ALU.mult).then_inc(self.full_ready, 1)
                    if 1 <= n <= len(self.jobs):
                        m = n - 1
                        w = self.jobs[m]["n"]
                        eng.wait_ge(self.high_ready, m + 1)
                        eng.tensor_tensor(self.full[:, m % 4, 0:w], self.full[:, m % 4, 0:w],
                                          self.parts[:, m % 4, 0, 0:w], ALU.subtract).then_inc(self.rest_ready, 1)
                    if n >= 2:
                        m = n - 2
                        w = self.jobs[m]["n"]
                        eng.wait_ge(self.middle_ready, m + 1)
                        eng.tensor_tensor(self.parts[:, m % 4, 2, 0:w], self.full[:, m % 4, 0:w],
                                          self.parts[:, m % 4, 1, 0:w], ALU.subtract).then_inc(self.low_ready, 1)

            def pool(self, eng):
                eng.memset(self.values, 0.0).then_inc(self.values_set, 1)
                eng.wait_ge(self.values_set, 1)
                eng.memset(self.values[:, :, :, DK:DK + 1], 1.0).then_inc(self.values_set, 1)

            def sp(self, eng):
                for n in range(self.steps):
                    for m in self.values_at(n):
                        v = self.value_jobs[m]
                        r = v["rows"]
                        eng.wait_ge(self.value_staged, m + 1)
                        eng.dma_start(v["dst"][v["c0"]:v["c0"] + r, :],
                                      self.values[0:r, m % self.SLOTS].rearrange("p h d -> p (h d)")
                                      ).then_inc(self.value_stored[m % self.SLOTS], 16)
                    if n < len(self.jobs):
                        j = self.jobs[n]
                        eng.wait_ge(self.low_ready, n + 1)
                        dst = j["dst"][:, j["half"] * P:(j["half"] + 1) * P, j["c0"]:j["c0"] + j["n"]]
                        eng.dma_start(dst.rearrange("a p c -> p a c"),
                                      self.parts[:, n % 4, :, 0:j["n"]]).then_inc(self.parts_stored[n % 4], 16)
                for i in range(4):
                    eng.wait_ge(self.parts_stored[i], 16 * len(range(i, len(self.jobs), 4)))
                for i in range(self.SLOTS):
                    eng.wait_ge(self.value_stored[i], 16 * len(range(i, len(self.value_jobs), self.SLOTS)))

        def feature_jobs(w, dst, width, scale=1.0, bias=None, turned=None):
            return [dict(w=w, turned=turned, bias=None if bias is None else bias[:, half:half + 1], scale=scale,
                         dst=dst, half=half, c0=c0, n=min(QB, width - c0))
                    for c0 in range(0, width, QB) for half in range(KH)]

        def value_jobs(w, dst, width, bias=None):
            return [dict(w=w, bias=bias, dst=dst, c0=c0, rows=min(P, width - c0)) for c0 in range(0, width, P)]

        class Context:

            def __init__(self):
                take = carver()
                self.rows = take(NC, D)
                turned = take(KH, NC * P)
                self.norm = Normalize(X[:], XN[:], take(NT, D))
                self.loaded = sem("ctx_loaded")
                self.x_loaded = sem("ctx_x_loaded")
                self.zeros = take(D)
                self.zeroed = sem("ctx_zeroed")
                self.zeros_stored = sem("ctx_zeros_stored")
                self.turn = Turn([(self.rows[:, t], min(P, C - t * P)) for t in range(NC)], turned)
                self.weights = weights = Weights(take, "k0", "v0", "kv2")
                kv2 = weights["kv2"]
                self.project = Project(
                    take, turned,
                    feature_jobs(weights["k0"], k_parts_ctx[0], C, bias=cols[:, COL["k0"], :])
                    + feature_jobs(kv2[:, :, 0:D], k_parts_ctx[2], C),
                    value_jobs(weights["v0"], v_ctx[0], C, bias=rows[:, ROW["v0"], :])
                    + value_jobs(kv2[:, :, D:2 * D], v_ctx[2], C))

            def sp(self, eng):
                full = C // P
                eng.dma_start(self.rows[:, 0:full, :], a["ctx"][0:full * P, :].rearrange("(t p) d -> p t d", p=P)
                              ).then_inc(self.loaded, 16)
                eng.dma_start(self.rows[0:C - full * P, full, :], a["ctx"][full * P:C, :]).then_inc(self.loaded, 16)
                eng.dma_start(X[:], a["x"].rearrange("(t p) d -> p t d", p=P)).then_inc(self.x_loaded, 16)
                self.weights.sp(eng)
                eng.wait_ge(self.zeroed, 1)
                eng.dma_start(rows_sorted.rearrange("(k p) d -> p k d", p=P),
                              self.zeros.unsqueeze(1).to_broadcast([P, Experts.K, D])).then_inc(self.zeros_stored, 16)
                self.project.sp(eng)
                eng.wait_ge(self.zeros_stored, 16)

            def pe(self, eng):
                eng.wait_ge(self.loaded, 32)
                self.turn.pe(eng)
                eng.wait_ge(self.turn.copied, len(self.turn.jobs))
                self.weights.wait(eng)
                self.project.pe(eng)

            def act(self, eng):
                self.turn.act(eng)
                self.project.act(eng, lambda n: n % 2 or self.norm.act(eng, n // 2, n // 2 + 1))

            def dve(self, eng):
                eng.wait_ge(self.x_loaded, 16)

                def norm_tick(n):
                    if n % 2 == 0 and n // 2 < self.norm.ticks:
                        self.norm.tick(eng, n // 2)

                self.project.dve(eng, norm_tick)

            def pool(self, eng):
                eng.memset(self.zeros, 0.0).then_inc(self.zeroed, 1)
                self.project.pool(eng)
                self.norm.pool(eng)

        class Normalize:

            CHUNKS = NT // SPB

            def __init__(self, x, xn, squares, layer=True, rms=False, summed=False):
                self.x, self.xn, self.squares, self.layer, self.rms = x, xn, squares, layer, rms
                self.summed = summed
                name = "norm"
                self.step = sem(f"{name}_step")
                self.centred = sem(f"{name}_centred")
                self.squared = sem(f"{name}_squared")
                self.spread = sem(f"{name}_spread")
                self.inverse = sem(f"{name}_inverse")
                self.done = sem(f"{name}_done")
                self.rounds = int(layer) + int(rms)
                self.result = squares if rms else xn
                self.ticks = self.CHUNKS + 2 * self.rounds
                self.order = [(r, t - 1 - 2 * r) for t in range(self.ticks) for r in range(self.rounds)
                              if 0 <= t - 1 - 2 * r < self.CHUNKS]
                self.steps = 0

            def at(self, chunk):
                return slice(chunk * SPB, (chunk + 1) * SPB)

            def over_rows(self, i, chunk):
                return stats[:, i, self.at(chunk)].unsqueeze(2).to_broadcast([P, SPB, D])

            def wait(self, eng, chunk):
                eng.wait_ge(self.done, 1 + self.order.index((self.rounds - 1, chunk)))

            def tick(self, eng, t):
                def step(ins):
                    self.steps += 1
                    ins.then_inc(self.step, 1)
                    eng.wait_ge(self.step, self.steps)

                if t < self.CHUNKS and not self.layer:
                    c = self.at(t)
                    eng.tensor_tensor(self.x[:, c, :], self.x[:, c, :], self.xn[:, c, :],
                                      ALU.add).then_inc(self.centred, 1)
                elif t < self.CHUNKS:
                    c = self.at(t)
                    if not self.summed:
                        step(eng.tensor_reduce(stats[:, 0, c], self.x[:, c, :], AX_X, ALU.add))
                    step(eng.tensor_scalar(stats[:, 1, c], stats[:, 0, c], 1.0 / D, None, ALU.mult))
                    eng.tensor_tensor(self.xn[:, c, :], self.x[:, c, :], self.over_rows(1, t),
                                      ALU.subtract).then_inc(self.centred, 1)
                for r in range(self.rounds):
                    is_rms = self.rms and r == self.rounds - 1
                    k = t - 1 - 2 * r
                    if 0 <= k < self.CHUNKS:
                        c, n = self.at(k), self.order.index((r, k))
                        eng.wait_ge(self.squared, n + 1)
                        eng.tensor_scalar(stats[:, 2, c], stats[:, 2, c], 1.0 / D, RMS_EPS if is_rms else LN_EPS,
                                          ALU.mult, ALU.add).then_inc(self.spread, 1)
                    k = t - 2 - 2 * r
                    if 0 <= k < self.CHUNKS:
                        c, n = self.at(k), self.order.index((r, k))
                        eng.wait_ge(self.inverse, n + 1)
                        eng.tensor_tensor((self.squares if is_rms else self.xn)[:, c, :], self.xn[:, c, :],
                                          self.over_rows(3, k), ALU.mult).then_inc(self.done, 1)

            def dve(self, eng):
                for t in range(self.ticks):
                    self.tick(eng, t)

            def act(self, eng, first=0, end=None):
                for r, k in self.order[first:end]:
                    if r == 0:
                        eng.wait_ge(self.centred, k + 1)
                    else:
                        eng.wait_ge(self.done, 1 + self.order.index((r - 1, k)))
                    for t in range(k * SPB, (k + 1) * SPB):
                        last = eng.activation(self.squares[:, t, :], self.xn[:, t, :], ACT.Square,
                                              accum_out=stats[:, 2, t:t + 1])
                    last.then_inc(self.squared, 1)

            def pool(self, eng, first=0, end=None):
                for n, (r, k) in list(enumerate(self.order))[first:end]:
                    c = self.at(k)
                    eng.wait_ge(self.spread, n + 1)
                    eng.tensor_tensor(stats[:, 3, c], stats[:, 2, c], minus_half[:, c], ALU.pow).then_inc(self.inverse, 1)

        class Prepare:

            def __init__(self, i, attention, output=None):
                self.i, self.attention, self.output = i, attention, output
                take = carver() if output is None else output.take
                turned = take(KH, S)
                self.norm = Normalize(X[:], XN[:], take(NT, D), rms=True, summed=True) if i == 1 else None
                source = self.norm.result if i == 1 else XN[:]
                self.turn = Turn([(source[:, t], P) for t in range(NT)], turned,
                                 gain=cols[:, COL["g1"], :] if i == 1 else None, norm=self.norm)
                self.tables_loaded = None
                self.weights = weights = Weights(take, *(("q0",), ("q1", "q1_turned", "k1", "k1_turned", "v1"),
                                                         ("q2", "kv2"))[i])
                if i == 0:
                    jobs, values_of = feature_jobs(weights["q0"], q_parts[0], S, SCALE, cols[:, COL["q0"], :]), []
                    self.project = Project(take, turned, jobs, values_of)
                elif i == 1:
                    self.tables = take(2, S)
                    self.tables_loaded = sem("prep1_tables_loaded")
                    jobs = (feature_jobs(weights["q1"], q_parts[1], S, SCALE, turned=weights["q1_turned"])
                            + feature_jobs(weights["k1"], k_parts_own[1], S, turned=weights["k1_turned"]))
                    self.project = Project(take, turned, jobs, value_jobs(weights["v1"], v_own[1], S),
                                           cos=self.tables[:, 0], sin=self.tables[:, 1])
                else:
                    jobs = (feature_jobs(weights["q2"], q_parts[2], S, SCALE)
                            + feature_jobs(weights["kv2"][:, :, 0:D], k_parts_own[2], S))
                    self.project = Project(take, turned, jobs,
                                           value_jobs(weights["kv2"][:, :, D:2 * D], v_own[2], S))
                if attention.has_ctx:
                    assert take.at[0] <= attention.early_at

            def sp(self, eng):
                if self.output is not None:
                    self.output.sp(eng)
                self.weights.sp(eng)
                if self.tables_loaded is not None:
                    eng.dma_start(self.tables, a["rope"].rearrange("m p s -> p m s")).then_inc(self.tables_loaded, 16)
                self.attention.load_early(eng)
                self.project.sp(eng)
                self.attention.wait_early(eng)

            def pe(self, eng):
                if self.output is not None:
                    self.output.pe(eng)
                self.turn.pe(eng)
                eng.wait_ge(self.turn.copied, len(self.turn.jobs))
                self.weights.wait(eng)
                self.project.pe(eng)

            def act(self, eng):
                if self.output is not None:
                    self.output.act(eng)
                    self.norm.act(eng)
                self.turn.act(eng)
                self.project.act(eng)

            def dve(self, eng):
                if self.output is not None:
                    self.output.dve(eng, self.norm)
                if self.tables_loaded is not None:
                    eng.wait_ge(self.tables_loaded, 16)
                self.project.dve(eng)

            def pool(self, eng):
                self.project.pool(eng)
                if self.norm is not None:
                    self.norm.pool(eng)

        class Attention:

            BLOCKS = 2 * NB

            def __init__(self, i, has_ctx, has_own):
                self.i, self.has_ctx, self.has_own = i, has_ctx, has_own
                name = "attention"
                self.own0 = C + C % 2 if has_ctx else 0
                self.keys = self.own0 + (S if has_own else 0)
                self.nctx = NC if has_ctx else 0
                self.nv = self.nctx + (NT if has_own else 0)
                take = carver()
                k1, v1 = take(G, self.keys, dt=BF16), take(self.nv, G, VW)
                self.q = [take(G, QB, dt=BF16) for _ in range(NB)]
                self.probs = [[take(2, QB) for _ in range(2)] for _ in range(2)]
                self.sums = [take(QB) for _ in range(2)]
                self.early_at = take.at[0]
                self.k, self.v = [take(G, self.keys, dt=BF16), k1], [take(self.nv, G, VW), v1]
                self.attended = XN[:] if i != 1 else take(NT, D)
                self.peaks = take(SPB * G, 8)
                self.peak = take(3, SPB * G)
                self.peak_parts = take(P // (SPB * G), SPB * G, dt=BF16)
                self.peak_rows = take(P, dt=BF16)
                self.inverse = take(SPB, G)
                self.k_landed = [sem(f"{name}_k_landed{i}") for i in range(2)]
                self.v_landed = [sem(f"{name}_v_landed{i}") for i in range(2)]
                self.early_landed = sem(f"{name}_early_landed")
                self.q_landed = [sem(f"{name}_q_landed{i}") for i in range(NB)]
                self.ones_set = sem(f"{name}_ones_set")
                self.ring_ready = sem(f"{name}_ring_ready")
                self.ring_read = sem(f"{name}_ring_read")
                self.peaks_split = sem(f"{name}_peaks_split")
                self.peaks_copied = sem(f"{name}_peaks_copied")
                self.peaks_landed = sem(f"{name}_peaks_landed")
                self.scores_ready = sem(f"{name}_scores_ready")
                self.probs_ready = sem(f"{name}_probs_ready")
                self.probs_used = sem(f"{name}_probs_used")
                self.sums_copied = sem(f"{name}_sums_copied")
                self.chain = sem(f"{name}_chain")
                self.plan()


            RING = (4, 5, 7)

            LOOK = 3

            def plan(self):
                self.pieces = [self.pieces_of(b) for b in range(NB)]
                self.units = [self.units_of(b) for b in range(NB)]
                while (2 * sum(map(len, self.pieces)) + 2 * self.BLOCKS) % len(self.RING):
                    self.pieces[0].append(min(self.pieces[0], key=self.width))
                self.units_loop = 2 * sum(map(len, self.units))
                assert self.units_loop % 2 == 0
                jobs = [(what, n, k) for n in range(2 * self.BLOCKS)
                        for what, k in [("piece", k) for k in range(len(self.pieces[n % NB]))] + [("peaks", 0)]]
                a_pass = sum(n < self.BLOCKS for _, n, _ in jobs)
                least = len(self.pieces[0]) + 1
                most = sum(len(self.pieces[n]) + 1 for n in range(self.LOOK))
                tries = [(lead, slack, margin) for lead in range(least, most, 3)
                         for slack in (0.01, 0.03, 0.06, 0.1, 0.2) for margin in (2, 3)]
                _, best = min((self.lay_out(jobs, a_pass, *x)[0], x) for x in tries)
                _, self.first, self.steps = self.lay_out(jobs, a_pass, *best)
                in_ring = ("piece", "peaks", "sums")
                self.ring_first = len(self.first)
                self.ring_loop = sum(x[0] in in_ring for x in self.steps)
                assert self.ring_loop % len(self.RING) == 0

            def lay_out(self, jobs, a_pass, lead, slack, margin):
                column, fixed, word, signal = 1 / 2.4, 66, 1.04, 150
                tensor = vector = scalar = 0.0
                read = [0.0] * len(self.RING)
                probs, ready = [0.0] * 2, [0.0] * 2
                landed = {}
                all_words = 2 * sum(self.width(x) for b in range(NB) for x in self.pieces[b])
                all_keys = 2 * sum(QB - q0 for b in range(NB) for _, _, _, q0, _ in self.units[b])
                steps, at, words, keys, split = [], 0, 0, 0, 0.0

                def job(what, n, k):
                    nonlocal tensor, vector, words, split
                    steps.append((what, n, k))
                    tensor = max(tensor, read[-len(self.RING)])
                    if what == "piece":
                        width = self.width(self.pieces[n % NB][k])
                        words += width
                        tensor += column * width
                        vector = max(vector, tensor + signal) + fixed + word * width
                        if k == len(self.pieces[n % NB]) - 1:
                            split = vector = vector + 1300
                    elif what == "peaks":
                        tensor = max(tensor, split + signal) + 60
                        vector = max(vector, tensor + signal) + 300
                        landed[n] = vector + 2500
                    else:
                        tensor += 900
                        vector = max(vector, tensor + signal) + 400
                    read.append(vector + signal)

                def next_jobs(needed, allowed):
                    nonlocal at
                    while at < lead + a_pass:
                        what, n, k = jobs[at]
                        if n > needed:
                            if n > allowed or read[-len(self.RING)] > tensor:
                                return
                            if what == "peaks" and split + signal > tensor:
                                return
                            if words / all_words - keys / all_keys > before + slack:
                                return
                        job(what, n, k)
                        at += 1

                while at < lead:
                    job(*jobs[at])
                    at += 1
                before = words / all_words
                first, last = len(steps), None
                start = tensor
                for n in range(self.BLOCKS):
                    nu = len(self.units[n % NB])
                    for u in range(nu):
                        q0 = self.units[n % NB][u][3]
                        allowed = n + self.LOOK - (u < 2)
                        if u == 0:
                            next_jobs(n, allowed)
                        for pair in range(2):
                            steps.append(("scores", n, (u, pair)))
                            tensor = max(tensor, probs[pair], landed[n]) + 2 * column * (QB - q0)
                            scalar = max(scalar, tensor + signal) + 1.67 * (QB - q0) + 50
                            probs[pair] = scalar + signal
                            next_jobs(n, allowed)
                        if last is not None:
                            steps.append(("attend", *last))
                            tensor = max(tensor, *ready) + 4 * column * (QB - q0) + 60
                            if u == 0:
                                scalar = max(scalar, tensor + signal) + 480
                        if u == 1 and n:
                            job("sums", n - 1, 0)
                        keys += QB - q0
                        next_jobs(n + 1 if u >= nu - margin else n, allowed)
                        ready = list(probs)
                        last = (n, u)
                steps += [("attend", *last), ("sums", self.BLOCKS - 1, 0)]
                while at < lead + a_pass:
                    job(*jobs[at])
                    at += 1
                time = start + (NG // 2) * (max(tensor, vector) - start)
                return time, steps[:first], steps[first:]

            @staticmethod
            def width(piece):
                return sum(w for _, _, _, w, _ in piece[4])

            def walk(self, steps, start):
                for what, n, x in steps:
                    if what in ("piece", "peaks", "sums"):
                        yield what, n, x, start
                        start += 1
                    else:
                        yield what, n, x, None

            def ring_bank(self, r):
                return self.RING[r % len(self.RING)]

            def pieces_of(self, b):
                found = []
                for s in range(SPB):
                    runs = [(0, C, None)] if self.has_ctx else []
                    if self.has_own:
                        own = (SPB * b + s) * P
                        if own:
                            runs.append((self.own0, own, None))
                        runs.append((self.own0 + own, P, 0))
                    banks, at = [[]], 0
                    for k0, n, m in runs:
                        while n:
                            if at == QB:
                                banks.append([])
                                at = 0
                            w = min(n, QB - at)
                            banks[-1].append((at, k0, w, m))
                            at, k0, n = at + w, k0 + w, n - w
                            m = None if m is None else m + w
                    for c, parts in enumerate(banks):
                        heads = min(QB // at, G) if c == len(banks) - 1 else 1
                        for j in range(0, G, heads):
                            heads = min(heads, G - j)
                            found.append((j, heads, s, c, [(j + h, h * at + x, k0, w, m)
                                                           for h in range(heads) for x, k0, w, m in parts]))
                return found

            def banks(self, b, s):
                return 1 + max(c for _, _, t, c, _ in self.pieces[b] if t == s)

            def units_of(self, b):
                units = [(t * P, min(P, C - t * P), t, 0, False) for t in range(self.nctx)]
                if self.has_own:
                    for t in range(SPB * (b + 1)):
                        units.append((self.own0 + t * P, P, self.nctx + t, max(0, t - SPB * b) * P, t >= SPB * b))
                return units

            def before(self, n, of):
                return sum(len(of[m % NB]) for m in range(n))

            def attended_count(self, it, n):
                return it * self.units_loop + self.before(n + 1, self.units) + 2


            def pe(self, eng):
                def piece(it, n, k, r):
                    b, par = n % NB, n // NB % 2
                    _, _, s, _, parts = self.pieces[b][k]
                    if k == 0:
                        eng.wait_ge(self.q_landed[b], it * (2 * 96) + 96 * (n // NB + 1))
                        if b == 0:
                            ks = 16 * self.k_loads
                            eng.wait_ge(self.k_landed[par], it * ks + ks * (1 + n // self.BLOCKS))
                    eng.wait_ge(self.ring_read, it * self.ring_loop + r + 1)
                    todo = [(at, w, self.q[b][0:PEAK_ROW, j, s * P:(s + 1) * P],
                             self.k[par][0:PEAK_ROW, j, k0:k0 + w]) for j, at, k0, w, _ in parts]
                    todo += [(at, w, identity16[:], mask_qk[:, m:m + w]) for _, at, _, w, m in parts if m is not None]
                    for x, (at, w, lhs, rhs) in enumerate(todo):
                        last = eng.matmul(PS[:, self.ring_bank(r), at:at + w], lhs, rhs, start=(x == 0),
                                          stop=(x == len(todo) - 1))
                    last.then_inc(self.ring_ready, 1)

                def turn_peaks(it, n, r):
                    eng.wait_ge(self.peaks_split, it * self.BLOCKS + n + 1)
                    eng.wait_ge(self.ring_read, it * self.ring_loop + r + 1)
                    eng.transpose(PS[:, self.ring_bank(r), :].bitcast(BF16)[:, 0:P],
                                  self.peak_parts[:, :, :].rearrange("p a b -> p (a b)"),
                                  identity16[:]).then_inc(self.ring_ready, 1)

                def scores(it, n, u, pair):
                    b, par = n % NB, n // NB
                    count = self.before(n, self.units) + u
                    k0, r, _, q0, masked = self.units[b][u]
                    if u == 0 and pair == 0:
                        eng.wait_ge(self.peaks_landed, it * (16 * self.BLOCKS) + 16 * (n + 1))
                    eng.wait_ge(self.probs_ready, it * (2 * self.units_loop) + 2 * count + pair + 1)
                    for h in range(2):
                        j = 2 * pair + h
                        last = eng.matmul(PS[0:r, j, q0:QB], self.k[par][0:SCORE_ROWS, j, k0:k0 + r],
                                          self.q[b][0:SCORE_ROWS, j, q0:QB], start=True, stop=not masked)
                        if masked:
                            last = eng.matmul(PS[:, j, q0:q0 + P], identity16[:], mask_kq[:], start=False, stop=True)
                    last.then_inc(self.scores_ready, 1)

                def attend(it, n, u):
                    b, par = n % NB, n // NB
                    count = self.before(n, self.units) + u
                    _, r, t, q0, _ = self.units[b][u]
                    eng.wait_ge(self.probs_ready, it * (2 * self.units_loop) + 2 * count + 4)
                    if u == 0:
                        eng.wait_ge(self.sums_copied, it * self.BLOCKS + n + 1)
                        if b == 0:
                            vs = 16 * self.v_loads
                            eng.wait_ge(self.v_landed[par], it * vs + vs)
                    for j in range(G):
                        last = eng.matmul(PS[VW * j:VW * (j + 1), 6, q0:QB], self.v[par][0:r, t, j, :],
                                          self.probs[count % 2][j // 2][0:r, j % 2, q0:QB],
                                          start=(u == 0), stop=(u == len(self.units[b]) - 1))
                    last.then_inc(self.probs_used, 1)

                def turn_sums(it, n, r):
                    eng.wait_ge(self.sums_copied, it * self.BLOCKS + n + 2)
                    eng.wait_ge(self.ring_read, it * self.ring_loop + r + 1)
                    for s in range(SPB):
                        last = eng.transpose(PS[:, self.ring_bank(r), s * P:(s + 1) * P],
                                             self.sums[n % 2][:, s * P:(s + 1) * P], identity[:])
                    last.then_inc(self.ring_ready, 1)

                def do(it, steps, start):
                    for what, n, x, r in self.walk(steps, start):
                        if what == "piece":
                            piece(it, n, x, r)
                        elif what == "peaks":
                            turn_peaks(it, n, r)
                        elif what == "sums":
                            turn_sums(it, n, r)
                        elif what == "scores":
                            scores(it, n, *x)
                        else:
                            attend(it, n, x)

                eng.sem_inc(self.probs_used, 2)
                do(0, self.first, 0)
                eng.wait_ge(self.ones_set, 2)
                with eng.Fori(0, NG // 2) as it:
                    do(it, self.steps, self.ring_first)


            def act(self, eng):
                def exponentials(it, n, u, pair):
                    count = self.before(n, self.units) + u
                    _, r, _, q0, _ = self.units[n % NB][u]
                    if pair == 0:
                        eng.wait_ge(self.probs_used, it * self.units_loop + count + 1)
                    eng.wait_ge(self.scores_ready, it * (2 * self.units_loop) + 2 * count + pair + 1)
                    eng.activation(self.probs[count % 2][pair][0:r, :, q0:QB], PS[0:r, 2 * pair:2 * pair + 2, q0:QB],
                                   ACT.Exp).then_inc(self.probs_ready, 1)

                def copy_sums(it, n):
                    eng.wait_ge(self.probs_used, self.attended_count(it, n))
                    eng.activation(self.sums[n % 2], PS[:, 6, :], ACT.Copy).then_inc(self.sums_copied, 1)

                eng.sem_inc(self.probs_ready, 2)
                with eng.Fori(0, NG // 2) as it:
                    for what, n, x in self.steps:
                        if what == "scores":
                            exponentials(it, n, *x)
                        elif what == "attend" and x == len(self.units[n % NB]) - 1:
                            copy_sums(it, n)


            def dve(self, eng):
                LINKS = 5 * self.BLOCKS
                links = [0]

                def link(it, ins):
                    links[0] += 1
                    ins.then_inc(self.chain, 1)
                    eng.wait_ge(self.chain, it * LINKS + links[0])

                def piece(it, n, k, r):
                    j, heads, s, c, parts = self.pieces[n % NB][k]
                    width = self.width(self.pieces[n % NB][k])
                    eng.wait_ge(self.ring_ready, it * self.ring_loop + r + 1)
                    if self.pieces[n % NB].index(self.pieces[n % NB][k]) < k:
                        eng.wait_ge(self.ring_read, it * self.ring_loop + r + 3)
                    eng.tensor_reduce(self.peaks[:, G * s + j:G * s + j + heads, c],
                                      PS[:, self.ring_bank(r), 0:width].rearrange("p (j k) -> p j k", j=heads), AX_X,
                                      ALU.max).then_inc(self.ring_read, 1)

                def split_peaks(it, n, r):
                    eng.wait_ge(self.ring_read, it * self.ring_loop + r + 4)
                    for s in range(SPB):
                        last = eng.tensor_reduce(self.peak[:, 0, :].rearrange("p (j s) -> p j s", j=G)[:, :, s],
                                                 self.peaks[:, G * s:G * (s + 1), 0:self.banks(n % NB, s)], AX_X,
                                                 ALU.max, negate=True)
                    link(it, last)
                    link(it, eng.tensor_copy(self.peak_parts[:, 0, :], self.peak[:, 0, :]))
                    link(it, eng.tensor_tensor(self.peak[:, 1, :], self.peak[:, 0, :], self.peak_parts[:, 0, :],
                                               ALU.subtract))
                    link(it, eng.tensor_copy(self.peak_parts[:, 1, :], self.peak[:, 1, :]))
                    eng.tensor_tensor(self.peak_parts[:, 2, :], self.peak[:, 1, :], self.peak_parts[:, 1, :],
                                      ALU.subtract).then_inc(self.peaks_split, 1)

                def copy_peaks(it, n, r):
                    eng.wait_ge(self.ring_ready, it * self.ring_loop + r + 1)
                    if n:
                        eng.wait_ge(self.peaks_landed, it * (16 * self.BLOCKS) + 16 * n)
                    rows48 = 3 * SPB * G
                    eng.tensor_copy(self.peak_rows[0:rows48, :],
                                    PS[0:rows48, self.ring_bank(r), :].bitcast(BF16)[:, 0:P]
                                    ).then_inc(self.peaks_copied, 1)
                    eng.wait_ge(self.peaks_copied, it * self.BLOCKS + n + 1)
                    eng.sem_inc(self.ring_read, 1)

                def divide(it, n, r):
                    b, group = n % NB, n // NB
                    eng.wait_ge(self.ring_ready, it * self.ring_loop + r + 1)
                    turned = PS[:, self.ring_bank(r), :].rearrange("p (s j d) -> p s j d", s=SPB, j=G)
                    link(it, eng.reciprocal(self.inverse, turned[:, :, :, DK]))
                    dst = self.attended[:, SPB * b:SPB * (b + 1), bass.ds(it * (2 * G * DK) + group * (G * DK), G * DK)]
                    eng.tensor_tensor(dst.rearrange("p s (j d) -> p s j d", j=G), turned[:, :, :, 0:DK],
                                      self.inverse.unsqueeze(3).to_broadcast([P, SPB, G, DK]),
                                      ALU.mult).then_inc(self.ring_read, 1)

                def do(it, steps, start):
                    for what, n, x, r in self.walk(steps, start):
                        if what == "piece":
                            piece(it, n, x, r)
                            if x == len(self.pieces[n % NB]) - 1:
                                split_peaks(it, n, r)
                        elif what == "peaks":
                            copy_peaks(it, n, r)
                        elif what == "sums":
                            divide(it, n, r)

                eng.sem_inc(self.ring_read, 3)
                eng.sem_inc(self.sums_copied, 1)
                link(0, eng.memset(self.peak_parts, 0.0))
                do(0, self.first, 0)
                before = links[0]
                with eng.Fori(0, NG // 2) as it:
                    do(it, self.steps, self.ring_first)
                assert links[0] - before == LINKS, links[0]

            def pool(self, eng):
                pair_of_ones = 1 + 0x3F80 / 2 ** 23
                for par in range(2):
                    ones_rows = self.k[par][PEAK_ROW:SCORE_ROWS].rearrange("p j c -> p (j c)").bitcast(F32)
                    eng.memset(ones_rows, pair_of_ones).then_inc(self.ones_set, 1)


            @property
            def k_loads(self):
                return 6 * (self.has_ctx + self.has_own)

            @property
            def v_loads(self):
                return 2 * self.has_ctx + self.has_own

            def load_keys(self, eng, par, group, own, landed):
                if not (self.has_own if own else self.has_ctx):
                    return
                src, c0, w = (k_parts_own.get(self.i), self.own0, S) if own else (k_parts_ctx.get(self.i), 0, C)
                for slot, part in enumerate(K_PARTS):
                    eng.dma_start(self.k[par][slot * DK:(slot + 1) * DK, :, c0:c0 + w],
                                  src[part, bass.ds(group * (G * DK), G * DK), :].rearrange("(j d) c -> d j c", d=DK)
                                  ).then_inc(landed, 16)

            def load_values(self, eng, par, group, own, landed):
                cols_of, full = bass.ds(group * (G * VW), G * VW), C // P
                if own and self.has_own:
                    eng.dma_start(self.v[par][:, self.nctx:self.nv].rearrange("p t j w -> p t (j w)"),
                                  v_own[self.i][:, cols_of].rearrange("(t p) w -> p t w", p=P)).then_inc(landed, 16)
                if not own and self.has_ctx:
                    src = v_ctx[self.i]
                    eng.dma_start(self.v[par][:, 0:full].rearrange("p t j w -> p t (j w)"),
                                  src[0:full * P, cols_of].rearrange("(t p) w -> p t w", p=P)).then_inc(landed, 16)
                    eng.dma_start(self.v[par][0:C - full * P, full].rearrange("p j w -> p (j w)"),
                                  src[full * P:C, cols_of]).then_inc(landed, 16)

            def load_early(self, eng):
                self.load_keys(eng, 0, 0, False, self.early_landed)
                self.load_values(eng, 0, 0, False, self.early_landed)

            def wait_early(self, eng):
                if self.has_ctx:
                    eng.wait_ge(self.early_landed, 16 * 8)

            def sp(self, eng):
                i, GD = self.i, G * DK

                def load_group(par, group):
                    for own in (True, False):
                        self.load_keys(eng, par, group, own, self.k_landed[par])
                    for own in (True, False):
                        self.load_values(eng, par, group, own, self.v_landed[par])

                def load_queries(b, group):
                    for slot, part in enumerate(Q_PARTS):
                        eng.dma_start(self.q[b][slot * DK:(slot + 1) * DK, :, :],
                                      q_parts[i][part, bass.ds(group * GD, GD), b * QB:(b + 1) * QB]
                                      .rearrange("(j d) c -> d j c", d=DK)).then_inc(self.q_landed[b], 16)

                def store_peaks(it, n):
                    eng.wait_ge(self.peaks_copied, it * self.BLOCKS + n + 1)
                    b = n % NB
                    eng.dma_start(self.q[b][PEAK_ROW:SCORE_ROWS].rearrange("p j (s c) -> p (j s) c", s=SPB),
                                  self.peak_rows[0:3 * SPB * G, :]).then_inc(self.peaks_landed, 16)

                if self.has_ctx:
                    eng.sem_inc(self.k_landed[0], 16 * 6)
                    eng.sem_inc(self.v_landed[0], 16 * 2)
                load_queries(0, 0)
                self.load_keys(eng, 0, 0, True, self.k_landed[0])
                self.load_values(eng, 0, 0, True, self.v_landed[0])
                for b in range(1, NB):
                    load_queries(b, 0)
                for what, n, _ in self.first:
                    if what == "peaks":
                        store_peaks(0, n)
                with eng.Fori(0, NG // 2) as it:
                    eng.wait_ge(self.probs_used, it * self.units_loop + 2)
                    load_group(1, it * 2 + 1)
                    for what, n, x in self.steps:
                        if what == "peaks":
                            store_peaks(it, n)
                        elif what == "attend" and x == len(self.units[n % NB]) - 1:
                            b, second = n % NB, n // NB
                            eng.wait_ge(self.probs_used, self.attended_count(it, n))
                            load_queries(b, it * 2 + 1 if not second else it * (-2) + 2)
                            if b == NB - 1 and not second:
                                load_group(0, it * (-2) + 2)
                loops = NG // 2
                for b in range(NB):
                    eng.wait_ge(self.q_landed[b], 96 * (1 + 2 * loops))
                for par in range(2):
                    eng.wait_ge(self.k_landed[par], 16 * self.k_loads * (1 - par + loops))
                    eng.wait_ge(self.v_landed[par], 16 * self.v_loads * (1 - par + loops))
                early = sum(what == "peaks" for what, _, _ in self.first)
                eng.wait_ge(self.peaks_landed, 16 * (early + loops * self.BLOCKS))

        class Output:

            def __init__(self, i, attended, residual, dst, bias):
                self.bias, self.residual, self.dst = bias, residual, dst
                self.take = take = carver()
                self.turned = take(KH, S)
                self.weights = Weights(take, f"o{i}", landed="out_weights_landed")
                self.w = self.weights[f"o{i}"]
                self.turn = Turn([(attended[:, t], P) for t in range(NT)], self.turned, name="out_turn")
                self.projected, self.added = sem("out_projected"), sem("out_added")

            def pe(self, eng):
                self.turn.pe(eng)
                eng.wait_ge(self.turn.copied, len(self.turn.jobs))
                self.weights.wait(eng)
                for n in range(NT // 2):
                    if n >= 4:
                        eng.wait_ge(self.added, n - 3)
                    for h in range(2):
                        t, dst = 2 * n + h, PS[:, 2 + n % 4, h * D:(h + 1) * D]
                        for k in range(KH):
                            last = eng.matmul(dst, self.turned[:, k, t * P:(t + 1) * P], self.w[:, k, :],
                                              start=(k == 0), stop=(k == KH - 1 and self.bias is None))
                        if self.bias is not None:
                            last = eng.matmul(dst, ones[0:1, :], self.bias, start=False, stop=True)
                    last.then_inc(self.projected, 1)

            def act(self, eng):
                self.turn.act(eng)

            def dve(self, eng, norm):
                for n in range(NT // 2):
                    eng.wait_ge(self.projected, n + 1)
                    for h in range(2):
                        t = 2 * n + h
                        last = eng.scalar_tensor_tensor(out=self.dst[:, t, :], in0=PS[:, 2 + n % 4, h * D:(h + 1) * D],
                                                        scalar=1.0, in1=self.residual[:, t, :], op0=ALU.mult,
                                                        op1=ALU.add, accum_out=stats[:, 0, t:t + 1])
                    last.then_inc(self.added, 1)
                    if n % 2:
                        eng.wait_ge(self.added, n + 1)
                        norm.tick(eng, n // 2)
                for t in range(norm.CHUNKS, norm.ticks):
                    norm.tick(eng, t)

            def sp(self, eng):
                self.weights.sp(eng)

        class ExpertRows:

            def __init__(self, output, normed):
                self.output = output
                self.norm = Normalize(X[:], XN[:], normed, layer=False, rms=True)

            def sp(self, eng):
                self.output.sp(eng)

            def pe(self, eng):
                self.output.pe(eng)

            def act(self, eng):
                self.output.act(eng)
                self.norm.act(eng)

            def dve(self, eng):
                self.output.dve(eng, self.norm)

            def pool(self, eng):
                self.norm.pool(eng)

        class Experts:

            FT = -(-F0 // P)
            FC = F0 // 2
            BLOCKS = 2 * S // P + E - 1
            K = BLOCKS + 1

            def __init__(self):
                take = carver()
                self.gate_up = take(E * 2 * KH, F0)
                self.down = take(E * self.FT, D)
                self.normed = take(NT, D)
                normed, used = self.normed.rearrange("p t d -> p (t d)"), [0]

                def reuse(n):
                    used[0] += n
                    assert used[0] <= NT * D
                    return normed[:, used[0] - n:used[0]]

                self.x_in = [reuse(D) for _ in range(2)]
                self.x_turned = [dims(reuse(KH * P), KH, P) for _ in range(2)]
                self.silu = [reuse(self.FC) for _ in range(2)]
                self.hidden = [reuse(F0) for _ in range(2)]
                self.hidden_turned = [take(self.FT, P) for _ in range(2)]
                self.y = [take(D) for _ in range(2)]
                self.weights = Weights(take, "router")
                self.share = [take(NT) for _ in range(2)]
                self.place = take(2 * NT).bitcast(mybir.dt.int32).rearrange("p (c t) -> p c t", c=2)
                self.expert = take(self.K).bitcast(mybir.dt.int32)
                words = XN[:].rearrange("p t d -> p (t d)")
                self.turned = words.rearrange("p (k s) -> p k s", k=KH)
                self.turn = Turn([(self.normed[:, t], P) for t in range(NT)], self.turned, gain=cols[:, COL["g2"], :])
                at = [0]

                def part(n):
                    at[0] += n
                    assert at[0] <= NT * D
                    return words[:, at[0] - n:at[0]]

                self.grid = [part(E * NT * NT) for _ in range(1)][0]
                self.by_expert = [part(NT * E) for _ in range(9)]
                self.few = [part(E) for _ in range(5)]
                self.row = [part(NT) for _ in range(2)]
                self.constants = take(E * E + NT * NT + NT + self.K)
                self.gathered = [self.gate_up[:, 2 * i:2 * i + 1, 0:2 * D].rearrange("p a (c d) -> p (a c) d", c=2)
                                 for i in range(4)]
                weights = self.gate_up.rearrange("p a f -> p (a f)")
                self.norm = Normalize(X[:], XN[:], dims(weights[:, 8 * F0:8 * F0 + NT * D], NT, D), summed=True)
                self.counting = self.hidden_turned[0][:, 0:2, :]
                self.constants_landed = sem("moe_constants_landed")
                self.counting_landed = sem("moe_counting_landed")
                self.w_landed = sem("moe_w_landed")
                self.routed = sem("moe_routed")
                self.chain = sem("moe_chain")
                self.shifted = sem("moe_shifted")
                self.route_exp = sem("moe_route_exp")
                self.chosen = sem("moe_chosen")
                self.counted = sem("moe_counted")
                self.placed = sem("moe_placed")
                self.scattered = sem("moe_scattered")
                self.x_landed = [sem(f"moe_x_landed{i}") for i in range(2)]
                self.x_read = sem("moe_x_read")
                self.x_copied = sem("moe_x_copied")
                self.multiplied = sem("moe_multiplied")
                self.activated = sem("moe_activated")
                self.gated = sem("moe_gated")
                self.hidden_read = sem("moe_hidden_read")
                self.hidden_copied = sem("moe_hidden_copied")
                self.mixed = sem("moe_mixed")
                self.y_copied = sem("moe_y_copied")
                self.y_stored = [sem(f"moe_y_stored{i}") for i in range(2)]
                self.gathered_row = [sem(f"moe_gathered{i}") for i in range(4)]
                self.added = sem("moe_added")

            def sp(self, eng):
                self.weights.sp(eng)
                eng.dma_start(self.constants, a["routing"]).then_inc(self.constants_landed, 16)
                eng.dma_start(self.counting, a["counting"].rearrange("p (r c) -> p r c", r=2)
                              ).then_inc(self.counting_landed, 16)
                full, n = F0 // P, 0
                for e in range(E):
                    for g, src in enumerate((a["wg"], a["wu"])):
                        at = (e * 2 + g) * KH
                        eng.dma_start(self.gate_up[:, at:at + KH, :],
                                      src[e * D:(e + 1) * D, :].rearrange("(k p) f -> p k f", p=P)
                                      ).then_inc(self.w_landed, 16)
                    eng.dma_start(self.down[:, e * self.FT:e * self.FT + full, :],
                                  a["wd"][e * F0:e * F0 + full * P, :].rearrange("(t p) d -> p t d", p=P)
                                  ).then_inc(self.w_landed, 16)
                    eng.dma_start(self.down[0:F0 - full * P, e * self.FT + full, :],
                                  a["wd"][e * F0 + full * P:(e + 1) * F0, :]).then_inc(self.w_landed, 16)
                eng.wait_ge(self.scattered, 16 * 2 * NT)

                def load(k, par):
                    eng.dma_start(self.x_in[par], rows_sorted[bass.ds(k * P, P), :]).then_inc(self.x_landed[par], 16)

                def store(k, par):
                    eng.wait_ge(self.y_copied, k + 2)
                    eng.dma_start(results_sorted[bass.ds(k * P, P), :], self.y[par]).then_inc(self.y_stored[par], 16)

                load(0, 0)
                load(1, 1)
                with eng.Fori(0, (self.BLOCKS - 1) // 2) as it:
                    for j in range(2):
                        k = it * 2 + (1 + j)
                        eng.wait_ge(self.x_read, k)
                        load(k + 1, j)
                        store(k - 1, j)
                store(self.BLOCKS - 1, (self.BLOCKS - 1) % 2)

            def pool(self, eng):
                eng.wait_ge(self.placed, 1)
                for t in range(NT):
                    for c in range(2):
                        eng.indirect_dma_start(rows_sorted, bass.IndirectOffsetOnAxis(self.place[:, c, t:t + 1], 0),
                                               self.normed[:, t, :], None).then_inc(self.scattered, 16)
                for par in range(2):
                    eng.wait_ge(self.y_stored[par], 16 * (1 + len(range(par, self.BLOCKS, 2))))
                for t in range(NT):
                    if t >= 4:
                        eng.wait_ge(self.added, t - 3)
                    for c in range(2):
                        eng.indirect_dma_start(self.gathered[t % 4][:, c, :], None, results_sorted,
                                               bass.IndirectOffsetOnAxis(self.place[:, c, t:t + 1], 0)
                                               ).then_inc(self.gathered_row[t % 4], 16)
                    if t % SPB == SPB - 1 and t // SPB >= 2:
                        self.norm.pool(eng, t // SPB - 2, t // SPB - 1)
                self.norm.pool(eng, self.norm.CHUNKS - 2)

            def pe(self, eng):
                FT, FC = self.FT, self.FC
                self.turn.pe(eng)
                eng.wait_ge(self.turn.copied, len(self.turn.jobs))
                self.weights.wait(eng)
                for t in range(NT):
                    for k in range(KH):
                        last = eng.matmul(PS[:, 7, t * E:(t + 1) * E], self.turned[:, k, t * P:(t + 1) * P],
                                          self.weights["router"][:, k, :], start=(k == 0), stop=(k == KH - 1))
                last.then_inc(self.routed, 1)
                eng.wait_ge(self.chosen, 1)
                eng.wait_ge(self.counting_landed, 16)
                for i in range(2):
                    last = eng.matmul(PS[:, 6, i * P:(i + 1) * P], self.counting[:, i, :], self.by_expert[4],
                                      start=True, stop=True)
                last.then_inc(self.counted, 1)
                eng.sem_inc(self.mixed, 2)
                eng.sem_inc(self.hidden_read, 4)
                eng.wait_ge(self.placed, 1)
                eng.wait_ge(self.w_landed, 16 * 4 * E)

                def turn_x(k, par, first=0):
                    eng.wait_ge(self.x_landed[par], first)
                    eng.wait_ge(self.x_copied, k + 1)
                    for h in range(KH):
                        last = eng.transpose(PS[:, 7, h * P:(h + 1) * P], self.x_in[par][:, h * P:(h + 1) * P],
                                             identity[:])
                    last.then_inc(self.x_read, 1)

                def multiply(k, par, c, e):
                    if c == 0:
                        eng.wait_ge(self.x_copied, k + 2)
                    eng.wait_ge(self.gated, k * 2 + (c + 1))
                    for g in range(2):
                        for h in range(KH):
                            w = self.gate_up[:, bass.ds(e * (2 * KH) + (g * KH + h), 1), c * FC:(c + 1) * FC]
                            last = eng.matmul(PS[:, 2 * c + g, 0:FC], self.x_turned[par][:, h, :],
                                              w.rearrange("p a f -> p (a f)"), start=(h == 0), stop=(h == KH - 1))
                    last.then_inc(self.multiplied, 1)

                def turn_hidden(k, par):
                    eng.wait_ge(self.gated, k * 2 + 4)
                    for h in range(2):
                        eng.wait_ge(self.hidden_copied, k * 2 + (h + 1))
                        for f in range(3 * h, 3 * h + 3):
                            r = min(P, F0 - f * P)
                            last = eng.transpose(PS[0:r, 4 + h, (f - 3 * h) * P:(f - 3 * h + 1) * P],
                                                 self.hidden[par][:, f * P:f * P + r], identity[:])
                        last.then_inc(self.hidden_read, 1)

                def mix(k, par, e):
                    eng.wait_ge(self.hidden_copied, k * 2 + 4)
                    eng.wait_ge(self.y_copied, k + 1)
                    for f in range(FT):
                        r = min(P, F0 - f * P)
                        w = self.down[0:r, bass.ds(e * FT + f, 1), :].rearrange("p a d -> p (a d)")
                        last = eng.matmul(PS[:, 6, 0:D], self.hidden_turned[par][0:r, f, :], w,
                                          start=(f == 0), stop=(f == FT - 1))
                    last.then_inc(self.mixed, 1)

                def expert_of(k):
                    return eng.value_load(self.expert[0:1, bass.ds(k, 1)], min_val=0, max_val=E - 1)

                turn_x(0, 0, 16)
                e = expert_of(0)
                for c in range(2):
                    multiply(0, 0, c, e)
                turn_x(1, 1, 16)
                with eng.Fori(0, (self.BLOCKS - 1) // 2) as it:
                    e = expert_of(it * 2 + 1)
                    for j in range(2):
                        k, par = it * 2 + (1 + j), 1 - j
                        multiply(k, par, 0, e)
                        turn_hidden(k - 1, 1 - par)
                        multiply(k, par, 1, e)
                        turn_x(k + 1, 1 - par, it * 16 + 32)
                        if j == 0:
                            e = expert_of(k + 1)
                        mix(k - 1, 1 - par, expert_of(k - 1))
                k = self.BLOCKS - 1
                turn_hidden(k, k % 2)
                mix(k, k % 2, expert_of(k))

            def act(self, eng):
                self.turn.act(eng)
                eng.wait_ge(self.shifted, 1)
                eng.activation(self.by_expert[1], self.by_expert[0], ACT.Exp).then_inc(self.route_exp, 1)
                eng.sem_inc(self.hidden_copied, 2)

                def silu(k, c):
                    eng.wait_ge(self.multiplied, k * 2 + (c + 1))
                    eng.wait_ge(self.gated, k * 2 + (c + 1))
                    eng.activation(self.silu[c], PS[:, 2 * c, 0:self.FC], ACT.Silu).then_inc(self.activated, 1)

                def copy_hidden(k, par):
                    eng.wait_ge(self.mixed, k + 1)
                    for h in range(2):
                        eng.wait_ge(self.hidden_read, k * 2 + (h + 5))
                        dst, left = self.hidden_turned[par], F0 - 5 * P
                        src = PS[:, 4 + h, 0:3 * P].rearrange("p (f c) -> p f c", f=3)
                        if h == 0:
                            last = eng.activation(dst[:, 0:3, :], src, ACT.Copy)
                        else:
                            eng.activation(dst[:, 3:5, :], src[:, 0:2, :], ACT.Copy)
                            last = eng.activation(dst[0:left, 5, :], src[0:left, 2, :], ACT.Copy)
                        last.then_inc(self.hidden_copied, 1)

                for c in range(2):
                    silu(0, c)
                with eng.Fori(0, (self.BLOCKS - 1) // 2) as it:
                    for j in range(2):
                        k, par = it * 2 + (1 + j), 1 - j
                        silu(k, 0)
                        copy_hidden(k - 1, 1 - par)
                        silu(k, 1)
                copy_hidden(self.BLOCKS - 1, (self.BLOCKS - 1) % 2)
                self.norm.act(eng)

            def dve(self, eng):
                chained = [0]

                def link(ins):
                    chained[0] += 1
                    ins.then_inc(self.chain, 1)
                    eng.wait_ge(self.chain, chained[0])

                eng.sem_inc(self.gated, 2)
                eng.sem_inc(self.x_copied, 1)
                eng.sem_inc(self.y_copied, 1)
                for par in range(2):
                    eng.sem_inc(self.y_stored[par], 16)
                logits = PS[:, 7, 0:NT * E].rearrange("p (t e) -> p t e", t=NT)
                flat = self.by_expert
                shifted, powers, probs, rank, chosen, share, first, second, place = [
                    x.rearrange("p (t e) -> p t e", t=NT) for x in flat]
                total, other_total = self.row
                rows_in, blocks_in, block_start, block_end, start = self.few
                at = 0
                consts = []
                for n in (E * E, NT * NT, NT, self.K):
                    consts.append(self.constants[:, at:at + n])
                    at += n
                earlier = consts[0].rearrange("p (e o) -> p e o", e=E)
                tile_before = consts[1].rearrange("p (t u) -> p t u", t=NT)
                tile_rows, block_number = consts[2:]

                def over_experts(x):
                    return x.unsqueeze(2).to_broadcast([P, NT, E])

                eng.wait_ge(self.routed, 1)
                link(eng.tensor_reduce(total, logits, AX_X, ALU.max))
                eng.tensor_tensor(shifted, logits, over_experts(total), ALU.subtract).then_inc(self.shifted, 1)
                eng.wait_ge(self.route_exp, 1)
                link(eng.tensor_reduce(other_total, powers, AX_X, ALU.add))
                link(eng.reciprocal(total, other_total))
                link(eng.tensor_tensor(probs, powers, over_experts(total), ALU.mult))
                better = self.grid[:, 0:NT * E * E].rearrange("p (t e o) -> p t e o", t=NT, e=E)
                link(eng.memset(self.grid[:, 0:NT * E * E], 0.0))
                for e in range(E):
                    for others, op in ((slice(0, e), ALU.is_ge), (slice(e + 1, E), ALU.is_gt)):
                        n = others.stop - others.start
                        if n:
                            last = eng.tensor_tensor(better[:, :, e, others], probs[:, :, others],
                                                     probs[:, :, e:e + 1].to_broadcast([P, NT, n]), op)
                link(last)
                link(eng.tensor_reduce(rank, better, AX_X, ALU.add))
                eng.tensor_scalar(chosen, rank, 1.5, None, ALU.is_lt).then_inc(self.chosen, 1)
                eng.wait_ge(self.chosen, 1)
                link(eng.tensor_scalar(first, rank, 0.5, None, ALU.is_lt))
                link(eng.tensor_tensor(second, chosen, first, ALU.subtract))
                eng.wait_ge(self.constants_landed, 16)
                eng.wait_ge(self.counted, 1)
                counts = PS[:, 6, P:2 * P].rearrange("p (t e) -> p e t", t=NT)
                link(eng.tensor_copy(powers.rearrange("p t e -> p (t e)"), PS[:, 6, P:2 * P]))
                link(eng.tensor_reduce(rows_in, counts, AX_X, ALU.add))
                tiles = self.grid.rearrange("p (e t u) -> p e t u", e=E, t=NT)
                by_tile = powers.rearrange("p t e -> p e t").unsqueeze(2).to_broadcast([P, E, NT, NT])
                link(eng.tensor_tensor(tiles, by_tile, tile_before.unsqueeze(1).to_broadcast([P, E, NT, NT]), ALU.mult))
                link(eng.tensor_reduce(shifted.rearrange("p t e -> p e t"), tiles, AX_X, ALU.add))
                filled = self.grid[:, 0:E * NT].rearrange("p (e t) -> p e t", e=E)
                link(eng.tensor_tensor(filled, rows_in.unsqueeze(2).to_broadcast([P, E, NT]),
                                       tile_rows.unsqueeze(1).to_broadcast([P, E, NT]), ALU.is_gt))
                link(eng.tensor_reduce(blocks_in, filled, AX_X, ALU.add))
                before = self.grid[:, 0:E * E].rearrange("p (e o) -> p e o", e=E)
                link(eng.tensor_tensor(before, blocks_in.unsqueeze(1).to_broadcast([P, E, E]), earlier, ALU.mult))
                link(eng.tensor_reduce(block_start, before, AX_X, ALU.add))
                link(eng.tensor_tensor(block_end, block_start, blocks_in, ALU.add))
                ended = self.grid[:, 0:self.K * E].rearrange("p (k e) -> p k e", e=E)
                link(eng.tensor_tensor(ended, block_end.unsqueeze(1).to_broadcast([P, self.K, E]),
                                       block_number.unsqueeze(2).to_broadcast([P, self.K, E]), ALU.is_le))
                number = self.grid[:, E * self.K:E * self.K + self.K]
                link(eng.tensor_reduce(number, ended, AX_X, ALU.add))
                eng.tensor_scalar(self.expert, number, float(E - 1), None, ALU.min)
                link(eng.tensor_scalar(start, block_start, float(P), None, ALU.mult))
                link(eng.tensor_tensor(place, PS[:, 6, 0:P].rearrange("p (t e) -> p t e", t=NT), shifted, ALU.add))
                link(eng.tensor_tensor(place, place, start.unsqueeze(1).to_broadcast([P, NT, E]), ALU.add))
                for c, which in enumerate((first, second)):
                    link(eng.tensor_tensor(powers, which, place, ALU.mult))
                    link(eng.tensor_reduce(total, powers, AX_X, ALU.add))
                    link(eng.tensor_copy(self.place[:, c, :], total))
                eng.sem_inc(self.placed, 1)
                link(eng.tensor_tensor(share, chosen, probs, ALU.mult))
                link(eng.tensor_reduce(other_total, share, AX_X, ALU.add))
                link(eng.reciprocal(total, other_total))
                link(eng.tensor_tensor(share, share, over_experts(total), ALU.mult))
                for c, which in enumerate((first, second)):
                    link(eng.tensor_tensor(powers, which, share, ALU.mult))
                    link(eng.tensor_reduce(self.share[c], powers, AX_X, ALU.add))

                def copy_x(k, par):
                    eng.wait_ge(self.x_read, k + 1)
                    if not isinstance(k, int) or k >= 2:
                        eng.wait_ge(self.multiplied, k * 2 - 2)
                    for h in range(KH):
                        last = eng.tensor_scalar(self.x_turned[par][:, h, :], PS[:, 7, h * P:(h + 1) * P],
                                                 cols[:, COL["g2"], h:h + 1], None, ALU.mult)
                    last.then_inc(self.x_copied, 1)

                def gate(k, par, c):
                    if c == 0:
                        eng.wait_ge(self.hidden_read, k * 2 + 2)
                    eng.wait_ge(self.activated, k * 2 + (c + 1))
                    eng.tensor_tensor(self.hidden[par][:, c * self.FC:(c + 1) * self.FC], PS[:, 2 * c + 1, 0:self.FC],
                                      self.silu[c], ALU.mult).then_inc(self.gated, 1)

                def copy_y(k, par, stored):
                    eng.wait_ge(self.mixed, k + 3)
                    eng.wait_ge(self.y_stored[par], stored)
                    eng.tensor_copy(self.y[par], PS[:, 6, 0:D]).then_inc(self.y_copied, 1)

                copy_x(0, 0)
                for c in range(2):
                    gate(0, 0, c)
                copy_x(1, 1)
                with eng.Fori(0, (self.BLOCKS - 1) // 2) as it:
                    for j in range(2):
                        k, par = it * 2 + (1 + j), 1 - j
                        for c in range(2):
                            gate(k, par, c)
                        copy_x(k + 1, 1 - par)
                        copy_y(k - 1, 1 - par, it * 16 + 16)
                copy_y(self.BLOCKS - 1, (self.BLOCKS - 1) % 2, 16 * (1 + (self.BLOCKS - 1) // 2))
                for t in range(NT):
                    eng.wait_ge(self.gathered_row[t % 4], 32 * (t // 4 + 1))
                    link(eng.scalar_tensor_tensor(out=X[:, t, :], in0=self.gathered[t % 4][:, 0, :],
                                                  scalar=self.share[0][:, t:t + 1], in1=X[:, t, :],
                                                  op0=ALU.mult, op1=ALU.add))
                    eng.scalar_tensor_tensor(out=X[:, t, :], in0=self.gathered[t % 4][:, 1, :],
                                             scalar=self.share[1][:, t:t + 1], in1=X[:, t, :],
                                             op0=ALU.mult, op1=ALU.add,
                                             accum_out=stats[:, 0, t:t + 1]).then_inc(self.added, 1)
                    if t % SPB == SPB - 1:
                        eng.wait_ge(self.added, t + 1)
                        self.norm.tick(eng, t // SPB)
                for t in range(self.norm.CHUNKS, self.norm.ticks):
                    self.norm.tick(eng, t)

        class FeedForward:

            FT = F1 // P
            PER_PASS = 2 * FT

            LINKS = 2 * 5

            def __init__(self, output):
                self.output, take = output, output.take
                self.turned = take(KH, S)
                self.norm = Normalize(X[:], XN[:], take(NT, D), summed=True)
                self.turn = Turn([(XN[:, t], P) for t in range(NT)], self.turned, norm=self.norm)
                self.w1, self.w2 = take(KH, F1), take(self.FT, D)
                self.b1 = take(self.FT)
                self.affine = take(2, D)
                self.hidden = [take(self.FT, QB) for _ in range(2)]
                self.y = [take(SPB, D) for _ in range(2)]
                self.squares = [take(SPB, D) for _ in range(2)]
                self.stats = [take(4, SPB) for _ in range(2)]
                self.loaded = sem("ffn_loaded")
                self.hidden_ready = sem("ffn_hidden_ready")
                self.activated = sem("ffn_activated")
                self.mixed = sem("ffn_mixed")
                self.added = sem("ffn_added")
                self.chain = sem("ffn_chain")
                self.centred = sem("ffn_centred")
                self.squared = sem("ffn_squared")
                self.spread = sem("ffn_spread")
                self.inverse = sem("ffn_inverse")
                self.final = sem("ffn_final")
                self.stored = [sem(f"ffn_stored{i}") for i in range(2)]

            def sp(self, eng):
                self.output.sp(eng)
                eng.dma_start(self.w1, a["w1"].rearrange("(k p) f -> p k f", p=P)).then_inc(self.loaded, 16)
                eng.dma_start(self.w2, a["w2"].rearrange("(t p) d -> p t d", p=P)).then_inc(self.loaded, 16)
                eng.dma_start(self.b1, a["b1"]).then_inc(self.loaded, 16)
                eng.dma_start(self.affine, a["affine"].rearrange("p (r d) -> p r d", r=2)).then_inc(self.loaded, 16)
                with eng.Fori(0, NB // 2) as it:
                    for x in range(2):
                        eng.wait_ge(self.final, it * 2 + (x + 1))
                        eng.dma_start(out[0][bass.ds((it * 2 + x) * QB, QB), :].rearrange("(t p) d -> p t d", p=P),
                                      self.y[x]).then_inc(self.stored[x], 16)
                for x in range(2):
                    eng.wait_ge(self.stored[x], 16 * (NB // 2 + 1))

            def pool(self, eng):
                self.norm.pool(eng)
                with eng.Fori(0, NB // 2) as it:
                    for x in range(2):
                        eng.wait_ge(self.spread, it * 2 + (x + 1))
                        eng.tensor_tensor(self.stats[x][:, 3, :], self.stats[x][:, 2, :], minus_half[:, 0:SPB],
                                          ALU.pow).then_inc(self.inverse, 1)

            def pe(self, eng):
                self.output.pe(eng)
                self.turn.pe(eng)
                eng.wait_ge(self.turn.copied, len(self.turn.jobs))
                eng.wait_ge(self.loaded, 64)
                eng.sem_inc(self.mixed, 4)

                def mix(it, x):
                    eng.wait_ge(self.activated, it * self.PER_PASS + self.FT * (x + 1) + 4)
                    for half in range(2):
                        eng.wait_ge(self.added, it * 4 + 2 * x + half + 1)
                        for h in range(2):
                            s, dst = 2 * half + h, PS[:, 4 + half, h * D:(h + 1) * D]
                            for f in range(self.FT):
                                eng.matmul(dst, self.hidden[x][:, f, s * P:(s + 1) * P], self.w2[:, f, :],
                                           start=(f == 0), stop=False)
                            last = eng.matmul(dst, ones[0:1, :], rows[:, ROW["b2"], :], start=False, stop=True)
                        last.then_inc(self.mixed, 1)

                with eng.Fori(0, NB // 2) as it:
                    for x in range(2):
                        for f in range(self.FT):
                            count = x * self.FT + f
                            eng.wait_ge(self.activated, it * self.PER_PASS + count + 1)
                            for k in range(KH):
                                last = eng.matmul(PS[:, count % 4, :], self.w1[:, k, f * P:(f + 1) * P],
                                                  self.turned[:, k, bass.ds(it * (2 * QB) + x * QB, QB)],
                                                  start=(k == 0), stop=(k == KH - 1))
                            last.then_inc(self.hidden_ready, 1)
                            if x and f == 1:
                                mix(it, 0)
                    mix(it, 1)

            def act(self, eng):
                self.output.act(eng)
                self.norm.act(eng)
                self.turn.act(eng)
                eng.wait_ge(self.loaded, 64)
                eng.sem_inc(self.activated, 4)

                def square(it, x):
                    eng.wait_ge(self.centred, it * 2 + (x + 1))
                    for t in range(SPB):
                        last = eng.activation(self.squares[x][:, t, :], self.y[x][:, t, :], ACT.Square,
                                              accum_out=self.stats[x][:, 2, t:t + 1])
                    last.then_inc(self.squared, 1)

                with eng.Fori(0, NB // 2) as it:
                    for x in range(2):
                        for f in range(self.FT):
                            count = x * self.FT + f
                            eng.wait_ge(self.hidden_ready, it * self.PER_PASS + count + 1)
                            if f == 0:
                                eng.wait_ge(self.mixed, it * 4 + 2 * x + 2)
                            eng.activation(self.hidden[x][:, f, :], PS[:, count % 4, :], ACT.Relu,
                                           bias=self.b1[:, f:f + 1]).then_inc(self.activated, 1)
                            if x and f == 5:
                                square(it, 0)
                    square(it, 1)

            def dve(self, eng):
                self.output.dve(eng, self.norm)
                eng.sem_inc(self.added, 2)
                for x in range(2):
                    eng.sem_inc(self.stored[x], 16)
                with eng.Fori(0, NB // 2) as it:
                    chained = [0]

                    def link(ins):
                        chained[0] += 1
                        ins.then_inc(self.chain, 1)
                        eng.wait_ge(self.chain, it * self.LINKS + chained[0])

                    for x in range(2):
                        y, (total, mean, square, inverse) = self.y[x], [self.stats[x][:, i, :] for i in range(4)]
                        tiles = bass.ds(it * (2 * SPB) + x * SPB, SPB)

                        def over_rows(v):
                            return v.unsqueeze(2).to_broadcast([P, SPB, D])

                        eng.wait_ge(self.stored[x], it * 16 + 16)
                        for half in range(2):
                            eng.wait_ge(self.mixed, it * 4 + 2 * x + half + 1 + 4)
                            eng.tensor_tensor(y[:, 2 * half:2 * half + 2, :],
                                              PS[:, 4 + half, :].rearrange("p (t d) -> p t d", t=2),
                                              XN[:, bass.ds(it * (2 * SPB) + (x * SPB + 2 * half), 2), :],
                                              ALU.add).then_inc(self.added, 1)
                        eng.wait_ge(self.added, it * 4 + 2 * x + 4)
                        link(eng.tensor_reduce(total, y, AX_X, ALU.add))
                        link(eng.tensor_scalar(mean, total, 1.0 / D, None, ALU.mult))
                        eng.tensor_tensor(y, y, over_rows(mean), ALU.subtract).then_inc(self.centred, 1)
                        eng.wait_ge(self.squared, it * 2 + (x + 1))
                        eng.tensor_scalar(square, square, 1.0 / D, LN_EPS, ALU.mult, ALU.add).then_inc(self.spread, 1)
                        eng.wait_ge(self.inverse, it * 2 + (x + 1))
                        link(eng.tensor_tensor(y, y, over_rows(inverse), ALU.mult))
                        for i, op in enumerate((ALU.mult, ALU.add)):
                            link(eng.tensor_tensor(y, y, self.affine[:, i, :].unsqueeze(1).to_broadcast([P, SPB, D]), op))
                        eng.tensor_tensor(y, y, X[:, tiles, :], ALU.add).then_inc(self.final, 1)
                    assert chained[0] == self.LINKS

        experts = Experts()
        attentions = [Attention(0, True, False), Attention(1, False, True), Attention(2, True, True)]
        outputs = [Output(0, attentions[0].attended, X[:], X[:], rows[:, ROW["o0"], :]),
                   Output(1, attentions[1].attended, XN[:], XN[:], None),
                   Output(2, attentions[2].attended, X[:], X[:], rows[:, ROW["o2"], :])]
        stages = [Setup(), Context(),
                  Prepare(0, attentions[0]), attentions[0],
                  Prepare(1, attentions[1], outputs[0]), attentions[1],
                  ExpertRows(outputs[1], experts.normed), experts,
                  Prepare(2, attentions[2]), attentions[2],
                  FeedForward(outputs[2])]

        numbers = sorted(x.num for x in roles.values())
        assert numbers == list(range(numbers[0], numbers[-1] + 1))

        stage_semaphores = range(numbers[0], numbers[-1] + 1)

        for stage in stages:
            with nc.Block() as block:
                @block.sync
                def _(eng):
                    stage.sp(eng)

                @block.scalar
                def _(eng):
                    stage.act(eng)

                @block.tensor
                def _(eng):
                    stage.pe(eng)

                @block.vector
                def _(eng):
                    stage.dve(eng)

                @block.gpsimd
                def _(eng):
                    stage.pool(eng)

            nc.all_engine_barrier(sems_to_clear=stage_semaphores)


def kernel(**inputs):
    import numpy as np
    import concourse.bacc as bacc
    from concourse.bass_utils import run_bass_kernel_spmd

    f = {k: np.asarray(v) for k, v in inputs.items()}

    def turned_heads(w):
        return w.reshape(D, H, 2, DK // 2)[:, :, ::-1, :].reshape(D, D)

    def column(v):
        return v.reshape(-1, P).T

    inverse_frequency = 1.0 / 10000.0 ** (np.arange(0, DK, 2, dtype=np.float32) / DK)
    angles = np.einsum("i,j->ij", np.arange(S, dtype=np.float32), inverse_frequency)
    angles = np.concatenate([angles, angles], axis=-1).astype(np.float32)
    sign = np.where(np.arange(DK) < DK // 2, -1.0, 1.0).astype(np.float32)
    rope = np.stack([np.tile(np.cos(angles).T, (P // DK, 1)), np.tile((np.sin(angles) * sign).T, (P // DK, 1))])
    later = np.triu(np.full((P, P), NEG, np.float32), 1)
    routing = np.concatenate([np.tril(np.ones((E, E)), -1).ravel(), np.tril(np.ones((NT, NT)), -1).ravel(),
                              P * np.arange(NT), np.arange(2 * S // P + E)]).astype(np.float32)
    counting = np.concatenate([np.triu(np.ones((P, P)), 1), np.ones((P, P))], 1).astype(np.float32)

    arrays = {
        "x": f["x"][0], "ctx": f["ctx_1024"][0],
        "identity": np.eye(P, dtype=np.float32), "masks": np.stack([later, later.T]),
        "rope": rope.astype(np.float32), "routing": routing.reshape(1, -1).repeat(P, 0),
        "counting": counting,
        "w_q0": f["L0_xattn_w_q"].T, "w_k0": f["L0_xattn_w_k"].T, "w_v0": f["L0_xattn_w_v"].T, "w_o0": f["L0_xattn_w_o"].T,
        "w_q1": f["L0_ffn_wq"], "w_q1_turned": turned_heads(f["L0_ffn_wq"]), "w_k1": f["L0_ffn_wk"],
        "w_k1_turned": turned_heads(f["L0_ffn_wk"]), "w_v1": f["L0_ffn_wv"], "w_o1": f["L0_ffn_wo"],
        "w_q2": f["L1_xattn_Wq"], "w_kv2": f["L1_xattn_Wkv"], "w_o2": f["L1_xattn_Wout"],
        "w_router": f["L0_ffn_w_router"],
        "rows": np.stack([f["L0_xattn_b_v"], f["L0_xattn_b_o"], f["L1_xattn_bout"], f["L1_ffn_b2"][0]]),
        "cols": np.concatenate([column(f[k]) for k in ("L0_xattn_b_q", "L0_xattn_b_k", "L0_ffn_g1", "L0_ffn_g2")], 1),
        "wg": f["L0_ffn_wg"].reshape(E * D, F0), "wu": f["L0_ffn_wu"].reshape(E * D, F0),
        "wd": f["L0_ffn_wd"].reshape(E * F0, D),
        "w1": f["L1_ffn_w1"][0], "w2": f["L1_ffn_w2"][0], "b1": column(f["L1_ffn_b1"][0]),
        "affine": np.stack([f["L1_ffn_gamma"], f["L1_ffn_beta"]]).reshape(1, 2 * D).repeat(P, 0),
    }
    arrays = {f"in_{k}": np.ascontiguousarray(v) for k, v in arrays.items()}
    nc = bacc.Bacc("TRN2", target_bir_lowering=False, num_devices=1)
    args = {k[3:]: nc.dram_tensor(k, v.shape, mybir.dt.from_np(v.dtype), kind="ExternalInput").ap()
            for k, v in arrays.items()}
    out = nc.dram_tensor("out_x", (1, S, D), F32, kind="ExternalOutput").ap()
    build(nc, args, out)
    result = run_bass_kernel_spmd(nc, [arrays], core_ids=[0])
    return result.results[0]["out_x"]
```
